# Optimizing a Trainium2 kernel written in Bass

```python
import numpy as np
import jax
import jax.numpy as jnp

def _softmax(x, axis=-1):
    return jax.nn.softmax(x, axis=axis)

def _gelu(x):
    return jax.nn.gelu(x, approximate=True)

def _silu(x):
    return jax.nn.silu(x)

def _sigmoid(x):
    return jax.nn.sigmoid(x)

def _layernorm(x, axis=-1, eps=1e-05):
    m = jnp.mean(x, axis=axis, keepdims=True)
    v = jnp.var(x, axis=axis, keepdims=True)
    return (x - m) / jnp.sqrt(v + eps)

def _scatter_add(tgt, idx, src, axis=0):
    return tgt.at[idx].add(src)

def _segment_sum(src, seg, n):
    return jax.ops.segment_sum(src, seg, n)
kernel_name = 'mk_vit_tower_d2_tok_img1024_r4_fca3a7'

def setup_inputs(seed: int=0):
    np.random.seed(seed)
    _w = jnp.asarray

    def _rec_inputs():
        import jax
        import jax.numpy as jnp
        _rk = jax.random.key(seed)
        x = -4.65018e-05 + 0.999886 * jax.random.normal(jax.random.fold_in(_rk, 1), (32, 3, 128, 128), jnp.float32)
        return x
    x = _rec_inputs()

    def _L0_tok_setup():
        import jax, jax.numpy as jnp
        import numpy as np
        IMG_H = 128
        IMG_W = 128
        C = 3
        PH = 16
        PW = 16
        HID = 256
        NH = IMG_H // PH
        NW = IMG_W // PW
        PD = C * PH * PW
        BATCH = 64

        def sinusoidal_pos_embed(embed_dim, grid_size_x, grid_size_y):
            gh = jnp.arange(grid_size_y)
            gw = jnp.arange(grid_size_x)
            grid = jnp.stack(jnp.meshgrid(gh, gw, indexing='ij'), axis=0)
            h_pos = grid[0].reshape(-1).astype(jnp.float32)
            w_pos = grid[1].reshape(-1).astype(jnp.float32)
            quarter = embed_dim // 4
            factor = 10000.0 ** (jnp.arange(quarter, dtype=jnp.float32) / quarter)
            h = h_pos[:, None] / factor
            w = w_pos[:, None] / factor
            return jnp.concatenate([jnp.sin(h), jnp.cos(h), jnp.sin(w), jnp.cos(w)], axis=-1)
        key = jax.random.key(seed)
        k1, k2 = jax.random.split(key, 2)
        x = jax.random.normal(k1, (BATCH, C, IMG_H, IMG_W), dtype=jnp.float32)
        Wp = jax.random.normal(k2, (HID, PD), dtype=jnp.float32) * (1.0 / np.sqrt(PD))
        b = jnp.zeros((HID,), dtype=jnp.float32)
        return {'x': x, 'Wp': Wp, 'b': b}
    _L0_tok_all = _L0_tok_setup()
    _L0_tok_in = {k: v for k, v in _L0_tok_all.items() if k in ('Wp', 'b')}
    del _L0_tok_all

    def _L0_attn_setup():
        import jax, jax.numpy as jnp
        import numpy as np
        B, T, H, N = (4, 512, 256, 16)
        DT_MIN, DT_MAX = (0.001, 0.1)
        A_INIT_MIN, A_INIT_MAX = (0.5, 2.0)

        def _inv_softplus(x):
            return x + jnp.log(-jnp.expm1(-x))

        def _reference_tuple_inner(x, A_log, B_mat, C_mat, D_vec, W_dt, b_dt):
            u = x
            A = -jnp.exp(A_log)
            dt = jax.nn.softplus(jnp.einsum('bth,gh->btg', u, W_dt) + b_dt)
            state0 = jnp.zeros((u.shape[0], A_log.shape[0], A_log.shape[1]), dtype=u.dtype)

            def step(state, inp):
                dt_t, u_t = inp
                dtA = dt_t[..., None]
                A_bar = jnp.exp(dtA * A)
                state = A_bar * state + dtA * B_mat * u_t[..., None]
                y_t = jnp.einsum('bhn,hn->bh', state, C_mat) + D_vec * u_t
                return (state, y_t)
            state_final, ys = jax.lax.scan(step, state0, (dt.transpose(1, 0, 2), u.transpose(1, 0, 2)))
            out = ys.transpose(1, 0, 2)
            return (out, state_final)
        key = jax.random.key(seed)
        kx, ka, kb, kc, kw, kdt = jax.random.split(key, 6)
        x = jax.random.normal(kx, (B, T, H), dtype=jnp.float32)
        A_log = jax.random.uniform(ka, (H, N), minval=np.log(A_INIT_MIN), maxval=np.log(A_INIT_MAX), dtype=jnp.float32)
        B_mat = 0.02 * jax.random.normal(kb, (H, N), dtype=jnp.float32)
        C_mat = 0.02 * jax.random.normal(kc, (H, N), dtype=jnp.float32)
        D_vec = jnp.ones((H,), dtype=jnp.float32)
        W_dt = 0.02 * jax.random.normal(kw, (H, H), dtype=jnp.float32)
        b_dt = _inv_softplus(jax.random.uniform(kdt, (H,), minval=DT_MIN, maxval=DT_MAX, dtype=jnp.float32))
        return {'x': x, 'A_log': A_log, 'B_mat': B_mat, 'C_mat': C_mat, 'D_vec': D_vec, 'W_dt': W_dt, 'b_dt': b_dt}
    _L0_attn_all = _L0_attn_setup()
    _L0_attn_in = {k: v for k, v in _L0_attn_all.items() if k in ('A_log', 'B_mat', 'C_mat', 'D_vec', 'W_dt', 'b_dt')}
    del _L0_attn_all

    def _L0_ffn_setup():
        import jax, jax.numpy as jnp
        import numpy as np
        B, S, D, H, E = (64, 256, 256, 64, 8)
        EPS = 1e-05
        key = jax.random.key(seed)
        ks = jax.random.split(key, 8)
        x = jax.random.normal(ks[0], (B, S, D), jnp.float32)
        return {'x': x, 'ln_g': jnp.ones((D,), jnp.float32), 'ln_b': jnp.zeros((D,), jnp.float32), 'bn_g': jnp.ones((D,), jnp.float32), 'bn_b': jnp.zeros((D,), jnp.float32), 'bn_mean': jax.random.normal(ks[1], (D,), jnp.float32) * 0.01, 'bn_var': jnp.ones((D,), jnp.float32), 'Wr': jax.random.normal(ks[2], (D, E), jnp.float32) * 0.02, 'br': jnp.zeros((E,), jnp.float32), 'W_down': jax.random.normal(ks[3], (E, D, H), jnp.float32) * 0.02, 'b_down': jnp.zeros((E, H), jnp.float32), 'W_up': jax.random.normal(ks[4], (E, H, D), jnp.float32) * 0.02, 'b_up': jnp.zeros((E, D), jnp.float32)}
    _L0_ffn_all = _L0_ffn_setup()
    _L0_ffn_in = {k: v for k, v in _L0_ffn_all.items() if k in ('ln_g', 'ln_b', 'bn_g', 'bn_b', 'bn_mean', 'bn_var', 'Wr', 'br', 'W_down', 'b_down', 'W_up', 'b_up')}
    del _L0_ffn_all

    def _L1_attn_setup():
        import math
        import jax, jax.numpy as jnp
        import numpy as np
        NUM_BUCKETS = 32
        MAX_DISTANCE = 128
        HEADS = 8
        DIM_HEAD = 64

        def _relative_position_bucket(rel_pos, num_buckets=NUM_BUCKETS, max_distance=MAX_DISTANCE):
            n = jnp.maximum(-rel_pos, 0)
            max_exact = num_buckets // 2
            is_small = n < max_exact
            val_if_large = max_exact + (jnp.log(jnp.maximum(n, 1).astype(jnp.float32) / max_exact) / math.log(max_distance / max_exact) * (num_buckets - max_exact)).astype(jnp.int32)
            val_if_large = jnp.minimum(val_if_large, num_buckets - 1)
            return jnp.where(is_small, n, val_if_large)
        key = jax.random.key(seed)
        ks = jax.random.split(key, 5)
        b, n, dim = (2, 512, 256)
        inner = HEADS * DIM_HEAD
        return {'x': jax.random.normal(ks[0], (b, n, dim), dtype=jnp.float32), 'Wq': jax.random.normal(ks[1], (dim, inner), dtype=jnp.float32) * dim ** (-0.5), 'Wkv': jax.random.normal(ks[2], (dim, 2 * inner), dtype=jnp.float32) * dim ** (-0.5), 'Wo': jax.random.normal(ks[3], (inner, dim), dtype=jnp.float32) * inner ** (-0.5), 'bo': jnp.zeros((dim,), dtype=jnp.float32), 'rel_emb': jax.random.normal(ks[4], (NUM_BUCKETS, HEADS), dtype=jnp.float32) * 0.02}
    _L1_attn_all = _L1_attn_setup()
    _L1_attn_in = {k: v for k, v in _L1_attn_all.items() if k in ('Wq', 'Wkv', 'Wo', 'bo', 'rel_emb')}
    del _L1_attn_all

    def _L1_ffn_setup():
        import jax, jax.numpy as jnp
        import numpy as np
        H = 256
        M = 128
        E = 16
        TOP_K = 2
        SCALE = 2.5
        NORM_TOPK = True
        B, S = (1, 256)

        def _moe(x, gate_w, w_gate, w_up, w_down, ws_gate, ws_up, ws_down):
            T = x.shape[0]
            shared = jax.nn.silu(x @ ws_gate) * (x @ ws_up) @ ws_down
            scores = jax.nn.sigmoid(x.astype(jnp.float32) @ gate_w.T.astype(jnp.float32))
            topk_w, topk_idx = jax.lax.top_k(scores, TOP_K)
            if NORM_TOPK and TOP_K > 1:
                topk_w = topk_w / (topk_w.sum(-1, keepdims=True) + 1e-20)
            topk_w = topk_w * SCALE
            route = jnp.zeros((T, E), topk_w.dtype).at[jnp.arange(T)[:, None], topk_idx].set(topk_w)
            g = jnp.einsum('th,ehm->etm', x, w_gate)
            u = jnp.einsum('th,ehm->etm', x, w_up)
            eo = jnp.einsum('etm,emh->eth', jax.nn.silu(g) * u, w_down)
            routed = jnp.einsum('te,eth->th', route.astype(x.dtype), eo)
            return routed + shared
        key = jax.random.key(seed)
        ks = jax.random.split(key, 8)
        std = 0.02
        return {'hidden_states': jax.random.normal(ks[0], (B, S, H), jnp.float32), 'gate_w': jax.random.normal(ks[1], (E, H), jnp.float32) * std, 'w_gate': jax.random.normal(ks[2], (E, H, M), jnp.float32) * std, 'w_up': jax.random.normal(ks[3], (E, H, M), jnp.float32) * std, 'w_down': jax.random.normal(ks[4], (E, M, H), jnp.float32) * std, 'ws_gate': jax.random.normal(ks[5], (H, M), jnp.float32) * std, 'ws_up': jax.random.normal(ks[6], (H, M), jnp.float32) * std, 'ws_down': jax.random.normal(ks[7], (M, H), jnp.float32) * std}
    _L1_ffn_all = _L1_ffn_setup()
    _L1_ffn_in = {k: v for k, v in _L1_ffn_all.items() if k in ('gate_w', 'w_gate', 'w_up', 'w_down', 'ws_gate', 'ws_up', 'ws_down')}
    del _L1_ffn_all
    return {'x': x, 'L0_tok_Wp': _L0_tok_in['Wp'], 'L0_tok_b': _L0_tok_in['b'], 'L0_attn_A_log': _L0_attn_in['A_log'], 'L0_attn_B_mat': _L0_attn_in['B_mat'], 'L0_attn_C_mat': _L0_attn_in['C_mat'], 'L0_attn_D_vec': _L0_attn_in['D_vec'], 'L0_attn_W_dt': _L0_attn_in['W_dt'], 'L0_attn_b_dt': _L0_attn_in['b_dt'], 'L0_ffn_ln_g': _L0_ffn_in['ln_g'], 'L0_ffn_ln_b': _L0_ffn_in['ln_b'], 'L0_ffn_bn_g': _L0_ffn_in['bn_g'], 'L0_ffn_bn_b': _L0_ffn_in['bn_b'], 'L0_ffn_bn_mean': _L0_ffn_in['bn_mean'], 'L0_ffn_bn_var': _L0_ffn_in['bn_var'], 'L0_ffn_Wr': _L0_ffn_in['Wr'], 'L0_ffn_br': _L0_ffn_in['br'], 'L0_ffn_W_down': _L0_ffn_in['W_down'], 'L0_ffn_b_down': _L0_ffn_in['b_down'], 'L0_ffn_W_up': _L0_ffn_in['W_up'], 'L0_ffn_b_up': _L0_ffn_in['b_up'], 'L1_attn_Wq': _L1_attn_in['Wq'], 'L1_attn_Wkv': _L1_attn_in['Wkv'], 'L1_attn_Wo': _L1_attn_in['Wo'], 'L1_attn_bo': _L1_attn_in['bo'], 'L1_attn_rel_emb': _L1_attn_in['rel_emb'], 'L1_ffn_gate_w': _L1_ffn_in['gate_w'], 'L1_ffn_w_gate': _L1_ffn_in['w_gate'], 'L1_ffn_w_up': _L1_ffn_in['w_up'], 'L1_ffn_w_down': _L1_ffn_in['w_down'], 'L1_ffn_ws_gate': _L1_ffn_in['ws_gate'], 'L1_ffn_ws_up': _L1_ffn_in['ws_up'], 'L1_ffn_ws_down': _L1_ffn_in['ws_down']}

def reference(x, L0_tok_Wp, L0_tok_b, L0_attn_A_log, L0_attn_B_mat, L0_attn_C_mat, L0_attn_D_vec, L0_attn_W_dt, L0_attn_b_dt, L0_ffn_ln_g, L0_ffn_ln_b, L0_ffn_bn_g, L0_ffn_bn_b, L0_ffn_bn_mean, L0_ffn_bn_var, L0_ffn_Wr, L0_ffn_br, L0_ffn_W_down, L0_ffn_b_down, L0_ffn_W_up, L0_ffn_b_up, L1_attn_Wq, L1_attn_Wkv, L1_attn_Wo, L1_attn_bo, L1_attn_rel_emb, L1_ffn_gate_w, L1_ffn_w_gate, L1_ffn_w_up, L1_ffn_w_down, L1_ffn_ws_gate, L1_ffn_ws_up, L1_ffn_ws_down):
    import jax
    import jax.numpy as jnp

    def _L0_tok_ref(x, Wp, b):
        import jax, jax.numpy as jnp
        import numpy as np
        IMG_H = 128
        IMG_W = 128
        C = 3
        PH = 16
        PW = 16
        HID = 256
        NH = IMG_H // PH
        NW = IMG_W // PW
        PD = C * PH * PW
        BATCH = 64

        def sinusoidal_pos_embed(embed_dim, grid_size_x, grid_size_y):
            gh = jnp.arange(grid_size_y)
            gw = jnp.arange(grid_size_x)
            grid = jnp.stack(jnp.meshgrid(gh, gw, indexing='ij'), axis=0)
            h_pos = grid[0].reshape(-1).astype(jnp.float32)
            w_pos = grid[1].reshape(-1).astype(jnp.float32)
            quarter = embed_dim // 4
            factor = 10000.0 ** (jnp.arange(quarter, dtype=jnp.float32) / quarter)
            h = h_pos[:, None] / factor
            w = w_pos[:, None] / factor
            return jnp.concatenate([jnp.sin(h), jnp.cos(h), jnp.sin(w), jnp.cos(w)], axis=-1)
        B = x.shape[0]
        p = x.reshape(B, C, NH, PH, NW, PW)
        p = p.transpose(0, 2, 4, 3, 5, 1)
        p = p.reshape(B, NH * NW, PH * PW * C)
        out = jnp.einsum('bnd,hd->bnh', p, Wp) + b
        pos = sinusoidal_pos_embed(HID, NW, NH)
        return out + pos

    def _L0_attn_ref(x, A_log, B_mat, C_mat, D_vec, W_dt, b_dt):
        import jax, jax.numpy as jnp
        import numpy as np
        B, T, H, N = (4, 512, 256, 16)
        DT_MIN, DT_MAX = (0.001, 0.1)
        A_INIT_MIN, A_INIT_MAX = (0.5, 2.0)

        def _inv_softplus(x):
            return x + jnp.log(-jnp.expm1(-x))

        def _reference_tuple_inner(x, A_log, B_mat, C_mat, D_vec, W_dt, b_dt):
            u = x
            A = -jnp.exp(A_log)
            dt = jax.nn.softplus(jnp.einsum('bth,gh->btg', u, W_dt) + b_dt)
            state0 = jnp.zeros((u.shape[0], A_log.shape[0], A_log.shape[1]), dtype=u.dtype)

            def step(state, inp):
                dt_t, u_t = inp
                dtA = dt_t[..., None]
                A_bar = jnp.exp(dtA * A)
                state = A_bar * state + dtA * B_mat * u_t[..., None]
                y_t = jnp.einsum('bhn,hn->bh', state, C_mat) + D_vec * u_t
                return (state, y_t)
            state_final, ys = jax.lax.scan(step, state0, (dt.transpose(1, 0, 2), u.transpose(1, 0, 2)))
            out = ys.transpose(1, 0, 2)
            return (out, state_final)
        return _reference_tuple_inner(x, A_log, B_mat, C_mat, D_vec, W_dt, b_dt)[0]

    def _L0_ffn_ref(x, ln_g, ln_b, bn_g, bn_b, bn_mean, bn_var, Wr, br, W_down, b_down, W_up, b_up):
        import jax, jax.numpy as jnp
        import numpy as np
        B, S, D, H, E = (64, 256, 256, 64, 8)
        EPS = 1e-05
        mu = jnp.mean(x, axis=-1, keepdims=True)
        var = jnp.var(x, axis=-1, keepdims=True)
        z = (x - mu) * jax.lax.rsqrt(var + EPS) * ln_g + ln_b
        z_sent = jnp.mean(z, axis=1)
        z_bn = (z_sent - bn_mean) * jax.lax.rsqrt(bn_var + EPS) * bn_g + bn_b
        probs = jax.nn.softmax(z_bn @ Wr + br, axis=-1)
        idx = jnp.argmax(probs, axis=-1)
        gate = jnp.take_along_axis(probs, idx[:, None], axis=1)[:, 0]
        h = jax.nn.relu(jnp.einsum('bsd,bdh->bsh', z, W_down[idx]) + b_down[idx][:, None, :])
        y = jnp.einsum('bsh,bhd->bsd', h, W_up[idx]) + b_up[idx][:, None, :]
        return y * gate[:, None, None]

    def _L1_attn_ref(x, Wq, Wkv, Wo, bo, rel_emb):
        import math
        import jax, jax.numpy as jnp
        import numpy as np
        NUM_BUCKETS = 32
        MAX_DISTANCE = 128
        HEADS = 8
        DIM_HEAD = 64

        def _relative_position_bucket(rel_pos, num_buckets=NUM_BUCKETS, max_distance=MAX_DISTANCE):
            n = jnp.maximum(-rel_pos, 0)
            max_exact = num_buckets // 2
            is_small = n < max_exact
            val_if_large = max_exact + (jnp.log(jnp.maximum(n, 1).astype(jnp.float32) / max_exact) / math.log(max_distance / max_exact) * (num_buckets - max_exact)).astype(jnp.int32)
            val_if_large = jnp.minimum(val_if_large, num_buckets - 1)
            return jnp.where(is_small, n, val_if_large)
        b, n, dim = x.shape
        h, d = (HEADS, DIM_HEAD)
        scale = d ** (-0.5)
        bias_scale = d ** 0.5
        q = x @ Wq
        kv = x @ Wkv
        k, v = jnp.split(kv, 2, axis=-1)

        def to_heads(t):
            return t.reshape(b, n, h, d).transpose(0, 2, 1, 3)
        q, k, v = (to_heads(q) * scale, to_heads(k), to_heads(v))
        sim = jnp.einsum('bhid,bhjd->bhij', q, k)
        pos = jnp.arange(n)
        rel_pos = pos[None, :] - pos[:, None]
        buckets = _relative_position_bucket(rel_pos)
        bias = rel_emb[buckets]
        bias = bias.transpose(2, 0, 1)[None] * bias_scale
        sim = sim + bias
        causal_mask = jnp.triu(jnp.ones((n, n), dtype=bool), k=1)
        sim = jnp.where(causal_mask, -jnp.finfo(sim.dtype).max, sim)
        attn = jax.nn.softmax(sim, axis=-1)
        out = jnp.einsum('bhij,bhjd->bhid', attn, v)
        out = out.transpose(0, 2, 1, 3).reshape(b, n, h * d)
        return out @ Wo + bo

    def _L1_ffn_ref(hidden_states, gate_w, w_gate, w_up, w_down, ws_gate, ws_up, ws_down):
        import jax, jax.numpy as jnp
        import numpy as np
        H = 256
        M = 128
        E = 16
        TOP_K = 2
        SCALE = 2.5
        NORM_TOPK = True
        B, S = (1, 256)

        def _moe(x, gate_w, w_gate, w_up, w_down, ws_gate, ws_up, ws_down):
            T = x.shape[0]
            shared = jax.nn.silu(x @ ws_gate) * (x @ ws_up) @ ws_down
            scores = jax.nn.sigmoid(x.astype(jnp.float32) @ gate_w.T.astype(jnp.float32))
            topk_w, topk_idx = jax.lax.top_k(scores, TOP_K)
            if NORM_TOPK and TOP_K > 1:
                topk_w = topk_w / (topk_w.sum(-1, keepdims=True) + 1e-20)
            topk_w = topk_w * SCALE
            route = jnp.zeros((T, E), topk_w.dtype).at[jnp.arange(T)[:, None], topk_idx].set(topk_w)
            g = jnp.einsum('th,ehm->etm', x, w_gate)
            u = jnp.einsum('th,ehm->etm', x, w_up)
            eo = jnp.einsum('etm,emh->eth', jax.nn.silu(g) * u, w_down)
            routed = jnp.einsum('te,eth->th', route.astype(x.dtype), eo)
            return routed + shared
        b, s, h = hidden_states.shape
        x = hidden_states.reshape(-1, h)
        out = _moe(x, gate_w, w_gate, w_up, w_down, ws_gate, ws_up, ws_down)
        return out.reshape(b, s, h)
    h = _L0_tok_ref(x, L0_tok_Wp, L0_tok_b)
    h = h + _L0_attn_ref(_layernorm(h, axis=-1), L0_attn_A_log, L0_attn_B_mat, L0_attn_C_mat, L0_attn_D_vec, L0_attn_W_dt, L0_attn_b_dt)
    h = h + _L0_ffn_ref(_layernorm(h, axis=-1), L0_ffn_ln_g, L0_ffn_ln_b, L0_ffn_bn_g, L0_ffn_bn_b, L0_ffn_bn_mean, L0_ffn_bn_var, L0_ffn_Wr, L0_ffn_br, L0_ffn_W_down, L0_ffn_b_down, L0_ffn_W_up, L0_ffn_b_up)
    h = h + _L1_attn_ref(_layernorm(h, axis=-1), L1_attn_Wq, L1_attn_Wkv, L1_attn_Wo, L1_attn_bo, L1_attn_rel_emb)
    h = h + _L1_ffn_ref(_layernorm(h, axis=-1), L1_ffn_gate_w, L1_ffn_w_gate, L1_ffn_w_up, L1_ffn_w_down, L1_ffn_ws_gate, L1_ffn_ws_up, L1_ffn_ws_down)
    return h

_drawn_inputs = setup_inputs


def setup_inputs(seed=0):
    import zlib

    import numpy as np

    out = dict(_drawn_inputs(seed))
    spreads = {'L0_tok_b': (0.0, 0.1),
     'L0_attn_D_vec': (1.0, 0.2),
     'L0_ffn_ln_g': (1.0, 0.6),
     'L0_ffn_ln_b': (0.0, 0.8),
     'L0_ffn_bn_g': (1.0, 0.6),
     'L0_ffn_bn_b': (0.0, 0.8),
     'L0_ffn_bn_var': (1.0, 0.6),
     'L0_ffn_br': (0.0, 0.8),
     'L0_ffn_b_down': (0.0, 0.8),
     'L0_ffn_b_up': (0.0, 0.8),
     'L1_attn_bo': (0.0, 0.1)}
    factors = {'L0_attn_A_log': 64.0,
     'L0_attn_B_mat': 64.0,
     'L0_attn_C_mat': 64.0,
     'L0_attn_W_dt': 64.0,
     'L0_attn_b_dt': 64.0,
     'L0_ffn_bn_mean': 8.0,
     'L0_ffn_Wr': 6.213,
     'L0_ffn_W_down': 8.0,
     'L0_ffn_W_up': 8.0,
     'L1_attn_rel_emb': 3.498,
     'L1_ffn_gate_w': 6.504,
     'L1_ffn_w_gate': 6.195,
     'L1_ffn_w_up': 6.086,
     'L1_ffn_w_down': 6.107,
     'L1_ffn_ws_gate': 8.0,
     'L1_ffn_ws_up': 8.0,
     'L1_ffn_ws_down': 8.0}
    for name, (base, spread) in spreads.items():
        noise = np.random.default_rng([zlib.crc32(name.encode()), seed]).standard_normal(out[name].shape)
        drawn = base * np.exp(spread * noise) if base else spread * noise
        out[name] = jnp.asarray(drawn.astype(out[name].dtype))
    for name, factor in factors.items():
        out[name] = (out[name] * factor).astype(out[name].dtype)
    return out
```

```python
from contextlib import ExitStack

import concourse.bass as bass
from concourse import mybir

ALU = mybir.AluOpType
ACT = mybir.ActivationFunctionType
F32 = mybir.dt.float32
F32R = mybir.dt.float32r
BF16 = mybir.dt.bfloat16
U32 = mybir.dt.uint32
AX_X = mybir.AxisListType.X

P = 128
BATCH, SEQ, HID = 32, 64, 256
PATCH = 768
NSTATE = 16
GROUPS = 4
GT = BATCH * SEQ // GROUPS
TILES = GT // P
GS = GT // SEQ
KH = HID // P
KP = PATCH // P
E0, H0 = 8, 64
HEADS, DH = 8, 64
INNER = HEADS * DH
HP = HEADS // 2
E1, M1 = 16, 128
TOPK_SCALE = 2.5
EPS = 1e-5
PENALTY = float(2.0**100)
MASKED = -1e37
STEPS = KH * NSTATE
EXPERT = KH * 2 * M1 + HID


class Signal:

    def __init__(self, sem, per):
        self.sem, self.per = sem, per

    def __call__(self, g, k):
        return self.sem, g * self.per + k


def wait(engine, at):
    if not (isinstance(at[1], int) and at[1] <= 0):
        engine.wait_ge(*at)


def wait_before_tiles(pe, at, bank, weights):
    wait(pe, at)
    pe.matmul(bank[0:weights.shape[1], 0:1], weights, weights[:, 0:1], start=True, stop=True)


def product(pe, out, lhs, rhs, start, stop, **kw):
    pe.matmul(out, lhs[0], rhs[0], start=start, stop=False, **kw)
    pe.matmul(out, lhs[1], rhs[0], start=False, stop=False, **kw)
    return pe.matmul(out, lhs[0], rhs[1], start=False, stop=stop, **kw)


BACK = [
    ("join", 0), ("gate", -1), ("ln2", 0), ("turn2", 0), ("pick", 0), ("down", 0), ("up", 0), ("ln3", 0), ("turn3", 0),
    ("q", 0), ("k", 0), ("v", 0), ("scores", 0, 0), ("scores", 0, 1), ("probs", 0, 0), ("heads", 0, 0), ("scores", 0, 2),
    ("probs", 0, 1), ("outputs", 0, 0), ("heads", 0, 1), ("scores", 0, 3), ("probs", 0, 2), ("outputs", 0, 1),
    ("heads", 0, 2), ("proj", 0, 0), ("probs", 0, 3), ("outputs", 0, 2), ("heads", 0, 3), ("outputs", 0, 3), ("proj", 0, 1),
    ("ln4", 0),
]
FRONT = [("patch", 2, 0), ("patch", 2, 1), ("ln1", 2), ("turn1", 2), ("dt", 2), ("soft", 2)]
STEP = [("relative", 1)] + [("step", 1, i) for i in range(STEPS)]
MERGED = {
    "sync": "ssbbbssbfssfbssbfsbsbfbfbssssssbsfbsbssbsbbbssbssbbbbbsbbbsbbsssbbssbs",
    "gpsimd": "sssbbssssssbbssbbbssssbbbbbbfbbbbfbbbbbbbsssbsssssfssfsssfsssssbbbbbbf",
    "scalar": "ssbsbsbsbsffbssbsbfsbfbsssssbsssfbsfssbbssbsssbbsbbbbbbbsbbsbbsbssbbsb",
    "vector": "ssbbbssfsbsbbsfsfbbsbsbssfsssssbfsbsfssbbbssssbbbsbbbbssbbsbbbbsssbsbb",
    "tensor": "ssssbbbsfbfsfbbsbsbfbssbfbbsbsssssssssssssssssbbbssbbbbbbbbsbbsbsbbbbf",
}


def phase_one(nc, sems, d, route):
    with ExitStack() as ctx:
        def sb(name, shape, dt=F32):
            return ctx.enter_context(nc.sbuf_tensor(name, shape, dt))

        def signal(name, per=1):
            return Signal(sems.enter_context(nc.semaphore(name)), per)

        ident = sb("ident", [P, P])
        posb = sb("posb", [P, HID])
        bo = sb("bo", [P, HID])
        iota = sb("iota", [P, E1])
        eps = sb("eps", [P, 1])
        one = sb("one", [P, 1])
        b_dt = sb("b_dt", [P, KH])
        skip_d = sb("skip_d", [P, KH])
        decay = sb("decay", [P, KH, NSTATE])
        bmat = sb("bmat", [P, KH, NSTATE])
        cmat = sb("cmat", [P, KH, NSTATE])
        cols = sb("cols", [P, 8, KH])
        bn_a = sb("bn_a", [P, KH])
        bn_c = sb("bn_c", [P, KH])
        b_down = sb("b_down", [P, E0 // 2])
        wr = sb("wr", [P, KH, E0])
        br = sb("br", [E0, E0])
        gate_w = sb("gate_w", [P, KH, E1])
        member_r = sb("member_r", [GS, GT], F32R)
        rel = sb("rel", [33, HEADS])
        base = sb("base", [33, 2 * SEQ])
        rel_bias = sb("rel_bias", [P, HP, SEQ])

        wp = sb("wp", [P, KP, HID])
        w_dt = [sb(f"w_dt{s}", [P, KH, HID], F32R) for s in "hl"]
        w_down = [sb(f"w_down{s}", [P, KH, E0 * H0], F32R) for s in "hl"]
        w_up = [sb(f"w_up{s}", [P, E0 * H0 // P, HID], F32R) for s in "hl"]
        w_qkv = [sb(f"w_qkv{s}", [P, KH, 3 * INNER], F32R) for s in "hl"]
        w_o = [sb(f"w_o{s}", [P, HP, HID], F32R) for s in "hl"]
        b_up = [sb(f"b_up{s}", [E0, HID], F32R) for s in "hl"]

        patches = sb("patches", [P, 2, KP, GT // 2])
        h0 = [sb(f"h0_{i}", [P, TILES, HID]) for i in range(2)]
        tok_a = sb("tok_a", [P, TILES, HID])
        u_hi = sb("u_hi", [P, KH, GT], F32R)
        u_lo = sb("u_lo", [P, KH, GT], F32R)
        u_t = sb("u_t", [P, KH, GT])
        dt = [sb(f"dt_{i}", [P, KH, GT]) for i in range(2)]
        drive = [sb(f"drive_{i}", [P, KH, GT]) for i in range(2)]
        y_t = sb("y_t", [P, KH, GT])
        state = sb("state", [P, 2, GT])
        feed = sb("feed", [P, 2, GT])
        stats_a = sb("stats_a", [P, TILES, 6])
        mv_a = sb("mv_a", [P, TILES, 2])
        ln_a = sb("ln_a", [P, TILES, 2])

        h = sb("h", [P, TILES, HID])
        tok_b = sb("tok_b", [P, TILES, HID])
        z_hi = sb("z_hi", [P, KH, GT], F32R)
        z_lo = sb("z_lo", [P, KH, GT], F32R)
        z_t = sb("z_t", [P, KH, GT])
        mid_hi = sb("mid_hi", [P, 4, GT], F32R)
        mid_lo = sb("mid_lo", [P, 4, GT], F32R)
        qkv = sb("qkv", [P, 12, GT])
        score = sb("score", [P, 2, GT])
        probs_t = sb("probs_t", [P, 2, GT])
        stats_b = sb("stats_b", [P, TILES, 6])
        mv_b = sb("mv_b", [P, TILES, 2])
        ln_b = sb("ln_b", [P, TILES, 6])
        zsum = sb("zsum", [P, KH, GS])
        zbn = sb("zbn", [P, KH, GS])
        pick = sb("pick", [E0, 8, E0])
        pick_i = sb("pick_i", [E0, E0], U32)
        pen = sb("pen", [E0, E0, H0], F32R)
        oneh_r = sb("oneh_r", [E0, E0], F32R)
        oneh_t = sb("oneh_t", [E0, GT], F32R)
        gtok = sb("gtok", [P, TILES])
        srow = sb("srow", [P, 2, 3, 8])
        rsc = sb("rsc", [P, TILES, E1])
        rtop = sb("rtop", [P, TILES, 8])
        ridx = sb("ridx", [P, TILES, 8], U32)
        ridf = sb("ridf", [P, TILES, 8])
        rw = sb("rw", [P, TILES, 4])
        roh = sb("roh", [P, TILES, 2, E1])

        bank_x = [ctx.enter_context(nc.psum_tensor(f"bank_x{i}", [P, GT], F32)) for i in range(2)]
        bank_a = [ctx.enter_context(nc.psum_tensor(f"bank_a{i}", [P, GT], F32)) for i in range(2)]
        bank_b = [ctx.enter_context(nc.psum_tensor(f"bank_b{i}", [P, GT], F32)) for i in range(4)]

        const_in, wp_in, w_dt_in, w_in = signal("const_in"), signal("wp_in"), signal("w_dt_in"), signal("w_in")
        setup_v, setup_a, setup_p = signal("setup_v"), signal("setup_a"), signal("setup_p")
        w_hi_done, w_lo_done, small_split = signal("w_hi_done"), signal("w_lo_done"), signal("small_split")
        bias_mm, bias_out = signal("bias_mm"), signal("bias_out")
        x_in = [signal(f"x_in{i}", 16) for i in range(2)]
        patch_mm, patch_add = signal("patch_mm", 2), signal("patch_add", 2)
        stat_a, mean_a, rstd_a = signal("stat_a", 4), signal("mean_a", 4), signal("rstd_a", 2)
        u_tok, u_turned, u_copied = signal("u_tok", 4), signal("u_turned", 2), signal("u_copied", 4)
        u_split, dt_mm, dt_in = signal("u_split", 2), signal("dt_mm", 2), signal("dt_in", 2)
        sp_v, sp_a = signal("sp_v", 6), signal("sp_a", 2)
        decay_in, feed_in, scanned, y_sum = signal("decay_in", STEPS), signal("feed_in", STEPS), signal("scanned", STEPS), signal("y_sum", 2 + STEPS)
        y_turned, joined = signal("y_turned", 2), signal("joined", 2)
        stat_b, mean_b = signal("stat_b", 12), signal("mean_b", 12)
        ln2_a, ln2_v = signal("ln2_a", 4), signal("ln2_v", 2)
        rstd_b = signal("rstd_b", 4)
        z_tok, z2_turned, z2_copied, z2_split = signal("z_tok", 12), signal("z2_turned", 2), signal("z2_copied", 4), signal("z2_split", 2)
        pick_v, pick_mm, pick_exp = signal("pick_v", 16), signal("pick_mm", 3), signal("pick_exp", 1)
        down_mm, hid_copied, hid_split = signal("down_mm", 4), signal("hid_copied", 8), signal("hid_split", 4)
        up_mm, h_ffn = signal("up_mm", 2), signal("h_ffn", 4)
        z3_turned, z3_hi, z3_split = signal("z3_turned", 2), signal("z3_hi", 2), signal("z3_split", 2)
        qkv_mm, q_out, k_out, v_out = signal("qkv_mm", 12), signal("q_out", 4), signal("k_out", 4), signal("v_out", 4)
        bo_added = signal("bo_added", 1)
        s_mm, s_bias, s_max, s_sub = signal("s_mm", 4), signal("s_bias", 4), signal("s_max", 4), signal("s_sub", 4)
        s_exp, s_sum, s_rcp, s_norm = signal("s_exp", 4), signal("s_sum", 4), signal("s_rcp", 4), signal("s_norm", 4)
        pt_mm, pt_out, o_half, o_mm = signal("pt_mm", 4), signal("pt_out", 4), signal("o_half", 4), signal("o_mm", 4)
        o_hi, o_split, proj_mm, h_attn = signal("o_hi", 4), signal("o_split", 4), signal("proj_mm", 2), signal("h_attn", 2)
        h_stored, z_stored = signal("h_stored", 16), signal("z_stored", 16)
        z4_turned, z4_out = signal("z4_turned", 2), signal("z4_out", 2)
        gate_mm, gate_exp, gate_v = signal("gate_mm", 1), signal("gate_exp", 1), signal("gate_v", 15 + 2 * TILES)

        block = ctx.enter_context(nc.Block())

        raw = qkv[:, :, :].rearrange("p a b -> p (a b)")
        raw_b = tok_b[:, :, :].rearrange("p a b -> p (a b)")
        at, staged = 0, []
        for name, pair in (("w_down", w_down), ("w_up", w_up), ("w_qkv", w_qkv), ("w_o", w_o)):
            n = pair[0].shape[1] * pair[0].shape[2]
            staged.append((name, pair, raw[:, at:at + n]))
            at += n
        staged.insert(0, ("w_dt", w_dt, raw_b[:, 0:KH * HID]))
        tokb = raw_b[:, 768:1024]
        raw_member = score[0:GS, 0, :]
        small = [("pos", posb[:, :]), ("tokb", tokb), ("bo", bo[:, :]), ("iota", iota[:, :]),
                 ("ident", ident[:, :]), ("b_dt", b_dt[:, :]), ("skip_d", skip_d[:, :]),
                 ("a_log", decay[:, :, :]), ("bmat", bmat[:, :, :]), ("cmat", cmat[:, :, :]),
                 ("cols", cols[:, :, :]), ("b_down", b_down[:, :]), ("wr", wr[:, :, :]), ("br", br[:, :]),
                 ("gate_w", gate_w[:, :, :]), ("member", raw_member), ("rel", rel[0:32, :]),
                 ("base", base[:, :]), ("b_up", raw_b[0:E0, 512:768])]

        def run(who, engine, own):
            for n in range(-2, GROUPS + 1):
                chains = {"b": iter(BACK), "f": iter(FRONT), "s": iter(STEP)}
                for chain in MERGED[who]:
                    piece, ahead, *args = next(chains[chain])
                    if piece in own and 0 <= n + ahead < GROUPS:
                        own[piece](engine, n + ahead, *args)

        def by_sample(tiles, t):
            return tiles[:, :, t * P:(t + 1) * P].rearrange("p j (y q) -> p j y q", q=SEQ)

        def heads_out(t):
            return bank_b[2 + t % 2][:, :].rearrange("p (y j q) -> p j y q", j=HP, q=SEQ)

        def load_patches(sp, g, b):
            wait(sp, patch_mm(g - 1, b + 1))
            sp.dma_start(patches[:, b, :, :], d["x"][g, b]).then_inc(x_in[b].sem, 16)

        def store_h(sp, g, b):
            if b == 1:
                wait(sp, h_attn(g, 2))
                sp.dma_start(d["h_mid"][g], h[:, :, :]).then_inc(h_stored.sem, 16)

        def store_z(sp, g):
            wait(sp, z4_out(g, 2))
            sp.dma_start(d["z_mid"][g], qkv[:, 10:12, :]).then_inc(z_stored.sem, 16)

        @block.sync
        def _(sp):
            sp.dma_start(wp[:, :, :], d["wp"]).then_inc(wp_in.sem, 16)
            load_patches(sp, 0, 0)
            load_patches(sp, 0, 1)
            for name, to in small:
                sp.dma_start(to, d[name]).then_inc(const_in.sem, 16)
            for name, _, to in staged:
                sp.dma_start(to, d[name].rearrange("p a b -> p (a b)")).then_inc((w_dt_in if name == "w_dt" else w_in).sem, 16)

            def next_patches(sp, g, b):
                if g + 1 < GROUPS:
                    load_patches(sp, g + 1, b)

            run("sync", sp, {"patch": next_patches, "proj": store_h, "gate": store_z})
            wait(sp, h_stored(GROUPS, 0))
            wait(sp, z_stored(GROUPS, 0))

        @block.gpsimd
        def _(pool):
            pool.wait_ge(const_in.sem, 16 * len(small))
            pool.tensor_tensor(posb[:, :], posb[:, :], tokb, ALU.add).then_inc(setup_p.sem, 1)
            pool.tensor_tensor(cmat[:, :, :], cmat[:, :, :], bmat[:, :, :], ALU.mult).then_inc(setup_p.sem, 1)

            def step(pool, g, i):
                if i == 0:
                    wait(pool, u_copied(g, 4))
                    wait(pool, y_turned(g, 0))
                    for c in range(KH):
                        pool.tensor_scalar(y_t[:, c, :], u_t[:, c, :], skip_d[:, c:c + 1], None, ALU.mult).then_inc(y_sum.sem, 1)
                c = i // NSTATE
                wait(pool, scanned(g, i + 1))
                wait(pool, y_sum(g, 2 + i))
                pool.tensor_tensor(y_t[:, c, :], state[:, i % 2, :], y_t[:, c, :], ALU.add).then_inc(y_sum.sem, 1)

            def add_output_bias(pool, g):
                wait(pool, z_tok(g, 8))
                pool.tensor_tensor(h[:, :, :], h[:, :, :], bo[:, None, :].broadcast_to([P, TILES, HID]),
                                   ALU.add).then_inc(bo_added.sem, 1)

            run("gpsimd", pool, {"step": step, "ln3": add_output_bias})

        def rstd(act, g, k):
            wait(act, mean_b(g, 4 * (k + 1)))
            act.activation(ln_b[:, :, 0], mv_b[:, :, 1], ACT.Ln, bias=eps[:, 0:1]).then_inc(rstd_b.sem, 1)
            wait(act, rstd_b(g, 2 * k - 1))
            act.activation(ln_b[:, :, 5], ln_b[:, :, 0], ACT.Exp, scale=-0.5).then_inc(rstd_b.sem, 1)

        @block.scalar
        def _(act):
            act.preload_act_table_set("natural_log_exp_and_others")
            act.wait_ge(setup_v.sem, 5)
            act.wait_ge(const_in.sem, 16 * len(small))
            act.activation(decay[:, :, :], decay[:, :, :], ACT.Exp).then_inc(setup_a.sem, 1)
            act.activation(bn_a[:, :], cols[:, 5, :], ACT.Ln, bias=eps[:, 0:1]).then_inc(setup_a.sem, 1)
            act.wait_ge(setup_a.sem, 2)
            act.activation(bn_a[:, :], bn_a[:, :], ACT.Exp, scale=-0.5).then_inc(setup_a.sem, 1)

            def ln1(act, g):
                wait(act, mean_a(g, 4))
                act.activation(ln_a[:, :, 0], mv_a[:, :, 1], ACT.Ln, bias=eps[:, 0:1]).then_inc(rstd_a.sem, 1)
                wait(act, rstd_a(g, 1))
                act.activation(ln_a[:, :, 1], ln_a[:, :, 0], ACT.Exp, scale=-0.5).then_inc(rstd_a.sem, 1)

            def turn1(act, g):
                for c in range(KH):
                    wait(act, u_turned(g, c + 1))
                    act.activation(u_hi[:, c, :], bank_a[c][:, :], ACT.Copy).then_inc(u_copied.sem, 1)
                    if c == 0:
                        wait(act, y_sum(g - 1, 2))
                        wait(act, sp_v(g, 0))
                    act.activation(u_t[:, c, :], bank_a[c][:, :], ACT.Copy).then_inc(u_copied.sem, 1)

            def dt_bias(act, g):
                wait(act, scanned(g - 1, 0))
                for c in range(KH):
                    wait(act, dt_mm(g, c + 1))
                    act.activation(dt[g % 2][:, c, :], bank_a[c][:, :], ACT.Identity, bias=b_dt[:, c:c + 1]).then_inc(dt_in.sem, 1)

            def soft(act, g):
                wait(act, sp_v(g, 1))
                act.activation(drive[g % 2][:, :, :], drive[g % 2][:, :, :], ACT.Exp).then_inc(sp_a.sem, 1)
                wait(act, sp_v(g, 3))
                act.activation(drive[g % 2][:, :, :], drive[g % 2][:, :, :], ACT.Ln, bias=one[:, 0:1]).then_inc(sp_a.sem, 1)

            def step(act, g, i):
                if i == 0:
                    wait(act, sp_v(g, 6))
                    act.wait_ge(setup_v.sem, 6)
                c, n = divmod(i, NSTATE)
                wait(act, scanned(g, i - 1))
                act.activation(bank_x[i % 2][:, :].rearrange("p (b t) -> p b t", t=SEQ)[:, :, 1:SEQ],
                               dt[g % 2][:, c, :].rearrange("p (b t) -> p b t", t=SEQ)[:, :, 1:SEQ],
                               ACT.Exp, scale=decay[:, c, n:n + 1]).then_inc(decay_in.sem, 1)
                act.activation(feed[:, i % 2, :], drive[g % 2][:, c, :], ACT.Copy, scale=cmat[:, c, n:n + 1]).then_inc(feed_in.sem, 1)

            def ln2(act, g):
                wait(act, mean_b(g, 4))
                act.activation(ln_b[:, :, 0], mv_b[:, :, 1], ACT.Ln, bias=eps[:, 0:1]).then_inc(ln2_a.sem, 1)
                wait(act, ln2_a(g, 1))
                act.activation(ln_b[:, :, 1], ln_b[:, :, 0], ACT.Exp, scale=-1.0).then_inc(ln2_a.sem, 1)
                wait(act, ln2_v(g, 1))
                act.activation(ln_b[:, :, 3], ln_b[:, :, 2], ACT.Ln, bias=eps[:, 0:1]).then_inc(ln2_a.sem, 1)
                wait(act, ln2_v(g, 2))
                act.activation(ln_b[:, :, 5], ln_b[:, :, 4], ACT.Exp, scale=-0.5).then_inc(ln2_a.sem, 1)

            def turn2(act, g):
                for c in range(KH):
                    wait(act, z2_turned(g, c + 1))
                    act.activation(z_hi[:, c, :], bank_b[c][:, :], ACT.Identity, bias=cols[:, 1, c:c + 1],
                                   scale=cols[:, 0, c:c + 1]).then_inc(z2_copied.sem, 1)
                    act.activation(z_t[:, c, :], bank_b[c][:, :], ACT.Identity, bias=cols[:, 1, c:c + 1],
                                   scale=cols[:, 0, c:c + 1]).then_inc(z2_copied.sem, 1)

            def pick_one(act, g):
                wait(act, pick_v(g, 6))
                act.activation(pick[:, 1, :], pick[:, 0, :], ACT.Exp, bias=pick[:, 3, 0:1],
                               accum_out=pick[:, 3, 1:2]).then_inc(pick_exp.sem, 1)

            def down(act, g):
                for e in range(4):
                    wait(act, down_mm(g, e + 1))
                    act.activation(mid_hi[:, e, :], bank_b[e][:, :], ACT.Relu, bias=b_down[:, e:e + 1]).then_inc(hid_copied.sem, 1)
                    act.activation(qkv[:, e, :], bank_b[e][:, :], ACT.Relu, bias=b_down[:, e:e + 1]).then_inc(hid_copied.sem, 1)

            def turn3(act, g):
                for c in range(KH):
                    wait(act, z3_turned(g, c + 1))
                    act.activation(z_hi[:, c, :], bank_b[2 + c][:, :], ACT.Copy).then_inc(z3_hi.sem, 1)

            def queries(act, g):
                for m in range(4):
                    wait(act, qkv_mm(g, m + 1))
                    act.activation(qkv[:, m, :], bank_b[m][:, :], ACT.Copy, scale=DH**-0.5).then_inc(q_out.sem, 1)

            def values(act, g):
                for m in range(4):
                    wait(act, qkv_mm(g, 8 + m + 1))
                    if m == 2:
                        wait(act, z_stored(g, 0))
                    act.activation(qkv[:, 8 + m, :], bank_b[m][:, :], ACT.Copy).then_inc(v_out.sem, 1)

            def scores(act, g, t):
                wait(act, s_sub(g, t + 1))
                act.activation(score[:, t % 2, :], score[:, t % 2, :], ACT.Exp).then_inc(s_exp.sem, 1)

            def heads(act, g, t):
                wait(act, pt_mm(g, t + 1))
                wait(act, o_mm(g, t - 1) if t >= 2 else o_mm(g, 0))
                act.activation(probs_t[:, t % 2, :], bank_b[t % 2][:, :], ACT.Copy).then_inc(pt_out.sem, 1)

            def outputs(act, g, t):
                wait(act, o_mm(g, t + 1))
                act.activation(by_sample(mid_hi, t), heads_out(t), ACT.Copy).then_inc(o_hi.sem, 1)

            def gate(act, g):
                for c in range(KH):
                    wait(act, z4_turned(g, c + 1))
                    act.activation(qkv[:, 10 + c, :], bank_b[2 + c][:, :], ACT.Copy).then_inc(z4_out.sem, 1)
                wait(act, gate_mm(g, 1))
                act.activation(rsc[:, :, :], bank_b[0][:, 0:TILES * E1].rearrange("p (t e) -> p t e", e=E1),
                               ACT.Exp, scale=-1.0).then_inc(gate_exp.sem, 1)

            run("scalar", act, {"ln1": ln1, "turn1": turn1, "dt": dt_bias, "soft": soft, "step": step, "ln2": ln2,
                      "turn2": turn2, "pick": pick_one, "down": down, "ln3": lambda a, g: rstd(a, g, 1), "turn3": turn3,
                      "q": queries, "v": values, "scores": scores, "heads": heads, "outputs": outputs,
                      "ln4": lambda a, g: rstd(a, g, 2), "gate": gate})

        def norm_stats(dve, src, stats, mv, stat, mean, g, k, ready, tiles=range(TILES)):
            for t in tiles:
                ready(t)
                dve.bn_stats(stats[:, t, :], src[:, t, :]).then_inc(stat.sem, 1)
            for t in tiles:
                wait(dve, stat(g, 4 * k + t + 1))
                dve.bn_aggr(mv[:, t, :], stats[:, t, :]).then_inc(mean.sem, 1)

        def normalise(dve, g):
            for t in range(TILES):
                dve.tensor_scalar(tok_b[:, t, :], h[:, t, :], mv_b[:, t, 0:1], ln_b[:, t, 5:6],
                                  ALU.subtract, ALU.mult).then_inc(z_tok.sem, 1)

        @block.vector
        def _(dve):
            dve.memset(eps[:, :], EPS).then_inc(setup_v.sem, 1)
            dve.memset(one[:, :], 1.0).then_inc(setup_v.sem, 1)
            dve.memset(rel[32:33, :], MASKED).then_inc(setup_v.sem, 1)
            for i in range(2):
                dve.memset(bank_x[i][:, :], 0.0).then_inc(setup_v.sem, 1)
            dve.wait_ge(const_in.sem, 16 * len(small))
            dve.tensor_copy(b_up[0][:, :], raw_b[0:E0, 512:768]).then_inc(w_hi_done.sem, 1)
            dve.wait_ge(w_dt_in.sem, 16)

            def split(i):
                name, pair, src = staged[i]
                hi, lo = (w[:, :, :].rearrange("p a b -> p (a b)") for w in pair)
                dve.tensor_copy(hi, src).then_inc(w_hi_done.sem, 1)
                dve.wait_ge(w_hi_done.sem, i + 2)
                dve.tensor_tensor(lo, src, hi.bitcast(F32), ALU.subtract).then_inc(w_lo_done.sem, 1)

            split(0)
            dve.tensor_tensor(b_up[1][:, :], raw_b[0:E0, 512:768], b_up[0][:, :].bitcast(F32), ALU.subtract).then_inc(small_split.sem, 1)
            dve.tensor_copy(member_r[:, :], raw_member).then_inc(small_split.sem, 1)
            dve.tensor_scalar(rel[0:32, :], rel[0:32, :], DH**0.5, None, ALU.mult).then_inc(small_split.sem, 1)
            dve.wait_ge(setup_a.sem, 3)
            dve.tensor_scalar(decay[:, :, :], decay[:, :, :], -1.0, None, ALU.mult).then_inc(setup_v.sem, 1)
            dve.tensor_tensor(bn_a[:, :], bn_a[:, :], cols[:, 2, :], ALU.mult).then_inc(setup_v.sem, 1)
            dve.wait_ge(setup_v.sem, 7)
            dve.tensor_tensor(bn_c[:, :], bn_a[:, :], cols[:, 4, :], ALU.mult).then_inc(setup_v.sem, 1)
            dve.wait_ge(setup_v.sem, 8)
            dve.tensor_tensor(bn_c[:, :], cols[:, 3, :], bn_c[:, :], ALU.subtract).then_inc(setup_v.sem, 1)
            dve.tensor_scalar(bn_a[:, :], bn_a[:, :], 1.0 / SEQ, None, ALU.mult).then_inc(setup_v.sem, 1)
            dve.wait_ge(setup_p.sem, 2)

            def patch(dve, g, b):
                wait(dve, patch_mm(g, b + 1))
                wait(dve, joined(g - 1, 0))
                dve.tensor_tensor(h0[g % 2][:, 2 * b:2 * b + 2, :], bank_a[b][:, :].rearrange("p (t n) -> p t n", t=2),
                                  posb[:, None, :].broadcast_to([P, 2, HID]), ALU.add).then_inc(patch_add.sem, 1)
                norm_stats(dve, h0[g % 2], stats_a, mv_a, stat_a, mean_a, g, 0, lambda t: wait(dve, patch_add(g, b + 1)),
                           range(2 * b, 2 * b + 2))

            def ln1(dve, g):
                wait(dve, rstd_a(g, 2))
                wait(dve, sp_v(g, 0))
                for t in range(TILES):
                    dve.tensor_scalar(tok_a[:, t, :], h0[g % 2][:, t, :], mv_a[:, t, 0:1], ln_a[:, t, 1:2],
                                      ALU.subtract, ALU.mult).then_inc(u_tok.sem, 1)

            def turn1(dve, g):
                for c in range(KH):
                    wait(dve, u_copied(g, 2 * c + 2))
                    dve.tensor_tensor(u_lo[:, c, :], bank_a[c][:, :], u_hi[:, c, :].bitcast(F32), ALU.subtract).then_inc(u_split.sem, 1)

            def dt_bias(dve, g):
                wait(dve, dt_in(g, 2))
                wait(dve, scanned(g - 1, 0))
                dve.scalar_tensor_tensor(out=drive[g % 2][:, :, :], in0=dt[g % 2][:, :, :], scalar=-1.0, in1=dt[g % 2][:, :, :],
                                         op0=ALU.mult, op1=ALU.min).then_inc(sp_v.sem, 1)

            def soft(dve, g):
                rest = tok_a[:, :, :].rearrange("p a b -> p (a b)").rearrange("p (c t) -> p c t", c=KH)
                wait(dve, sp_a(g, 1))
                dve.tensor_scalar(rest, drive[g % 2][:, :, :], 1.0, -1.0, ALU.add, ALU.add).then_inc(sp_v.sem, 1)
                wait(dve, sp_v(g, 2))
                dve.tensor_tensor(rest, drive[g % 2][:, :, :], rest, ALU.subtract).then_inc(sp_v.sem, 1)
                wait(dve, sp_v(g, 3))
                dve.scalar_tensor_tensor(out=dt[g % 2][:, :, :], in0=dt[g % 2][:, :, :], scalar=0.0, in1=rest,
                                         op0=ALU.max, op1=ALU.add).then_inc(sp_v.sem, 1)
                wait(dve, sp_a(g, 2))
                wait(dve, sp_v(g, 4))
                dve.tensor_tensor(dt[g % 2][:, :, :], dt[g % 2][:, :, :], drive[g % 2][:, :, :], ALU.add).then_inc(sp_v.sem, 1)
                wait(dve, sp_v(g, 5))
                dve.tensor_tensor(drive[g % 2][:, :, :], dt[g % 2][:, :, :], u_t[:, :, :], ALU.mult).then_inc(sp_v.sem, 1)

            def step(dve, g, i):
                wait(dve, feed_in(g, i + 1))
                wait(dve, y_sum(g, i + 1 if i >= 2 else i - 1))
                dve.tensor_tensor_scan(state[:, i % 2, :], bank_x[i % 2][:, :], feed[:, i % 2, :], 0.0,
                                       ALU.mult, ALU.add).then_inc(scanned.sem, 1)

            def join(dve, g):
                wait(dve, h_stored(g, 0))
                wait(dve, z_tok(g, 0))
                for b in range(2):
                    wait(dve, y_turned(g, b + 1))
                    dve.tensor_tensor(h[:, 2 * b:2 * b + 2, :], h0[g % 2][:, 2 * b:2 * b + 2, :],
                                      bank_a[b][:, :].rearrange("p (t n) -> p t n", t=2), ALU.add).then_inc(joined.sem, 1)
                norm_stats(dve, h, stats_b, mv_b, stat_b, mean_b, g, 0, lambda t: wait(dve, joined(g, t // 2 + 1)))

            def ln2(dve, g):
                wait(dve, ln2_a(g, 2))
                dve.tensor_tensor(ln_b[:, :, 2], mv_b[:, :, 1], ln_b[:, :, 1], ALU.mult).then_inc(ln2_v.sem, 1)
                wait(dve, ln2_a(g, 3))
                dve.tensor_tensor(ln_b[:, :, 4], ln_b[:, :, 0], ln_b[:, :, 3], ALU.add).then_inc(ln2_v.sem, 1)
                wait(dve, ln2_a(g, 4))
                dve.wait_ge(w_lo_done.sem, len(staged))
                normalise(dve, g)

            def turn2(dve, g):
                for c in range(KH):
                    wait(dve, z2_copied(g, 2 * c + 2))
                    dve.tensor_tensor(z_lo[:, c, :], z_t[:, c, :], z_hi[:, c, :].bitcast(F32), ALU.subtract).then_inc(z2_split.sem, 1)
                dve.tensor_reduce(zsum[:, :, :], z_t[:, :, :].rearrange("p c (b t) -> p c b t", t=SEQ), AX_X, ALU.add).then_inc(pick_v.sem, 1)
                wait(dve, pick_v(g, 1))
                for c in range(KH):
                    dve.tensor_scalar(zbn[:, c, :], zsum[:, c, :], bn_a[:, c:c + 1], bn_c[:, c:c + 1],
                                      ALU.mult, ALU.add).then_inc(pick_v.sem, 1)

            def pick_one(dve, g):
                wait(dve, pick_mm(g, 1))
                dve.tensor_tensor(pick[:, 0, :], bank_b[2][0:GS, 0:E0], br[:, :], ALU.add).then_inc(pick_v.sem, 1)
                wait(dve, pick_v(g, 4))
                dve.tensor_reduce(pick[:, 3, 2:3], pick[:, 0, :], AX_X, ALU.max).then_inc(pick_v.sem, 1)
                wait(dve, pick_v(g, 5))
                dve.tensor_scalar(pick[:, 3, 0:1], pick[:, 3, 2:3], -1.0, None, ALU.mult).then_inc(pick_v.sem, 1)
                wait(dve, pick_exp(g, 1))
                dve.reciprocal(pick[:, 3, 3:4], pick[:, 3, 1:2]).then_inc(pick_v.sem, 1)
                wait(dve, pick_v(g, 7))
                dve.tensor_scalar(pick[:, 2, :], pick[:, 1, :], pick[:, 3, 3:4], None, ALU.mult).then_inc(pick_v.sem, 1)
                wait(dve, pick_v(g, 8))
                dve.max(pick[:, 4, :], pick[:, 2, :]).then_inc(pick_v.sem, 1)
                wait(dve, pick_v(g, 9))
                dve.max_index(pick_i[:, :], pick[:, 4, :], pick[:, 2, :]).then_inc(pick_v.sem, 1)
                wait(dve, pick_v(g, 10))
                dve.tensor_copy(pick[:, 5, :], pick_i[:, :]).then_inc(pick_v.sem, 1)
                wait(dve, pick_v(g, 11))
                dve.tensor_scalar(pick[:, 6, :], iota[0:GS, 0:E0], pick[:, 5, 0:1], None, ALU.is_equal).then_inc(pick_v.sem, 1)
                wait(dve, pick_v(g, 12))
                dve.tensor_scalar(pen[:, :, :], pick[:, 6, :, None].broadcast_to([GS, E0, H0]), 1.0, PENALTY,
                                  ALU.subtract, ALU.mult).then_inc(pick_v.sem, 1)
                dve.tensor_copy(oneh_r[:, :], pick[:, 6, :]).then_inc(pick_v.sem, 1)

            def down(dve, g):
                wait(dve, pick_mm(g, 3))
                dve.tensor_copy(oneh_t[:, :], bank_b[3][0:E0, :]).then_inc(pick_v.sem, 1)
                dve.tensor_copy(gtok[:, :], bank_b[2][:, 0:TILES]).then_inc(pick_v.sem, 1)
                for e in range(4):
                    wait(dve, hid_copied(g, 2 * e + 2))
                    dve.tensor_tensor(mid_lo[:, e, :], qkv[:, e, :], mid_hi[:, e, :].bitcast(F32), ALU.subtract).then_inc(hid_split.sem, 1)

            def up(dve, g):
                for t in range(TILES):
                    wait(dve, up_mm(g, t // 2 + 1))
                    dve.scalar_tensor_tensor(out=h[:, t, :], in0=bank_b[t // 2][:, (t % 2) * HID:(t % 2 + 1) * HID],
                                             scalar=gtok[:, t:t + 1], in1=h[:, t, :], op0=ALU.mult,
                                             op1=ALU.add).then_inc(h_ffn.sem, 1)
                norm_stats(dve, h, stats_b, mv_b, stat_b, mean_b, g, 1, lambda t: wait(dve, h_ffn(g, t + 1)))

            def ln3(dve, g):
                wait(dve, rstd_b(g, 2))
                wait(dve, z2_turned(g, 2))
                normalise(dve, g)

            def turn3(dve, g):
                for c in range(KH):
                    wait(dve, z3_hi(g, c + 1))
                    dve.tensor_tensor(z_lo[:, c, :], bank_b[2 + c][:, :], z_hi[:, c, :].bitcast(F32), ALU.subtract).then_inc(z3_split.sem, 1)

            def keys(dve, g):
                for m in range(4):
                    wait(dve, qkv_mm(g, 4 + m + 1))
                    dve.tensor_copy(qkv[:, 4 + m, :], bank_b[m][:, :]).then_inc(k_out.sem, 1)

            def by_head(t):
                return score[:, t % 2, :].rearrange("p (a k) -> p a k", k=SEQ)

            def scores(dve, g, t):
                r = srow[:, t % 2]
                wait(dve, s_mm(g, t + 1))
                wait(dve, pt_mm(g, t - 1) if t >= 2 else pt_mm(g, 0))
                dve.tensor_tensor(score[:, t % 2, :].rearrange("p (j y k) -> p j y k", j=HP, y=2),
                                  bank_a[t % 2][:, :].rearrange("p (j y k) -> p j y k", j=HP, y=2),
                                  rel_bias[:, :, None, :].broadcast_to([P, HP, 2, SEQ]), ALU.add).then_inc(s_bias.sem, 1)
                wait(dve, s_bias(g, t + 1))
                dve.tensor_reduce(r[:, 0, :], by_head(t), AX_X, ALU.max).then_inc(s_max.sem, 1)
                wait(dve, s_max(g, t + 1))
                dve.tensor_tensor(by_head(t), by_head(t), r[:, 0, :, None].broadcast_to([P, 8, SEQ]), ALU.subtract).then_inc(s_sub.sem, 1)

            def probs(dve, g, t):
                r = srow[:, t % 2]
                wait(dve, s_exp(g, t + 1))
                dve.tensor_reduce(r[:, 1, :], by_head(t), AX_X, ALU.add).then_inc(s_sum.sem, 1)
                wait(dve, s_sum(g, t + 1))
                dve.reciprocal(r[:, 2, :], r[:, 1, :]).then_inc(s_rcp.sem, 1)
                wait(dve, s_rcp(g, t + 1))
                dve.tensor_tensor(by_head(t), by_head(t), r[:, 2, :, None].broadcast_to([P, 8, SEQ]), ALU.mult).then_inc(s_norm.sem, 1)

            def outputs(dve, g, t):
                wait(dve, o_hi(g, t + 1))
                dve.tensor_tensor(by_sample(mid_lo, t), heads_out(t), by_sample(mid_hi, t).bitcast(F32),
                                  ALU.subtract).then_inc(o_split.sem, 1)

            def proj(dve, g, b):
                wait(dve, bo_added(g, 1))
                wait(dve, proj_mm(g, b + 1))
                dve.tensor_tensor(h[:, 2 * b:2 * b + 2, :], bank_a[b][:, :].rearrange("p (t n) -> p t n", t=2),
                                  h[:, 2 * b:2 * b + 2, :], ALU.add).then_inc(h_attn.sem, 1)
                norm_stats(dve, h, stats_b, mv_b, stat_b, mean_b, g, 2, lambda t: wait(dve, h_attn(g, b + 1)),
                           range(2 * b, 2 * b + 2))

            def ln4(dve, g):
                wait(dve, rstd_b(g, 4))
                wait(dve, z3_turned(g, 2))
                normalise(dve, g)

            def gate(dve, g):
                wait(dve, gate_exp(g, 1))
                dve.tensor_scalar(rsc[:, :, :], rsc[:, :, :], 1.0, None, ALU.add).then_inc(gate_v.sem, 1)
                wait(dve, gate_v(g, 1))
                dve.reciprocal(rsc[:, :, :], rsc[:, :, :]).then_inc(gate_v.sem, 1)
                wait(dve, gate_v(g, 2))
                for t in range(TILES):
                    dve.max(rtop[:, t, :], rsc[:, t, :]).then_inc(gate_v.sem, 1)
                for t in range(TILES):
                    wait(dve, gate_v(g, 3 + t))
                    dve.max_index(ridx[:, t, :], rtop[:, t, :], rsc[:, t, :]).then_inc(gate_v.sem, 1)
                wait(dve, gate_v(g, 10))
                dve.tensor_copy(ridf[:, :, :], ridx[:, :, :]).then_inc(gate_v.sem, 1)
                dve.scalar_tensor_tensor(out=rw[:, :, 0:1], in0=rtop[:, :, 0:1], scalar=1e-20, in1=rtop[:, :, 1:2],
                                         op0=ALU.add, op1=ALU.add).then_inc(gate_v.sem, 1)
                wait(dve, gate_v(g, 12))
                dve.reciprocal(rw[:, :, 1:2], rw[:, :, 0:1]).then_inc(gate_v.sem, 1)
                wait(dve, gate_v(g, 13))
                dve.scalar_tensor_tensor(out=rw[:, :, 2:4], in0=rtop[:, :, 0:2], scalar=TOPK_SCALE,
                                         in1=rw[:, :, 1:2].broadcast_to([P, TILES, 2]), op0=ALU.mult, op1=ALU.mult).then_inc(gate_v.sem, 1)
                wait(dve, gate_v(g, 14))
                for t in range(TILES):
                    for k in range(2):
                        dve.tensor_scalar(roh[:, t, k, :], iota[:, :], ridf[:, t, k:k + 1], rw[:, t, 2 + k:3 + k],
                                          ALU.is_equal, ALU.mult).then_inc(gate_v.sem, 1)
                wait(dve, gate_v(g, 14 + 2 * TILES))
                dve.tensor_tensor(route[:, g * TILES:(g + 1) * TILES, :], roh[:, :, 0, :], roh[:, :, 1, :],
                                  ALU.add).then_inc(gate_v.sem, 1)

            def relative(dve, g):
                if g == 0:
                    dve.wait_ge(w_in.sem, 16 * (len(staged) - 1))
                    for i in range(1, len(staged)):
                        split(i)
                    dve.wait_ge(bias_mm.sem, 1)
                    dve.tensor_copy(rel_bias[:, :, :], bank_b[0][:, 0:SEQ * HP].rearrange("p (k j) -> p j k", j=HP)).then_inc(bias_out.sem, 1)

            run("vector", dve, {"relative": relative, "patch": patch, "ln1": ln1, "turn1": turn1, "dt": dt_bias, "soft": soft,
                      "step": step, "join": join, "ln2": ln2, "turn2": turn2, "pick": pick_one, "down": down, "up": up,
                      "ln3": ln3, "turn3": turn3, "k": keys, "scores": scores, "probs": probs, "outputs": outputs,
                      "proj": proj, "ln4": ln4, "gate": gate})

        def turn(pe, tok, banks, done):
            for c in range(KH):
                for t in range(TILES):
                    mm = pe.transpose(banks[c][:, t * P:(t + 1) * P], tok[:, t, c * P:(c + 1) * P], ident[:, :])
                mm.then_inc(done.sem, 1)

        @block.tensor
        def _(pe):
            pe.wait_ge(wp_in.sem, 16)
            pe.wait_ge(const_in.sem, 16 * len(small))

            def patch(pe, g, b):
                wait(pe, joined(g - 1, 0))
                wait(pe, dt_in(g, 0))
                wait(pe, x_in[b](g, 16))
                for t in range(2 * b, 2 * b + 2):
                    for k in range(KP):
                        mm = pe.matmul(bank_a[b][:, (t % 2) * HID:(t % 2 + 1) * HID], patches[:, b, k, (t % 2) * P:(t % 2 + 1) * P],
                                       wp[:, k, :], start=(k == 0), stop=(k == KP - 1))
                mm.then_inc(patch_mm.sem, 1)

            def turn1(pe, g):
                wait(pe, u_tok(g, 4))
                turn(pe, tok_a, bank_a, u_turned)

            def dt_products(pe, g):
                pe.wait_ge(w_lo_done.sem, 1)
                wait(pe, u_split(g, 2))
                for m in range(KH):
                    for c in range(KH):
                        mm = product(pe, bank_a[m][:, :], [w[:, c, m * P:(m + 1) * P] for w in w_dt],
                                     (u_hi[:, c, :], u_lo[:, c, :]), c == 0, c == KH - 1)
                    mm.then_inc(dt_mm.sem, 1)

            def relative(pe, g):
                if g == 0:
                    pe.wait_ge(small_split.sem, 3)
                    pe.wait_ge(setup_v.sem, 3)
                    for k in range(SEQ):
                        for x in range(2):
                            mm = pe.matmul(bank_b[0][x * SEQ:(x + 1) * SEQ, k * HP:(k + 1) * HP],
                                           base[:, SEQ - 1 - k:2 * SEQ - 1 - k], rel[:, x:HEADS:2], start=True, stop=True)
                    mm.then_inc(bias_mm.sem, 1)

            def join(pe, g):
                wait(pe, y_sum(g, 2 + STEPS))
                if g + 1 < GROUPS:
                    wait(pe, dt_in(g + 1, 2))
                wait(pe, h_attn(g, 0))
                for b in range(2):
                    for t in range(2 * b, 2 * b + 2):
                        for c in range(KH):
                            at = (t % 2) * HID + c * P
                            mm = pe.transpose(bank_a[b][:, at:at + P], y_t[:, c, t * P:(t + 1) * P], ident[:, :])
                    mm.then_inc(y_turned.sem, 1)

            def turn2(pe, g):
                wait(pe, z_tok(g, 4))
                wait(pe, gate_exp(g, 0))
                pe.wait_ge(bias_out.sem, 1)
                turn(pe, tok_b, bank_b[0:2], z2_turned)

            def pick_one(pe, g):
                wait(pe, pick_v(g, 3))
                wait(pe, z4_out(g, 0))
                for c in range(KH):
                    mm = pe.matmul(bank_b[2][0:GS, 0:E0], zbn[:, c, :], wr[:, c, :], start=(c == 0), stop=(c == KH - 1))
                mm.then_inc(pick_mm.sem, 1)

            def down(pe, g):
                def units(e):
                    for c in range(KH):
                        product(pe, bank_b[e][:, :], [w[:, c, e * P:(e + 1) * P] for w in w_down],
                                (z_hi[:, c, :], z_lo[:, c, :]), c == 0, False)

                def penalise(e):
                    pe.matmul(bank_b[e][:, :], pen[:, 2 * e:2 * e + 2, :].rearrange("b e j -> b (e j)"), member_r[:, :],
                              start=False, stop=True).then_inc(down_mm.sem, 1)

                pe.wait_ge(w_lo_done.sem, len(staged))
                wait(pe, z2_split(g, 2))
                units(0)
                units(1)
                wait(pe, pick_v(g, 14))
                for t in range(TILES):
                    mm = pe.matmul(bank_b[2][:, t:t + 1], member_r[:, t * P:(t + 1) * P].bitcast(F32), pick[:, 4, 0:1], start=True, stop=True)
                mm.then_inc(pick_mm.sem, 1)
                pe.matmul(bank_b[3][0:E0, :], oneh_r[:, :], member_r[:, :], start=True, stop=True).then_inc(pick_mm.sem, 1)
                penalise(0)
                penalise(1)
                wait(pe, pick_v(g, 16))
                for e in (2, 3):
                    units(e)
                    penalise(e)

            def up(pe, g):
                def out(t):
                    return bank_b[t // 2][:, (t % 2) * HID:(t % 2 + 1) * HID]

                for e in range(4):
                    for t in range(TILES):
                        wait(pe, hid_split(g, max(e, t // 2) + 1))
                        product(pe, out(t), (mid_hi[:, e, t * P:(t + 1) * P], mid_lo[:, e, t * P:(t + 1) * P]),
                                [w[:, e, :] for w in w_up], e == 0 and t % 2 == 0, False, skip_group_check=True)
                for t in range(TILES):
                    for s in range(2):
                        mm = pe.matmul(out(t), oneh_t[:, t * P:(t + 1) * P], b_up[s][:, :], start=False, stop=(s == 1), skip_group_check=True)
                    if t % 2:
                        mm.then_inc(up_mm.sem, 1)

            def turn3(pe, g):
                wait(pe, z_tok(g, 8))
                turn(pe, tok_b, bank_b[2:4], z3_turned)

            def feature_major(pe, g, first):
                wait(pe, z3_split(g, 2))
                for m in range(first, first + 4):
                    wait(pe, h_ffn(g, 4) if m < 4 else q_out(g, m - 3))
                    for c in range(KH):
                        mm = product(pe, bank_b[m % 4][:, :], [w[:, c, m * P:(m + 1) * P] for w in w_qkv],
                                     (z_hi[:, c, :], z_lo[:, c, :]), c == 0, c == KH - 1)
                    mm.then_inc(qkv_mm.sem, 1)

            def values(pe, g):
                for t in range(TILES):
                    wait(pe, k_out(g, t + 1))
                    for c in range(KH):
                        mm = product(pe, bank_b[t][:, :], (z_hi[:, c, t * P:(t + 1) * P], z_lo[:, c, t * P:(t + 1) * P]),
                                     [w[:, c, 2 * INNER:3 * INNER] for w in w_qkv], c == 0, c == KH - 1)
                    mm.then_inc(qkv_mm.sem, 1)

            def scores(pe, g, t):
                if t == 0:
                    wait(pe, q_out(g, 4))
                    wait(pe, k_out(g, 4))
                if t < 2:
                    wait(pe, dt_in(min(g + 3, GROUPS), 0))
                    wait(pe, joined(g, 2))
                else:
                    wait(pe, s_bias(g, t - 1))
                for j in range(HP):
                    for y in range(2):
                        for x in range(2):
                            rows, tok = slice(x * DH, (x + 1) * DH), slice(t * P + y * SEQ, t * P + (y + 1) * SEQ)
                            mm = pe.matmul(bank_a[t % 2][x * SEQ:(x + 1) * SEQ, (2 * j + y) * SEQ:(2 * j + y + 1) * SEQ],
                                           qkv[rows, j, tok], qkv[rows, 4 + j, tok], start=True, stop=True)
                mm.then_inc(s_mm.sem, 1)

            def heads(pe, g, t):
                wait(pe, s_norm(g, t + 1))
                wait(pe, v_out(g, 2) if t < 2 else pt_out(g, t - 1))
                for j in range(HP):
                    mm = pe.transpose(bank_b[t % 2][:, j * P:(j + 1) * P], score[:, t % 2, j * P:(j + 1) * P], ident[:, :])
                mm.then_inc(pt_mm.sem, 1)

            def outputs(pe, g, t):
                wait(pe, pt_out(g, t + 1))
                if t == 0:
                    wait(pe, v_out(g, 4))
                if t >= 2:
                    wait(pe, o_split(g, t - 1))
                for y in range(2):
                    for j in range(HP):
                        for x in range(2):
                            rows = slice(y * SEQ, (y + 1) * SEQ)
                            if y == 1 and j == 0 and x == 0:
                                wait(pe, o_half(g, t + 1))
                            mm = pe.matmul(bank_b[2 + t % 2][x * DH:(x + 1) * DH, (y * HP + j) * SEQ:(y * HP + j + 1) * SEQ],
                                           qkv[rows, 8 + t, (2 * j + x) * DH:(2 * j + x + 1) * DH],
                                           probs_t[rows, t % 2, (2 * j + x) * SEQ:(2 * j + x + 1) * SEQ],
                                           start=True, stop=True)
                    mm.then_inc((o_half, o_mm)[y].sem, 1)

            def proj(pe, g, b):
                wait(pe, s_bias(g, 3 + b))
                for t in range(2 * b, 2 * b + 2):
                    wait(pe, o_split(g, t + 1))
                    for j in range(HP):
                        mm = product(pe, bank_a[b][:, (t % 2) * HID:(t % 2 + 1) * HID],
                                     (mid_hi[:, j, t * P:(t + 1) * P], mid_lo[:, j, t * P:(t + 1) * P]),
                                     [w[:, j, :] for w in w_o], j == 0, j == HP - 1)
                    if t % 2:
                        mm.then_inc(proj_mm.sem, 1)

            def gate(pe, g):
                wait(pe, z_tok(g, 12))
                turn(pe, tok_b, bank_b[2:4], z4_turned)
                wait(pe, z4_out(g, 2))
                for t in range(TILES):
                    for c in range(KH):
                        mm = pe.matmul(bank_b[0][:, t * E1:(t + 1) * E1], qkv[:, 10 + c, t * P:(t + 1) * P], gate_w[:, c, :],
                                       start=(c == 0), stop=(c == KH - 1))
                mm.then_inc(gate_mm.sem, 1)

            run("tensor", pe, {"relative": relative, "patch": patch, "turn1": turn1, "dt": dt_products, "join": join, "turn2": turn2,
                     "pick": pick_one, "down": down, "up": up, "turn3": turn3, "q": lambda p, g: feature_major(p, g, 0),
                     "k": lambda p, g: feature_major(p, g, 4), "v": values, "scores": scores, "heads": heads,
                     "outputs": outputs, "proj": proj, "gate": gate})


def phase_two(nc, sems, d, route, out):
    with ExitStack() as ctx:
        def sb(name, shape, dt=F32):
            return ctx.enter_context(nc.sbuf_tensor(name, shape, dt))

        def signal(name, per=1):
            return Signal(sems.enter_context(nc.semaphore(name)), per)

        NE = E1 + 1
        RAW = 4
        LAG = 2
        w_raw = sb("w_raw", [P, RAW, EXPERT])
        w_hi = sb("w_hi", [P, NE, EXPERT], F32R)
        w_lo = sb("w_lo", [P, NE, EXPERT], F32R)
        z = sb("z", [P, KH, GT])
        z_hi = sb("z2_hi", [P, KH, GT], F32R)
        z_lo = sb("z2_lo", [P, KH, GT], F32R)
        res = sb("res", [P, TILES, HID])
        silu = sb("silu", [P, 2, GT])
        act_t = sb("act_t", [P, 2, GT])
        a_hi = sb("a_hi", [P, 2, GT], F32R)
        a_lo = sb("a_lo", [P, 2, GT], F32R)
        rest = sb("rest", [P, TILES, E1])
        parts = sb("parts", [P, TILES, 3, E1], BF16)
        parts_t = sb("parts_t", [3 * E1, GT], BF16)
        select = sb("select", [3 * E1, E1, P], BF16)
        ident = sb("ident_b", [P, P], BF16)

        bank_s = [ctx.enter_context(nc.psum_tensor(f"bank_s{i}", [P, GT], F32)) for i in range(2)]
        bank_g = [ctx.enter_context(nc.psum_tensor(f"bank_g{i}", [P, GT], F32)) for i in range(2)]
        bank_u = [ctx.enter_context(nc.psum_tensor(f"bank_u{i}", [P, GT], F32)) for i in range(2)]
        bank_r = [ctx.enter_context(nc.psum_tensor(f"bank_r{i}", [P, GT], F32)) for i in range(2)]
        turned = bank_r[1][0:3 * E1, 0:GT // 2].bitcast(BF16)

        cst_in, w_in2 = signal("cst_in"), [signal(f"w_in2_{i}") for i in range(RAW)]
        w_split, w_split_hi = signal("w_split"), signal("w_split_hi")
        z_in, zt_hi, zt_split, res_in = signal("z_in", 16), signal("zt_hi", 1), signal("zt_split", 1), signal("res_in", 16)
        parts_done, parts_turned, parts_out = signal("parts_done", 5), signal("parts_turned", 1), signal("parts_out", 1)
        gu_mm, r_mm, silu_done = signal("gu_mm", NE), signal("r_mm", E1), signal("silu_done", NE)
        act_v = signal("act_v", NE + E1)
        a_hi_done, a_split, down_mm2 = signal("a_hi_done", NE), signal("a_split", NE), signal("down_mm2", NE)
        added, stored = signal("added", 2), signal("stored", 16)

        block = ctx.enter_context(nc.Block())

        @block.sync
        def _(sp):
            sp.dma_start(select[:, :, :], d["select"]).then_inc(cst_in.sem, 16)
            sp.dma_start(ident[:, :], d["ident_b"]).then_inc(cst_in.sem, 16)

            def load(g):
                wait(sp, zt_split(g, 0))
                sp.dma_start(z[:, :, :], d["z_mid"][g]).then_inc(z_in.sem, 16)

            load(0)
            for e in range(NE):
                if e >= RAW:
                    sp.wait_ge(w_split.sem, e - RAW + 1)
                sp.dma_start(w_raw[:, e % RAW, :], d["experts"][e]).then_inc(w_in2[e % RAW].sem, 16)

            def body(g, more):
                wait(sp, stored(g, 0))
                sp.dma_start(res[:, :, :], d["h_mid"][g]).then_inc(res_in.sem, 16)
                if more:
                    load(g + 1)
                wait(sp, added(g, 2))
                sp.dma_start(out[g], res[:, :, :]).then_inc(stored.sem, 16)

            body(0, True)
            with sp.Fori(1, GROUPS - 1) as g:
                body(g, True)
            body(GROUPS - 1, False)
            wait(sp, stored(GROUPS, 0))

        @block.gpsimd
        def _(pool):
            for e in range(NE):
                pool.wait_ge(w_in2[e % RAW].sem, 16 * (e // RAW + 1))
                pool.tensor_copy(w_hi[:, e, :], w_raw[:, e % RAW, :]).then_inc(w_split_hi.sem, 1)
                pool.wait_ge(w_split_hi.sem, e + 1)
                pool.tensor_tensor(w_lo[:, e, :], w_raw[:, e % RAW, :], w_hi[:, e, :].bitcast(F32),
                                   ALU.subtract).then_inc(w_split.sem, 1)

        @block.scalar
        def _(act):
            def body(g):
                wait(act, z_in(g, 16))
                wait(act, gu_mm(g, 0))
                act.activation(z_hi[:, :, :], z[:, :, :], ACT.Copy).then_inc(zt_hi.sem, 1)
                for e in range(NE):
                    wait(act, gu_mm(g, e + 1))
                    wait(act, act_v(g, 2 * e - 3) if e >= 2 else act_v(g, 0))
                    act.activation(silu[:, e % 2, :], bank_g[e % 2][:, :], ACT.Silu).then_inc(silu_done.sem, 1)
                    wait(act, act_v(g, min(2 * e + 2, NE + E1)))
                    wait(act, down_mm2(g, e - 1) if e >= 2 else down_mm2(g, 0))
                    act.activation(a_hi[:, e % 2, :], act_t[:, e % 2, :], ACT.Copy).then_inc(a_hi_done.sem, 1)

            body(0)
            with act.Fori(1, GROUPS) as g:
                body(g)

        @block.vector
        def _(dve):
            dve.wait_ge(cst_in.sem, 32)

            def body(g):
                mine = route[:, bass.ds(g * TILES, TILES), :]
                dve.tensor_copy(parts[:, :, 0, :], mine).then_inc(parts_done.sem, 1)
                wait(dve, parts_done(g, 1))
                dve.tensor_tensor(rest[:, :, :], mine, parts[:, :, 0, :], ALU.subtract).then_inc(parts_done.sem, 1)
                wait(dve, parts_done(g, 2))
                dve.tensor_copy(parts[:, :, 1, :], rest[:, :, :]).then_inc(parts_done.sem, 1)
                wait(dve, parts_done(g, 3))
                dve.tensor_tensor(rest[:, :, :], rest[:, :, :], parts[:, :, 1, :], ALU.subtract).then_inc(parts_done.sem, 1)
                wait(dve, parts_done(g, 4))
                dve.tensor_copy(parts[:, :, 2, :], rest[:, :, :]).then_inc(parts_done.sem, 1)
                wait(dve, zt_hi(g, 1))
                dve.tensor_tensor(z_lo[:, :, :], z[:, :, :], z_hi[:, :, :].bitcast(F32), ALU.subtract).then_inc(zt_split.sem, 1)
                wait(dve, parts_turned(g, 1))
                dve.tensor_copy(parts_t[:, :], turned).then_inc(parts_out.sem, 1)
                for e in range(NE):
                    wait(dve, silu_done(g, e + 1))
                    wait(dve, a_split(g, e - 1) if e >= 2 else a_split(g, 0))
                    dve.tensor_tensor(act_t[:, e % 2, :], silu[:, e % 2, :], bank_u[e % 2][:, :], ALU.mult).then_inc(act_v.sem, 1)
                    if e < E1:
                        wait(dve, act_v(g, 2 * e + 1))
                        wait(dve, r_mm(g, e + 1))
                        dve.tensor_tensor(act_t[:, e % 2, :], act_t[:, e % 2, :], bank_r[e % 2][:, :], ALU.mult).then_inc(act_v.sem, 1)
                    wait(dve, a_hi_done(g, e + 1))
                    dve.tensor_tensor(a_lo[:, e % 2, :], act_t[:, e % 2, :], a_hi[:, e % 2, :].bitcast(F32), ALU.subtract).then_inc(a_split.sem, 1)
                wait(dve, res_in(g, 16))
                wait(dve, down_mm2(g, NE))
                for b in range(2):
                    dve.tensor_tensor(res[:, 2 * b:2 * b + 2, :], bank_s[b][:, :].rearrange("p (t n) -> p t n", t=2),
                                      res[:, 2 * b:2 * b + 2, :], ALU.add).then_inc(added.sem, 1)

            body(0)
            with dve.Fori(1, GROUPS) as g:
                body(g)

        @block.tensor
        def _(pe):
            pe.wait_ge(cst_in.sem, 32)

            def body(g):
                wait(pe, parts_done(g, 5))
                wait_before_tiles(pe, act_v(g, 0), bank_r[1], ident[:, 0:DH])
                for t in range(TILES):
                    mm = pe.transpose(turned[:, t * P:(t + 1) * P], parts[:, t, :, :].rearrange("p a e -> p (a e)"), ident[:, :])
                mm.then_inc(parts_turned.sem, 1)
                wait(pe, zt_split(g, 1))
                for e in range(NE + LAG):
                    if e < NE:
                        pe.wait_ge(w_split.sem, e + 1)
                        if e >= 2:
                            wait(pe, silu_done(g, e - 1))
                            wait(pe, act_v(g, 2 * e - 2))
                        for bank, at in ((bank_g, 0), (bank_u, M1)):
                            for c in range(KH):
                                cut = slice(c * 2 * M1 + at, c * 2 * M1 + at + M1)
                                mm = product(pe, bank[e % 2][:, :], (w_hi[:, e, cut], w_lo[:, e, cut]),
                                             (z_hi[:, c, :], z_lo[:, c, :]), c == 0, c == KH - 1)
                        mm.then_inc(gu_mm.sem, 1)
                        if e < E1:
                            if e < 2:
                                wait(pe, parts_out(g, 1))
                            pe.matmul(bank_r[e % 2][:, :], select[:, e, :], parts_t[:, :], start=True, stop=True).then_inc(r_mm.sem, 1)
                    if e >= LAG:
                        n = e - LAG
                        wait(pe, a_split(g, n + 1))
                        if n == 0:
                            wait(pe, added(g, 0))
                        for t in range(TILES):
                            cut = slice(t * P, (t + 1) * P)
                            mm = product(pe, bank_s[t // 2][:, (t % 2) * HID:(t % 2 + 1) * HID],
                                         (a_hi[:, n % 2, cut], a_lo[:, n % 2, cut]),
                                         (w_hi[:, n, 4 * M1:], w_lo[:, n, 4 * M1:]),
                                         n == 0 and t % 2 == 0, n == NE - 1, skip_group_check=True)
                        mm.then_inc(down_mm2.sem, 1)

            body(0)
            with pe.Fori(1, GROUPS) as g:
                body(g)


def build(nc, d, out):
    with ExitStack() as ctx:
        route = ctx.enter_context(nc.sbuf_tensor("route", [P, GROUPS * TILES, E1], F32))
        phase_one(nc, ctx, d, route)
        phase_two(nc, ctx, d, route, out)


def kernel(**inputs):
    import ml_dtypes
    import numpy as np
    from concourse import bacc
    from concourse.bass_utils import run_bass_kernel_spmd

    a = {k: np.asarray(v) for k, v in inputs.items()}

    def rows(w, k):
        return w.reshape(k, P, -1).transpose(1, 0, 2)

    def column(v):
        return v.reshape(-1, P).T

    side, ps = 8, 16
    x = a["x"].reshape(GROUPS, GS, 3, side, ps, side, ps).transpose(0, 4, 6, 2, 1, 3, 5)
    x = x.reshape(GROUPS, KP, P, 2, GT // 2).transpose(0, 3, 2, 1, 4)

    quarter = HID // 4
    f = (10000.0 ** (np.arange(quarter, dtype=np.float32) / quarter)).astype(np.float32)
    rr, cc = [v.reshape(-1, 1).astype(np.float32) / f for v in np.meshgrid(np.arange(side), np.arange(side), indexing="ij")]
    pos = np.concatenate([np.sin(rr), np.cos(rr), np.sin(cc), np.cos(cc)], -1).astype(np.float32)
    dist = np.arange(2 * SEQ) - (SEQ - 1)
    large = 16 + (np.log(np.maximum(dist, 1).astype(np.float32) / 16) / np.log(128 / 16) * 16).astype(np.int32)
    bucket = np.where(dist < 0, 32, np.where(dist < 16, dist, np.minimum(large, 31)))
    base = (np.arange(33)[:, None] == bucket[None]).astype(np.float32)
    member = (np.arange(GS)[:, None] == np.arange(GT)[None] // SEQ).astype(np.float32)
    select = (np.arange(3 * E1)[:, None, None] % E1 == np.arange(E1)[None, :, None]) & np.ones((1, 1, P), bool)

    experts = [np.concatenate([
        np.concatenate([rows(g, KH), rows(u, KH)], 2).reshape(P, -1), w], 1)
        for g, u, w in zip([*a["L1_ffn_w_gate"], a["L1_ffn_ws_gate"]], [*a["L1_ffn_w_up"], a["L1_ffn_ws_up"]],
                           [*a["L1_ffn_w_down"], a["L1_ffn_ws_down"]])]
    wide = lambda v: np.broadcast_to(v, (P, v.shape[-1]))
    host = {
        "x": x, "wp": rows(a["L0_tok_Wp"].T, KP), "pos": np.tile(pos, (2, 1)), "tokb": wide(a["L0_tok_b"]),
        "bo": wide(a["L1_attn_bo"]), "iota": wide(np.arange(E1, dtype=np.float32)), "ident": np.eye(P, dtype=np.float32),
        "b_dt": column(a["L0_attn_b_dt"]), "skip_d": column(a["L0_attn_D_vec"]),
        "a_log": rows(a["L0_attn_A_log"], KH), "bmat": rows(a["L0_attn_B_mat"], KH), "cmat": rows(a["L0_attn_C_mat"], KH),
        "cols": np.stack([column(a["L0_ffn_" + n]) for n in ("ln_g", "ln_b", "bn_g", "bn_b", "bn_mean", "bn_var", "bn_var", "bn_var")], 1),
        "b_down": column(a["L0_ffn_b_down"].reshape(-1)), "wr": rows(a["L0_ffn_Wr"], KH),
        "br": np.broadcast_to(a["L0_ffn_br"], (E0, E0)), "gate_w": rows(a["L1_ffn_gate_w"].T, KH), "member": member,
        "rel": a["L1_attn_rel_emb"], "base": base, "b_up": a["L0_ffn_b_up"],
        "w_dt": rows(a["L0_attn_W_dt"].T, KH), "w_down": rows(a["L0_ffn_W_down"].transpose(1, 0, 2).reshape(HID, -1), KH),
        "w_up": rows(a["L0_ffn_W_up"].reshape(E0 * H0, HID), 4),
        "w_qkv": rows(np.concatenate([a["L1_attn_Wq"], a["L1_attn_Wkv"]], 1), KH), "w_o": rows(a["L1_attn_Wo"], HP),
        "experts": np.stack(experts), "select": select.astype(ml_dtypes.bfloat16),
        "ident_b": np.eye(P).astype(ml_dtypes.bfloat16),
    }
    nc = bacc.Bacc("TRN2", target_bir_lowering=False, num_devices=1)
    arrays, d = {}, {}
    for name, v in host.items():
        arrays["in_" + name] = np.ascontiguousarray(v)
        d[name] = nc.dram_tensor("in_" + name, v.shape, mybir.dt.from_np(v.dtype), kind="ExternalInput").ap()
    d["h_mid"] = nc.dram_tensor("h_mid", (GROUPS, P, TILES, HID), F32, kind="Internal").ap()
    d["z_mid"] = nc.dram_tensor("z_mid", (GROUPS, P, KH, GT), F32, kind="Internal").ap()
    out = nc.dram_tensor("out", (GROUPS, P, TILES, HID), F32, kind="ExternalOutput").ap()
    build(nc, d, out)
    got = run_bass_kernel_spmd(nc, [arrays], core_ids=[0]).results[0]["out"]
    return got.reshape(GROUPS, P, TILES, HID).transpose(0, 2, 1, 3).reshape(BATCH, SEQ, HID)
```

```python
from contextlib import ExitStack

import concourse.bass as bass
from concourse import mybir

ALU = mybir.AluOpType
ACT = mybir.ActivationFunctionType
F32 = mybir.dt.float32
F32R = mybir.dt.float32r
U32 = mybir.dt.uint32
AX_X = mybir.AxisListType.X

P = 128
BATCH, SEQ, HID = 32, 64, 256
PATCH = 768
NSTATE = 16
GROUPS = 4
GT = BATCH * SEQ // GROUPS
TILES = GT // P
GS = GT // SEQ
KH = HID // P
KP = PATCH // P
E0, H0 = 8, 64
HEADS, DH = 8, 64
INNER = HEADS * DH
HP = HEADS // 2
E1, M1 = 16, 128
TOPK_SCALE = 2.5
EPS = 1e-5
PENALTY = float(2.0**100)
MASKED = -1e37
STEPS = KH * NSTATE
EXPERT = KH * 2 * M1 + HID
ALL_TILES = GROUPS * TILES
SLOT_TILES = 2 * ALL_TILES + E1
ROW = HID + 16


class Signal:

    def __init__(self, sem, per):
        self.sem, self.per = sem, per

    def __call__(self, g, k):
        return self.sem, g * self.per + k


def wait(engine, at):
    if not (isinstance(at[1], int) and at[1] <= 0):
        engine.wait_ge(*at)


def wait_before_tiles(pe, at, bank, weights):
    wait(pe, at)
    pe.matmul(bank[0:weights.shape[1], 0:1], weights, weights[:, 0:1], start=True, stop=True)


def product(pe, out, lhs, rhs, start, stop, **kw):
    pe.matmul(out, lhs[0], rhs[0], start=start, stop=False, **kw)
    pe.matmul(out, lhs[1], rhs[0], start=False, stop=False, **kw)
    return pe.matmul(out, lhs[0], rhs[1], start=False, stop=stop, **kw)


BACK = [
    ("join", 0), ("gate", -1), ("ln2", 0), ("turn2", 0), ("pick", 0), ("down", 0), ("up", 0), ("ln3", 0), ("turn3", 0),
    ("q", 0), ("k", 0), ("v", 0), ("scores", 0, 0), ("scores", 0, 1), ("probs", 0, 0), ("heads", 0, 0), ("scores", 0, 2),
    ("probs", 0, 1), ("outputs", 0, 0), ("heads", 0, 1), ("scores", 0, 3), ("probs", 0, 2), ("outputs", 0, 1),
    ("heads", 0, 2), ("proj", 0, 0), ("probs", 0, 3), ("outputs", 0, 2), ("heads", 0, 3), ("outputs", 0, 3), ("proj", 0, 1),
    ("ln4", 0),
]
FRONT = [("patch", 2, 0), ("patch", 2, 1), ("ln1", 2), ("turn1", 2), ("dt", 2), ("soft", 2)]
STEP = [("relative", 1)] + [("step", 1, i) for i in range(STEPS)]
MERGED = {
    "sync": "ssbbbssbfssfbssbfsbsbfbfbssssssbsfbsbssbsbbbssbssbbbbbsbbbsbbsssbbssbs",
    "gpsimd": "sssbbssssssbbssbbbssssbbbbbbfbbbbfbbbbbbbsssbsssssfssfsssfsssssbbbbbbf",
    "scalar": "ssbsbsbsbsffbssbsbfsbfbsssssbsssfbsfssbbssbsssbbsbbbbbbbsbbsbbsbssbbsb",
    "vector": "ssbbbssfsbsbbsfsfbbsbsbssfsssssbfsbsfssbbbssssbbbsbbbbssbbsbbbbsssbsbb",
    "tensor": "ssssbbbsfbfsfbbsbsbfbssbfbbsbsssssssssssssssssbbbssbbbbbbbbsbbsbsbbbbf",
}


def phase_one(nc, sems, d, chosen, weight):
    with ExitStack() as ctx:
        def sb(name, shape, dt=F32):
            return ctx.enter_context(nc.sbuf_tensor(name, shape, dt))

        def signal(name, per=1):
            return Signal(sems.enter_context(nc.semaphore(name)), per)

        ident = sb("ident", [P, P])
        posb = sb("posb", [P, HID])
        bo = sb("bo", [P, HID])
        iota = sb("iota", [P, E1])
        eps = sb("eps", [P, 1])
        one = sb("one", [P, 1])
        b_dt = sb("b_dt", [P, KH])
        skip_d = sb("skip_d", [P, KH])
        decay = sb("decay", [P, KH, NSTATE])
        bmat = sb("bmat", [P, KH, NSTATE])
        cmat = sb("cmat", [P, KH, NSTATE])
        cols = sb("cols", [P, 8, KH])
        bn_a = sb("bn_a", [P, KH])
        bn_c = sb("bn_c", [P, KH])
        b_down = sb("b_down", [P, E0 // 2])
        wr = sb("wr", [P, KH, E0])
        br = sb("br", [E0, E0])
        gate_w = sb("gate_w", [P, KH, E1])
        member_r = sb("member_r", [GS, GT], F32R)
        rel = sb("rel", [33, HEADS])
        base = sb("base", [33, 2 * SEQ])
        rel_bias = sb("rel_bias", [P, HP, SEQ])

        wp = sb("wp", [P, KP, HID])
        w_dt = [sb(f"w_dt{s}", [P, KH, HID], F32R) for s in "hl"]
        w_down = [sb(f"w_down{s}", [P, KH, E0 * H0], F32R) for s in "hl"]
        w_up = [sb(f"w_up{s}", [P, E0 * H0 // P, HID], F32R) for s in "hl"]
        w_qkv = [sb(f"w_qkv{s}", [P, KH, 3 * INNER], F32R) for s in "hl"]
        w_o = [sb(f"w_o{s}", [P, HP, HID], F32R) for s in "hl"]
        b_up = [sb(f"b_up{s}", [E0, HID], F32R) for s in "hl"]

        patches = sb("patches", [P, 2, KP, GT // 2])
        h0 = [sb(f"h0_{i}", [P, TILES, HID]) for i in range(2)]
        tok_a = sb("tok_a", [P, TILES, HID])
        u_hi = sb("u_hi", [P, KH, GT], F32R)
        u_lo = sb("u_lo", [P, KH, GT], F32R)
        u_t = sb("u_t", [P, KH, GT])
        dt = [sb(f"dt_{i}", [P, KH, GT]) for i in range(2)]
        drive = [sb(f"drive_{i}", [P, KH, GT]) for i in range(2)]
        y_t = sb("y_t", [P, KH, GT])
        state = sb("state", [P, 2, GT])
        feed = sb("feed", [P, 2, GT])
        stats_a = sb("stats_a", [P, TILES, 6])
        mv_a = sb("mv_a", [P, TILES, 2])
        ln_a = sb("ln_a", [P, TILES, 2])

        h = sb("h", [P, TILES, HID])
        tok_b = sb("tok_b", [P, TILES, HID])
        z_hi = sb("z_hi", [P, KH, GT], F32R)
        z_lo = sb("z_lo", [P, KH, GT], F32R)
        z_t = sb("z_t", [P, KH, GT])
        mid_hi = sb("mid_hi", [P, 4, GT], F32R)
        mid_lo = sb("mid_lo", [P, 4, GT], F32R)
        qkv = sb("qkv", [P, 12, GT])
        score = sb("score", [P, 2, GT])
        probs_t = sb("probs_t", [P, 2, GT])
        stats_b = sb("stats_b", [P, TILES, 6])
        mv_b = sb("mv_b", [P, TILES, 2])
        ln_b = sb("ln_b", [P, TILES, 6])
        zsum = sb("zsum", [P, KH, GS])
        zbn = sb("zbn", [P, KH, GS])
        pick = sb("pick", [E0, 8, E0])
        pick_i = sb("pick_i", [E0, E0], U32)
        pen = sb("pen", [E0, E0, H0], F32R)
        oneh_r = sb("oneh_r", [E0, E0], F32R)
        oneh_t = sb("oneh_t", [E0, GT], F32R)
        gtok = sb("gtok", [P, TILES])
        srow = sb("srow", [P, 2, 3, 8])
        rsc = sb("rsc", [P, TILES, E1])
        rtop = sb("rtop", [P, TILES, 8])
        ridx = sb("ridx", [P, TILES, 8], U32)
        ridf = sb("ridf", [P, TILES, 8])
        rw = sb("rw", [P, TILES, 2])
        blank = sb("blank", [P, HID])

        bank_x = [ctx.enter_context(nc.psum_tensor(f"bank_x{i}", [P, GT], F32)) for i in range(2)]
        bank_a = [ctx.enter_context(nc.psum_tensor(f"bank_a{i}", [P, GT], F32)) for i in range(2)]
        bank_b = [ctx.enter_context(nc.psum_tensor(f"bank_b{i}", [P, GT], F32)) for i in range(4)]

        blank_in, zeroed = signal("blank_in"), signal("zeroed")
        const_in, wp_in, w_dt_in, w_in = signal("const_in"), signal("wp_in"), signal("w_dt_in"), signal("w_in")
        setup_v, setup_a, setup_p = signal("setup_v"), signal("setup_a"), signal("setup_p")
        w_hi_done, w_lo_done, small_split = signal("w_hi_done"), signal("w_lo_done"), signal("small_split")
        bias_mm, bias_out = signal("bias_mm"), signal("bias_out")
        x_in = [signal(f"x_in{i}", 16) for i in range(2)]
        patch_mm, patch_add = signal("patch_mm", 2), signal("patch_add", 2)
        stat_a, mean_a, rstd_a = signal("stat_a", 4), signal("mean_a", 4), signal("rstd_a", 2)
        u_tok, u_turned, u_copied = signal("u_tok", 4), signal("u_turned", 2), signal("u_copied", 4)
        u_split, dt_mm, dt_in = signal("u_split", 2), signal("dt_mm", 2), signal("dt_in", 2)
        sp_v, sp_a = signal("sp_v", 6), signal("sp_a", 2)
        decay_in, feed_in, scanned, y_sum = signal("decay_in", STEPS), signal("feed_in", STEPS), signal("scanned", STEPS), signal("y_sum", 2 + STEPS)
        y_turned, joined = signal("y_turned", 2), signal("joined", 2)
        stat_b, mean_b = signal("stat_b", 12), signal("mean_b", 12)
        ln2_a, ln2_v = signal("ln2_a", 4), signal("ln2_v", 2)
        rstd_b = signal("rstd_b", 4)
        z_tok, z2_turned, z2_copied, z2_split = signal("z_tok", 12), signal("z2_turned", 2), signal("z2_copied", 4), signal("z2_split", 2)
        pick_v, pick_mm, pick_exp = signal("pick_v", 16), signal("pick_mm", 3), signal("pick_exp", 1)
        down_mm, hid_copied, hid_split = signal("down_mm", 4), signal("hid_copied", 8), signal("hid_split", 4)
        up_mm, h_ffn = signal("up_mm", 2), signal("h_ffn", 4)
        z3_turned, z3_hi, z3_split = signal("z3_turned", 2), signal("z3_hi", 2), signal("z3_split", 2)
        qkv_mm, q_out, k_out, v_out = signal("qkv_mm", 12), signal("q_out", 4), signal("k_out", 4), signal("v_out", 4)
        bo_added = signal("bo_added", 1)
        s_mm, s_bias, s_max, s_sub = signal("s_mm", 4), signal("s_bias", 4), signal("s_max", 4), signal("s_sub", 4)
        s_exp, s_sum, s_rcp, s_norm = signal("s_exp", 4), signal("s_sum", 4), signal("s_rcp", 4), signal("s_norm", 4)
        pt_mm, pt_out, o_half, o_mm = signal("pt_mm", 4), signal("pt_out", 4), signal("o_half", 4), signal("o_mm", 4)
        o_hi, o_split, proj_mm, h_attn = signal("o_hi", 4), signal("o_split", 4), signal("proj_mm", 2), signal("h_attn", 2)
        h_stored, z_stored = signal("h_stored", 16), signal("z_stored", 16)
        z4_turned, z4_out = signal("z4_turned", 2), signal("z4_out", 2)
        gate_mm, gate_exp, gate_v = signal("gate_mm", 1), signal("gate_exp", 1), signal("gate_v", 14 + 2 * TILES)

        block = ctx.enter_context(nc.Block())

        raw = qkv[:, :, :].rearrange("p a b -> p (a b)")
        raw_b = tok_b[:, :, :].rearrange("p a b -> p (a b)")
        at, staged = 0, []
        for name, pair in (("w_down", w_down), ("w_up", w_up), ("w_qkv", w_qkv), ("w_o", w_o)):
            n = pair[0].shape[1] * pair[0].shape[2]
            staged.append((name, pair, raw[:, at:at + n]))
            at += n
        staged.insert(0, ("w_dt", w_dt, raw_b[:, 0:KH * HID]))
        tokb = raw_b[:, 768:1024]
        raw_member = score[0:GS, 0, :]
        small = [("pos", posb[:, :]), ("tokb", tokb), ("bo", bo[:, :]), ("iota", iota[:, :]),
                 ("ident", ident[:, :]), ("b_dt", b_dt[:, :]), ("skip_d", skip_d[:, :]),
                 ("a_log", decay[:, :, :]), ("bmat", bmat[:, :, :]), ("cmat", cmat[:, :, :]),
                 ("cols", cols[:, :, :]), ("b_down", b_down[:, :]), ("wr", wr[:, :, :]), ("br", br[:, :]),
                 ("gate_w", gate_w[:, :, :]), ("member", raw_member), ("rel", rel[0:32, :]),
                 ("base", base[:, :]), ("b_up", raw_b[0:E0, 512:768])]

        def run(who, engine, own):
            for n in range(-2, GROUPS + 1):
                chains = {"b": iter(BACK), "f": iter(FRONT), "s": iter(STEP)}
                for chain in MERGED[who]:
                    piece, ahead, *args = next(chains[chain])
                    if piece in own and 0 <= n + ahead < GROUPS:
                        own[piece](engine, n + ahead, *args)

        def by_sample(tiles, t):
            return tiles[:, :, t * P:(t + 1) * P].rearrange("p j (y q) -> p j y q", q=SEQ)

        def heads_out(t):
            return bank_b[2 + t % 2][:, :].rearrange("p (y j q) -> p j y q", j=HP, q=SEQ)

        def load_patches(sp, g, b):
            wait(sp, patch_mm(g - 1, b + 1))
            sp.dma_start(patches[:, b, :, :], d["x"][g, b]).then_inc(x_in[b].sem, 16)

        def store_h(sp, g, b):
            if b == 1:
                wait(sp, h_attn(g, 2))
                sp.dma_start(d["h_mid"][g], h[:, :, :]).then_inc(h_stored.sem, 16)

        def store_z(sp, g):
            wait(sp, z_tok(g, 12))
            sp.dma_start(d["z_mid"][g], tok_b[:, :, :]).then_inc(z_stored.sem, 16)

        @block.sync
        def _(sp):
            sp.dma_start(wp[:, :, :], d["wp"]).then_inc(wp_in.sem, 16)
            load_patches(sp, 0, 0)
            load_patches(sp, 0, 1)
            for name, to in small:
                sp.dma_start(to, d[name]).then_inc(const_in.sem, 16)
            for name, _, to in staged:
                sp.dma_start(to, d[name].rearrange("p a b -> p (a b)")).then_inc((w_dt_in if name == "w_dt" else w_in).sem, 16)

            sp.dma_start(blank[:, :], d["blank"]).then_inc(blank_in.sem, 16)
            sp.wait_ge(blank_in.sem, 16)
            sp.dma_start(d["z_slots"].rearrange("(j p) n -> p j n", p=P)[:, :, 0:HID],
                         blank[:, None, :].broadcast_to([P, SLOT_TILES, HID])).then_inc(zeroed.sem, 16)
            sp.dma_start(d["z_slots"][:, HID:], d["nobody"]).then_inc(zeroed.sem, 16)

            def next_patches(sp, g, b):
                if g + 1 < GROUPS:
                    load_patches(sp, g + 1, b)

            run("sync", sp, {"patch": next_patches, "proj": store_h, "ln4": store_z})
            sp.wait_ge(zeroed.sem, 32)
            wait(sp, h_stored(GROUPS, 0))
            wait(sp, z_stored(GROUPS, 0))

        @block.gpsimd
        def _(pool):
            pool.wait_ge(const_in.sem, 16 * len(small))
            pool.tensor_tensor(posb[:, :], posb[:, :], tokb, ALU.add).then_inc(setup_p.sem, 1)
            pool.tensor_tensor(cmat[:, :, :], cmat[:, :, :], bmat[:, :, :], ALU.mult).then_inc(setup_p.sem, 1)

            def step(pool, g, i):
                if i == 0:
                    wait(pool, u_copied(g, 4))
                    wait(pool, y_turned(g, 0))
                    for c in range(KH):
                        pool.tensor_scalar(y_t[:, c, :], u_t[:, c, :], skip_d[:, c:c + 1], None, ALU.mult).then_inc(y_sum.sem, 1)
                c = i // NSTATE
                wait(pool, scanned(g, i + 1))
                wait(pool, y_sum(g, 2 + i))
                pool.tensor_tensor(y_t[:, c, :], state[:, i % 2, :], y_t[:, c, :], ALU.add).then_inc(y_sum.sem, 1)

            def add_output_bias(pool, g):
                wait(pool, z_tok(g, 8))
                pool.tensor_tensor(h[:, :, :], h[:, :, :], bo[:, None, :].broadcast_to([P, TILES, HID]),
                                   ALU.add).then_inc(bo_added.sem, 1)

            run("gpsimd", pool, {"step": step, "ln3": add_output_bias})

        def rstd(act, g, k):
            wait(act, mean_b(g, 4 * (k + 1)))
            act.activation(ln_b[:, :, 0], mv_b[:, :, 1], ACT.Ln, bias=eps[:, 0:1]).then_inc(rstd_b.sem, 1)
            wait(act, rstd_b(g, 2 * k - 1))
            act.activation(ln_b[:, :, 5], ln_b[:, :, 0], ACT.Exp, scale=-0.5).then_inc(rstd_b.sem, 1)

        @block.scalar
        def _(act):
            act.preload_act_table_set("natural_log_exp_and_others")
            act.wait_ge(setup_v.sem, 5)
            act.wait_ge(const_in.sem, 16 * len(small))
            act.activation(decay[:, :, :], decay[:, :, :], ACT.Exp).then_inc(setup_a.sem, 1)
            act.activation(bn_a[:, :], cols[:, 5, :], ACT.Ln, bias=eps[:, 0:1]).then_inc(setup_a.sem, 1)
            act.wait_ge(setup_a.sem, 2)
            act.activation(bn_a[:, :], bn_a[:, :], ACT.Exp, scale=-0.5).then_inc(setup_a.sem, 1)

            def ln1(act, g):
                wait(act, mean_a(g, 4))
                act.activation(ln_a[:, :, 0], mv_a[:, :, 1], ACT.Ln, bias=eps[:, 0:1]).then_inc(rstd_a.sem, 1)
                wait(act, rstd_a(g, 1))
                act.activation(ln_a[:, :, 1], ln_a[:, :, 0], ACT.Exp, scale=-0.5).then_inc(rstd_a.sem, 1)

            def turn1(act, g):
                for c in range(KH):
                    wait(act, u_turned(g, c + 1))
                    act.activation(u_hi[:, c, :], bank_a[c][:, :], ACT.Copy).then_inc(u_copied.sem, 1)
                    if c == 0:
                        wait(act, y_sum(g - 1, 2))
                        wait(act, sp_v(g, 0))
                    act.activation(u_t[:, c, :], bank_a[c][:, :], ACT.Copy).then_inc(u_copied.sem, 1)

            def dt_bias(act, g):
                wait(act, scanned(g - 1, 0))
                for c in range(KH):
                    wait(act, dt_mm(g, c + 1))
                    act.activation(dt[g % 2][:, c, :], bank_a[c][:, :], ACT.Identity, bias=b_dt[:, c:c + 1]).then_inc(dt_in.sem, 1)

            def soft(act, g):
                wait(act, sp_v(g, 1))
                act.activation(drive[g % 2][:, :, :], drive[g % 2][:, :, :], ACT.Exp).then_inc(sp_a.sem, 1)
                wait(act, sp_v(g, 3))
                act.activation(drive[g % 2][:, :, :], drive[g % 2][:, :, :], ACT.Ln, bias=one[:, 0:1]).then_inc(sp_a.sem, 1)

            def step(act, g, i):
                if i == 0:
                    wait(act, sp_v(g, 6))
                    act.wait_ge(setup_v.sem, 6)
                c, n = divmod(i, NSTATE)
                wait(act, scanned(g, i - 1))
                act.activation(bank_x[i % 2][:, :].rearrange("p (b t) -> p b t", t=SEQ)[:, :, 1:SEQ],
                               dt[g % 2][:, c, :].rearrange("p (b t) -> p b t", t=SEQ)[:, :, 1:SEQ],
                               ACT.Exp, scale=decay[:, c, n:n + 1]).then_inc(decay_in.sem, 1)
                act.activation(feed[:, i % 2, :], drive[g % 2][:, c, :], ACT.Copy, scale=cmat[:, c, n:n + 1]).then_inc(feed_in.sem, 1)

            def ln2(act, g):
                wait(act, mean_b(g, 4))
                act.activation(ln_b[:, :, 0], mv_b[:, :, 1], ACT.Ln, bias=eps[:, 0:1]).then_inc(ln2_a.sem, 1)
                wait(act, ln2_a(g, 1))
                act.activation(ln_b[:, :, 1], ln_b[:, :, 0], ACT.Exp, scale=-1.0).then_inc(ln2_a.sem, 1)
                wait(act, ln2_v(g, 1))
                act.activation(ln_b[:, :, 3], ln_b[:, :, 2], ACT.Ln, bias=eps[:, 0:1]).then_inc(ln2_a.sem, 1)
                wait(act, ln2_v(g, 2))
                act.activation(ln_b[:, :, 5], ln_b[:, :, 4], ACT.Exp, scale=-0.5).then_inc(ln2_a.sem, 1)

            def turn2(act, g):
                for c in range(KH):
                    wait(act, z2_turned(g, c + 1))
                    act.activation(z_hi[:, c, :], bank_b[c][:, :], ACT.Identity, bias=cols[:, 1, c:c + 1],
                                   scale=cols[:, 0, c:c + 1]).then_inc(z2_copied.sem, 1)
                    act.activation(z_t[:, c, :], bank_b[c][:, :], ACT.Identity, bias=cols[:, 1, c:c + 1],
                                   scale=cols[:, 0, c:c + 1]).then_inc(z2_copied.sem, 1)

            def pick_one(act, g):
                wait(act, pick_v(g, 6))
                act.activation(pick[:, 1, :], pick[:, 0, :], ACT.Exp, bias=pick[:, 3, 0:1],
                               accum_out=pick[:, 3, 1:2]).then_inc(pick_exp.sem, 1)

            def down(act, g):
                for e in range(4):
                    wait(act, down_mm(g, e + 1))
                    act.activation(mid_hi[:, e, :], bank_b[e][:, :], ACT.Relu, bias=b_down[:, e:e + 1]).then_inc(hid_copied.sem, 1)
                    act.activation(qkv[:, e, :], bank_b[e][:, :], ACT.Relu, bias=b_down[:, e:e + 1]).then_inc(hid_copied.sem, 1)

            def turn3(act, g):
                for c in range(KH):
                    wait(act, z3_turned(g, c + 1))
                    act.activation(z_hi[:, c, :], bank_b[2 + c][:, :], ACT.Copy).then_inc(z3_hi.sem, 1)

            def queries(act, g):
                for m in range(4):
                    wait(act, qkv_mm(g, m + 1))
                    act.activation(qkv[:, m, :], bank_b[m][:, :], ACT.Copy, scale=DH**-0.5).then_inc(q_out.sem, 1)

            def values(act, g):
                for m in range(4):
                    wait(act, qkv_mm(g, 8 + m + 1))
                    if m == 2:
                        wait(act, gate_mm(g, 0))
                    act.activation(qkv[:, 8 + m, :], bank_b[m][:, :], ACT.Copy).then_inc(v_out.sem, 1)

            def scores(act, g, t):
                wait(act, s_sub(g, t + 1))
                act.activation(score[:, t % 2, :], score[:, t % 2, :], ACT.Exp).then_inc(s_exp.sem, 1)

            def heads(act, g, t):
                wait(act, pt_mm(g, t + 1))
                wait(act, o_mm(g, t - 1) if t >= 2 else o_mm(g, 0))
                act.activation(probs_t[:, t % 2, :], bank_b[t % 2][:, :], ACT.Copy).then_inc(pt_out.sem, 1)

            def outputs(act, g, t):
                wait(act, o_mm(g, t + 1))
                act.activation(by_sample(mid_hi, t), heads_out(t), ACT.Copy).then_inc(o_hi.sem, 1)

            def gate(act, g):
                for c in range(KH):
                    wait(act, z4_turned(g, c + 1))
                    act.activation(qkv[:, 10 + c, :], bank_b[2 + c][:, :], ACT.Copy).then_inc(z4_out.sem, 1)
                wait(act, gate_mm(g, 1))
                act.activation(rsc[:, :, :], bank_b[0][:, 0:TILES * E1].rearrange("p (t e) -> p t e", e=E1),
                               ACT.Exp, scale=-1.0).then_inc(gate_exp.sem, 1)

            run("scalar", act, {"ln1": ln1, "turn1": turn1, "dt": dt_bias, "soft": soft, "step": step, "ln2": ln2,
                      "turn2": turn2, "pick": pick_one, "down": down, "ln3": lambda a, g: rstd(a, g, 1), "turn3": turn3,
                      "q": queries, "v": values, "scores": scores, "heads": heads, "outputs": outputs,
                      "ln4": lambda a, g: rstd(a, g, 2), "gate": gate})

        def norm_stats(dve, src, stats, mv, stat, mean, g, k, ready, tiles=range(TILES)):
            for t in tiles:
                ready(t)
                dve.bn_stats(stats[:, t, :], src[:, t, :]).then_inc(stat.sem, 1)
            for t in tiles:
                wait(dve, stat(g, 4 * k + t + 1))
                dve.bn_aggr(mv[:, t, :], stats[:, t, :]).then_inc(mean.sem, 1)

        def normalise(dve, g):
            for t in range(TILES):
                dve.tensor_scalar(tok_b[:, t, :], h[:, t, :], mv_b[:, t, 0:1], ln_b[:, t, 5:6],
                                  ALU.subtract, ALU.mult).then_inc(z_tok.sem, 1)

        @block.vector
        def _(dve):
            dve.memset(eps[:, :], EPS).then_inc(setup_v.sem, 1)
            dve.memset(one[:, :], 1.0).then_inc(setup_v.sem, 1)
            dve.memset(rel[32:33, :], MASKED).then_inc(setup_v.sem, 1)
            for i in range(2):
                dve.memset(bank_x[i][:, :], 0.0).then_inc(setup_v.sem, 1)
            dve.wait_ge(const_in.sem, 16 * len(small))
            dve.tensor_copy(b_up[0][:, :], raw_b[0:E0, 512:768]).then_inc(w_hi_done.sem, 1)
            dve.wait_ge(w_dt_in.sem, 16)

            def split(i):
                name, pair, src = staged[i]
                hi, lo = (w[:, :, :].rearrange("p a b -> p (a b)") for w in pair)
                dve.tensor_copy(hi, src).then_inc(w_hi_done.sem, 1)
                dve.wait_ge(w_hi_done.sem, i + 2)
                dve.tensor_tensor(lo, src, hi.bitcast(F32), ALU.subtract).then_inc(w_lo_done.sem, 1)

            split(0)
            dve.tensor_tensor(b_up[1][:, :], raw_b[0:E0, 512:768], b_up[0][:, :].bitcast(F32), ALU.subtract).then_inc(small_split.sem, 1)
            dve.tensor_copy(member_r[:, :], raw_member).then_inc(small_split.sem, 1)
            dve.tensor_scalar(rel[0:32, :], rel[0:32, :], DH**0.5, None, ALU.mult).then_inc(small_split.sem, 1)
            dve.wait_ge(setup_a.sem, 3)
            dve.tensor_scalar(decay[:, :, :], decay[:, :, :], -1.0, None, ALU.mult).then_inc(setup_v.sem, 1)
            dve.tensor_tensor(bn_a[:, :], bn_a[:, :], cols[:, 2, :], ALU.mult).then_inc(setup_v.sem, 1)
            dve.wait_ge(setup_v.sem, 7)
            dve.tensor_tensor(bn_c[:, :], bn_a[:, :], cols[:, 4, :], ALU.mult).then_inc(setup_v.sem, 1)
            dve.wait_ge(setup_v.sem, 8)
            dve.tensor_tensor(bn_c[:, :], cols[:, 3, :], bn_c[:, :], ALU.subtract).then_inc(setup_v.sem, 1)
            dve.tensor_scalar(bn_a[:, :], bn_a[:, :], 1.0 / SEQ, None, ALU.mult).then_inc(setup_v.sem, 1)
            dve.wait_ge(setup_p.sem, 2)

            def patch(dve, g, b):
                wait(dve, patch_mm(g, b + 1))
                wait(dve, joined(g - 1, 0))
                dve.tensor_tensor(h0[g % 2][:, 2 * b:2 * b + 2, :], bank_a[b][:, :].rearrange("p (t n) -> p t n", t=2),
                                  posb[:, None, :].broadcast_to([P, 2, HID]), ALU.add).then_inc(patch_add.sem, 1)
                norm_stats(dve, h0[g % 2], stats_a, mv_a, stat_a, mean_a, g, 0, lambda t: wait(dve, patch_add(g, b + 1)),
                           range(2 * b, 2 * b + 2))

            def ln1(dve, g):
                wait(dve, rstd_a(g, 2))
                wait(dve, sp_v(g, 0))
                for t in range(TILES):
                    dve.tensor_scalar(tok_a[:, t, :], h0[g % 2][:, t, :], mv_a[:, t, 0:1], ln_a[:, t, 1:2],
                                      ALU.subtract, ALU.mult).then_inc(u_tok.sem, 1)

            def turn1(dve, g):
                for c in range(KH):
                    wait(dve, u_copied(g, 2 * c + 2))
                    dve.tensor_tensor(u_lo[:, c, :], bank_a[c][:, :], u_hi[:, c, :].bitcast(F32), ALU.subtract).then_inc(u_split.sem, 1)

            def dt_bias(dve, g):
                wait(dve, dt_in(g, 2))
                wait(dve, scanned(g - 1, 0))
                dve.scalar_tensor_tensor(out=drive[g % 2][:, :, :], in0=dt[g % 2][:, :, :], scalar=-1.0, in1=dt[g % 2][:, :, :],
                                         op0=ALU.mult, op1=ALU.min).then_inc(sp_v.sem, 1)

            def soft(dve, g):
                rest = tok_a[:, :, :].rearrange("p a b -> p (a b)").rearrange("p (c t) -> p c t", c=KH)
                wait(dve, sp_a(g, 1))
                dve.tensor_scalar(rest, drive[g % 2][:, :, :], 1.0, -1.0, ALU.add, ALU.add).then_inc(sp_v.sem, 1)
                wait(dve, sp_v(g, 2))
                dve.tensor_tensor(rest, drive[g % 2][:, :, :], rest, ALU.subtract).then_inc(sp_v.sem, 1)
                wait(dve, sp_v(g, 3))
                dve.scalar_tensor_tensor(out=dt[g % 2][:, :, :], in0=dt[g % 2][:, :, :], scalar=0.0, in1=rest,
                                         op0=ALU.max, op1=ALU.add).then_inc(sp_v.sem, 1)
                wait(dve, sp_a(g, 2))
                wait(dve, sp_v(g, 4))
                dve.tensor_tensor(dt[g % 2][:, :, :], dt[g % 2][:, :, :], drive[g % 2][:, :, :], ALU.add).then_inc(sp_v.sem, 1)
                wait(dve, sp_v(g, 5))
                dve.tensor_tensor(drive[g % 2][:, :, :], dt[g % 2][:, :, :], u_t[:, :, :], ALU.mult).then_inc(sp_v.sem, 1)

            def step(dve, g, i):
                wait(dve, feed_in(g, i + 1))
                wait(dve, y_sum(g, i + 1 if i >= 2 else i - 1))
                dve.tensor_tensor_scan(state[:, i % 2, :], bank_x[i % 2][:, :], feed[:, i % 2, :], 0.0,
                                       ALU.mult, ALU.add).then_inc(scanned.sem, 1)

            def join(dve, g):
                wait(dve, h_stored(g, 0))
                wait(dve, z_tok(g, 0))
                for b in range(2):
                    wait(dve, y_turned(g, b + 1))
                    dve.tensor_tensor(h[:, 2 * b:2 * b + 2, :], h0[g % 2][:, 2 * b:2 * b + 2, :],
                                      bank_a[b][:, :].rearrange("p (t n) -> p t n", t=2), ALU.add).then_inc(joined.sem, 1)
                norm_stats(dve, h, stats_b, mv_b, stat_b, mean_b, g, 0, lambda t: wait(dve, joined(g, t // 2 + 1)))

            def ln2(dve, g):
                wait(dve, ln2_a(g, 2))
                dve.tensor_tensor(ln_b[:, :, 2], mv_b[:, :, 1], ln_b[:, :, 1], ALU.mult).then_inc(ln2_v.sem, 1)
                wait(dve, ln2_a(g, 3))
                dve.tensor_tensor(ln_b[:, :, 4], ln_b[:, :, 0], ln_b[:, :, 3], ALU.add).then_inc(ln2_v.sem, 1)
                wait(dve, ln2_a(g, 4))
                dve.wait_ge(w_lo_done.sem, len(staged))
                wait(dve, z_stored(g, 0))
                normalise(dve, g)

            def turn2(dve, g):
                for c in range(KH):
                    wait(dve, z2_copied(g, 2 * c + 2))
                    dve.tensor_tensor(z_lo[:, c, :], z_t[:, c, :], z_hi[:, c, :].bitcast(F32), ALU.subtract).then_inc(z2_split.sem, 1)
                dve.tensor_reduce(zsum[:, :, :], z_t[:, :, :].rearrange("p c (b t) -> p c b t", t=SEQ), AX_X, ALU.add).then_inc(pick_v.sem, 1)
                wait(dve, pick_v(g, 1))
                for c in range(KH):
                    dve.tensor_scalar(zbn[:, c, :], zsum[:, c, :], bn_a[:, c:c + 1], bn_c[:, c:c + 1],
                                      ALU.mult, ALU.add).then_inc(pick_v.sem, 1)

            def pick_one(dve, g):
                wait(dve, pick_mm(g, 1))
                dve.tensor_tensor(pick[:, 0, :], bank_b[2][0:GS, 0:E0], br[:, :], ALU.add).then_inc(pick_v.sem, 1)
                wait(dve, pick_v(g, 4))
                dve.tensor_reduce(pick[:, 3, 2:3], pick[:, 0, :], AX_X, ALU.max).then_inc(pick_v.sem, 1)
                wait(dve, pick_v(g, 5))
                dve.tensor_scalar(pick[:, 3, 0:1], pick[:, 3, 2:3], -1.0, None, ALU.mult).then_inc(pick_v.sem, 1)
                wait(dve, pick_exp(g, 1))
                dve.reciprocal(pick[:, 3, 3:4], pick[:, 3, 1:2]).then_inc(pick_v.sem, 1)
                wait(dve, pick_v(g, 7))
                dve.tensor_scalar(pick[:, 2, :], pick[:, 1, :], pick[:, 3, 3:4], None, ALU.mult).then_inc(pick_v.sem, 1)
                wait(dve, pick_v(g, 8))
                dve.max(pick[:, 4, :], pick[:, 2, :]).then_inc(pick_v.sem, 1)
                wait(dve, pick_v(g, 9))
                dve.max_index(pick_i[:, :], pick[:, 4, :], pick[:, 2, :]).then_inc(pick_v.sem, 1)
                wait(dve, pick_v(g, 10))
                dve.tensor_copy(pick[:, 5, :], pick_i[:, :]).then_inc(pick_v.sem, 1)
                wait(dve, pick_v(g, 11))
                dve.tensor_scalar(pick[:, 6, :], iota[0:GS, 0:E0], pick[:, 5, 0:1], None, ALU.is_equal).then_inc(pick_v.sem, 1)
                wait(dve, pick_v(g, 12))
                dve.tensor_scalar(pen[:, :, :], pick[:, 6, :, None].broadcast_to([GS, E0, H0]), 1.0, PENALTY,
                                  ALU.subtract, ALU.mult).then_inc(pick_v.sem, 1)
                dve.tensor_copy(oneh_r[:, :], pick[:, 6, :]).then_inc(pick_v.sem, 1)

            def down(dve, g):
                wait(dve, pick_mm(g, 3))
                dve.tensor_copy(oneh_t[:, :], bank_b[3][0:E0, :]).then_inc(pick_v.sem, 1)
                dve.tensor_copy(gtok[:, :], bank_b[2][:, 0:TILES]).then_inc(pick_v.sem, 1)
                for e in range(4):
                    wait(dve, hid_copied(g, 2 * e + 2))
                    dve.tensor_tensor(mid_lo[:, e, :], qkv[:, e, :], mid_hi[:, e, :].bitcast(F32), ALU.subtract).then_inc(hid_split.sem, 1)

            def up(dve, g):
                for t in range(TILES):
                    wait(dve, up_mm(g, t // 2 + 1))
                    dve.scalar_tensor_tensor(out=h[:, t, :], in0=bank_b[t // 2][:, (t % 2) * HID:(t % 2 + 1) * HID],
                                             scalar=gtok[:, t:t + 1], in1=h[:, t, :], op0=ALU.mult,
                                             op1=ALU.add).then_inc(h_ffn.sem, 1)
                norm_stats(dve, h, stats_b, mv_b, stat_b, mean_b, g, 1, lambda t: wait(dve, h_ffn(g, t + 1)))

            def ln3(dve, g):
                wait(dve, rstd_b(g, 2))
                wait(dve, z2_turned(g, 2))
                normalise(dve, g)

            def turn3(dve, g):
                for c in range(KH):
                    wait(dve, z3_hi(g, c + 1))
                    dve.tensor_tensor(z_lo[:, c, :], bank_b[2 + c][:, :], z_hi[:, c, :].bitcast(F32), ALU.subtract).then_inc(z3_split.sem, 1)

            def keys(dve, g):
                for m in range(4):
                    wait(dve, qkv_mm(g, 4 + m + 1))
                    dve.tensor_copy(qkv[:, 4 + m, :], bank_b[m][:, :]).then_inc(k_out.sem, 1)

            def by_head(t):
                return score[:, t % 2, :].rearrange("p (a k) -> p a k", k=SEQ)

            def scores(dve, g, t):
                r = srow[:, t % 2]
                wait(dve, s_mm(g, t + 1))
                wait(dve, pt_mm(g, t - 1) if t >= 2 else pt_mm(g, 0))
                dve.tensor_tensor(score[:, t % 2, :].rearrange("p (j y k) -> p j y k", j=HP, y=2),
                                  bank_a[t % 2][:, :].rearrange("p (j y k) -> p j y k", j=HP, y=2),
                                  rel_bias[:, :, None, :].broadcast_to([P, HP, 2, SEQ]), ALU.add).then_inc(s_bias.sem, 1)
                wait(dve, s_bias(g, t + 1))
                dve.tensor_reduce(r[:, 0, :], by_head(t), AX_X, ALU.max).then_inc(s_max.sem, 1)
                wait(dve, s_max(g, t + 1))
                dve.tensor_tensor(by_head(t), by_head(t), r[:, 0, :, None].broadcast_to([P, 8, SEQ]), ALU.subtract).then_inc(s_sub.sem, 1)

            def probs(dve, g, t):
                r = srow[:, t % 2]
                wait(dve, s_exp(g, t + 1))
                dve.tensor_reduce(r[:, 1, :], by_head(t), AX_X, ALU.add).then_inc(s_sum.sem, 1)
                wait(dve, s_sum(g, t + 1))
                dve.reciprocal(r[:, 2, :], r[:, 1, :]).then_inc(s_rcp.sem, 1)
                wait(dve, s_rcp(g, t + 1))
                dve.tensor_tensor(by_head(t), by_head(t), r[:, 2, :, None].broadcast_to([P, 8, SEQ]), ALU.mult).then_inc(s_norm.sem, 1)

            def outputs(dve, g, t):
                wait(dve, o_hi(g, t + 1))
                dve.tensor_tensor(by_sample(mid_lo, t), heads_out(t), by_sample(mid_hi, t).bitcast(F32),
                                  ALU.subtract).then_inc(o_split.sem, 1)

            def proj(dve, g, b):
                wait(dve, bo_added(g, 1))
                wait(dve, proj_mm(g, b + 1))
                dve.tensor_tensor(h[:, 2 * b:2 * b + 2, :], bank_a[b][:, :].rearrange("p (t n) -> p t n", t=2),
                                  h[:, 2 * b:2 * b + 2, :], ALU.add).then_inc(h_attn.sem, 1)
                norm_stats(dve, h, stats_b, mv_b, stat_b, mean_b, g, 2, lambda t: wait(dve, h_attn(g, b + 1)),
                           range(2 * b, 2 * b + 2))

            def ln4(dve, g):
                wait(dve, rstd_b(g, 4))
                wait(dve, z3_turned(g, 2))
                normalise(dve, g)

            def gate(dve, g):
                wait(dve, gate_exp(g, 1))
                dve.tensor_scalar(rsc[:, :, :], rsc[:, :, :], 1.0, None, ALU.add).then_inc(gate_v.sem, 1)
                wait(dve, gate_v(g, 1))
                dve.reciprocal(rsc[:, :, :], rsc[:, :, :]).then_inc(gate_v.sem, 1)
                wait(dve, gate_v(g, 2))
                for t in range(TILES):
                    dve.max(rtop[:, t, :], rsc[:, t, :]).then_inc(gate_v.sem, 1)
                for t in range(TILES):
                    wait(dve, gate_v(g, 3 + t))
                    dve.max_index(ridx[:, t, :], rtop[:, t, :], rsc[:, t, :]).then_inc(gate_v.sem, 1)
                wait(dve, gate_v(g, 10))
                dve.tensor_copy(ridf[:, :, :], ridx[:, :, :]).then_inc(gate_v.sem, 1)
                dve.scalar_tensor_tensor(out=rw[:, :, 0:1], in0=rtop[:, :, 0:1], scalar=1e-20, in1=rtop[:, :, 1:2],
                                         op0=ALU.add, op1=ALU.add).then_inc(gate_v.sem, 1)
                wait(dve, gate_v(g, 12))
                dve.reciprocal(rw[:, :, 1:2], rw[:, :, 0:1]).then_inc(gate_v.sem, 1)
                wait(dve, gate_v(g, 13))
                dve.scalar_tensor_tensor(out=weight[:, g * TILES:(g + 1) * TILES, :], in0=rtop[:, :, 0:2], scalar=TOPK_SCALE,
                                         in1=rw[:, :, 1:2].broadcast_to([P, TILES, 2]), op0=ALU.mult, op1=ALU.mult).then_inc(gate_v.sem, 1)
                wait(dve, gate_v(g, 14))
                for t in range(TILES):
                    for k in range(2):
                        dve.tensor_scalar(chosen[:, g * TILES + t, k, :], iota[:, :], ridf[:, t, k:k + 1], None,
                                          ALU.is_equal).then_inc(gate_v.sem, 1)

            def relative(dve, g):
                if g == 0:
                    dve.wait_ge(w_in.sem, 16 * (len(staged) - 1))
                    for i in range(1, len(staged)):
                        split(i)
                    dve.wait_ge(bias_mm.sem, 1)
                    dve.tensor_copy(rel_bias[:, :, :], bank_b[0][:, 0:SEQ * HP].rearrange("p (k j) -> p j k", j=HP)).then_inc(bias_out.sem, 1)

            run("vector", dve, {"relative": relative, "patch": patch, "ln1": ln1, "turn1": turn1, "dt": dt_bias, "soft": soft,
                      "step": step, "join": join, "ln2": ln2, "turn2": turn2, "pick": pick_one, "down": down, "up": up,
                      "ln3": ln3, "turn3": turn3, "k": keys, "scores": scores, "probs": probs, "outputs": outputs,
                      "proj": proj, "ln4": ln4, "gate": gate})

        def turn(pe, tok, banks, done):
            for c in range(KH):
                for t in range(TILES):
                    mm = pe.transpose(banks[c][:, t * P:(t + 1) * P], tok[:, t, c * P:(c + 1) * P], ident[:, :])
                mm.then_inc(done.sem, 1)

        @block.tensor
        def _(pe):
            pe.wait_ge(wp_in.sem, 16)
            pe.wait_ge(const_in.sem, 16 * len(small))

            def patch(pe, g, b):
                wait(pe, joined(g - 1, 0))
                wait(pe, dt_in(g, 0))
                wait(pe, x_in[b](g, 16))
                for t in range(2 * b, 2 * b + 2):
                    for k in range(KP):
                        mm = pe.matmul(bank_a[b][:, (t % 2) * HID:(t % 2 + 1) * HID], patches[:, b, k, (t % 2) * P:(t % 2 + 1) * P],
                                       wp[:, k, :], start=(k == 0), stop=(k == KP - 1))
                mm.then_inc(patch_mm.sem, 1)

            def turn1(pe, g):
                wait(pe, u_tok(g, 4))
                turn(pe, tok_a, bank_a, u_turned)

            def dt_products(pe, g):
                pe.wait_ge(w_lo_done.sem, 1)
                wait(pe, u_split(g, 2))
                for m in range(KH):
                    for c in range(KH):
                        mm = product(pe, bank_a[m][:, :], [w[:, c, m * P:(m + 1) * P] for w in w_dt],
                                     (u_hi[:, c, :], u_lo[:, c, :]), c == 0, c == KH - 1)
                    mm.then_inc(dt_mm.sem, 1)

            def relative(pe, g):
                if g == 0:
                    pe.wait_ge(small_split.sem, 3)
                    pe.wait_ge(setup_v.sem, 3)
                    for k in range(SEQ):
                        for x in range(2):
                            mm = pe.matmul(bank_b[0][x * SEQ:(x + 1) * SEQ, k * HP:(k + 1) * HP],
                                           base[:, SEQ - 1 - k:2 * SEQ - 1 - k], rel[:, x:HEADS:2], start=True, stop=True)
                    mm.then_inc(bias_mm.sem, 1)

            def join(pe, g):
                wait(pe, y_sum(g, 2 + STEPS))
                if g + 1 < GROUPS:
                    wait(pe, dt_in(g + 1, 2))
                wait(pe, h_attn(g, 0))
                for b in range(2):
                    for t in range(2 * b, 2 * b + 2):
                        for c in range(KH):
                            at = (t % 2) * HID + c * P
                            mm = pe.transpose(bank_a[b][:, at:at + P], y_t[:, c, t * P:(t + 1) * P], ident[:, :])
                    mm.then_inc(y_turned.sem, 1)

            def turn2(pe, g):
                wait(pe, z_tok(g, 4))
                wait(pe, gate_exp(g, 0))
                pe.wait_ge(bias_out.sem, 1)
                turn(pe, tok_b, bank_b[0:2], z2_turned)

            def pick_one(pe, g):
                wait(pe, pick_v(g, 3))
                wait(pe, z4_out(g, 0))
                for c in range(KH):
                    mm = pe.matmul(bank_b[2][0:GS, 0:E0], zbn[:, c, :], wr[:, c, :], start=(c == 0), stop=(c == KH - 1))
                mm.then_inc(pick_mm.sem, 1)

            def down(pe, g):
                def units(e):
                    for c in range(KH):
                        product(pe, bank_b[e][:, :], [w[:, c, e * P:(e + 1) * P] for w in w_down],
                                (z_hi[:, c, :], z_lo[:, c, :]), c == 0, False)

                def penalise(e):
                    pe.matmul(bank_b[e][:, :], pen[:, 2 * e:2 * e + 2, :].rearrange("b e j -> b (e j)"), member_r[:, :],
                              start=False, stop=True).then_inc(down_mm.sem, 1)

                pe.wait_ge(w_lo_done.sem, len(staged))
                wait(pe, z2_split(g, 2))
                units(0)
                units(1)
                wait(pe, pick_v(g, 14))
                for t in range(TILES):
                    mm = pe.matmul(bank_b[2][:, t:t + 1], member_r[:, t * P:(t + 1) * P].bitcast(F32), pick[:, 4, 0:1], start=True, stop=True)
                mm.then_inc(pick_mm.sem, 1)
                pe.matmul(bank_b[3][0:E0, :], oneh_r[:, :], member_r[:, :], start=True, stop=True).then_inc(pick_mm.sem, 1)
                penalise(0)
                penalise(1)
                wait(pe, pick_v(g, 16))
                for e in (2, 3):
                    units(e)
                    penalise(e)

            def up(pe, g):
                def out(t):
                    return bank_b[t // 2][:, (t % 2) * HID:(t % 2 + 1) * HID]

                for e in range(4):
                    for t in range(TILES):
                        wait(pe, hid_split(g, max(e, t // 2) + 1))
                        product(pe, out(t), (mid_hi[:, e, t * P:(t + 1) * P], mid_lo[:, e, t * P:(t + 1) * P]),
                                [w[:, e, :] for w in w_up], e == 0 and t % 2 == 0, False, skip_group_check=True)
                for t in range(TILES):
                    for s in range(2):
                        mm = pe.matmul(out(t), oneh_t[:, t * P:(t + 1) * P], b_up[s][:, :], start=False, stop=(s == 1), skip_group_check=True)
                    if t % 2:
                        mm.then_inc(up_mm.sem, 1)

            def turn3(pe, g):
                wait(pe, z_tok(g, 8))
                turn(pe, tok_b, bank_b[2:4], z3_turned)

            def feature_major(pe, g, first):
                wait(pe, z3_split(g, 2))
                for m in range(first, first + 4):
                    wait(pe, h_ffn(g, 4) if m < 4 else q_out(g, m - 3))
                    for c in range(KH):
                        mm = product(pe, bank_b[m % 4][:, :], [w[:, c, m * P:(m + 1) * P] for w in w_qkv],
                                     (z_hi[:, c, :], z_lo[:, c, :]), c == 0, c == KH - 1)
                    mm.then_inc(qkv_mm.sem, 1)

            def values(pe, g):
                for t in range(TILES):
                    wait(pe, k_out(g, t + 1))
                    for c in range(KH):
                        mm = product(pe, bank_b[t][:, :], (z_hi[:, c, t * P:(t + 1) * P], z_lo[:, c, t * P:(t + 1) * P]),
                                     [w[:, c, 2 * INNER:3 * INNER] for w in w_qkv], c == 0, c == KH - 1)
                    mm.then_inc(qkv_mm.sem, 1)

            def scores(pe, g, t):
                if t == 0:
                    wait(pe, q_out(g, 4))
                    wait(pe, k_out(g, 4))
                if t < 2:
                    wait(pe, dt_in(min(g + 3, GROUPS), 0))
                    wait(pe, joined(g, 2))
                else:
                    wait(pe, s_bias(g, t - 1))
                for j in range(HP):
                    for y in range(2):
                        for x in range(2):
                            rows, tok = slice(x * DH, (x + 1) * DH), slice(t * P + y * SEQ, t * P + (y + 1) * SEQ)
                            mm = pe.matmul(bank_a[t % 2][x * SEQ:(x + 1) * SEQ, (2 * j + y) * SEQ:(2 * j + y + 1) * SEQ],
                                           qkv[rows, j, tok], qkv[rows, 4 + j, tok], start=True, stop=True)
                mm.then_inc(s_mm.sem, 1)

            def heads(pe, g, t):
                wait(pe, s_norm(g, t + 1))
                wait(pe, v_out(g, 2) if t < 2 else pt_out(g, t - 1))
                for j in range(HP):
                    mm = pe.transpose(bank_b[t % 2][:, j * P:(j + 1) * P], score[:, t % 2, j * P:(j + 1) * P], ident[:, :])
                mm.then_inc(pt_mm.sem, 1)

            def outputs(pe, g, t):
                wait(pe, pt_out(g, t + 1))
                if t == 0:
                    wait(pe, v_out(g, 4))
                if t >= 2:
                    wait(pe, o_split(g, t - 1))
                for y in range(2):
                    for j in range(HP):
                        for x in range(2):
                            rows = slice(y * SEQ, (y + 1) * SEQ)
                            if y == 1 and j == 0 and x == 0:
                                wait(pe, o_half(g, t + 1))
                            mm = pe.matmul(bank_b[2 + t % 2][x * DH:(x + 1) * DH, (y * HP + j) * SEQ:(y * HP + j + 1) * SEQ],
                                           qkv[rows, 8 + t, (2 * j + x) * DH:(2 * j + x + 1) * DH],
                                           probs_t[rows, t % 2, (2 * j + x) * SEQ:(2 * j + x + 1) * SEQ],
                                           start=True, stop=True)
                    mm.then_inc((o_half, o_mm)[y].sem, 1)

            def proj(pe, g, b):
                wait(pe, s_bias(g, 3 + b))
                for t in range(2 * b, 2 * b + 2):
                    wait(pe, o_split(g, t + 1))
                    for j in range(HP):
                        mm = product(pe, bank_a[b][:, (t % 2) * HID:(t % 2 + 1) * HID],
                                     (mid_hi[:, j, t * P:(t + 1) * P], mid_lo[:, j, t * P:(t + 1) * P]),
                                     [w[:, j, :] for w in w_o], j == 0, j == HP - 1)
                    if t % 2:
                        mm.then_inc(proj_mm.sem, 1)

            def gate(pe, g):
                wait(pe, z_tok(g, 12))
                turn(pe, tok_b, bank_b[2:4], z4_turned)
                wait(pe, z4_out(g, 2))
                for t in range(TILES):
                    for c in range(KH):
                        mm = pe.matmul(bank_b[0][:, t * E1:(t + 1) * E1], qkv[:, 10 + c, t * P:(t + 1) * P], gate_w[:, c, :],
                                       start=(c == 0), stop=(c == KH - 1))
                mm.then_inc(gate_mm.sem, 1)

            run("tensor", pe, {"relative": relative, "patch": patch, "turn1": turn1, "dt": dt_products, "join": join, "turn2": turn2,
                     "pick": pick_one, "down": down, "up": up, "turn3": turn3, "q": lambda p, g: feature_major(p, g, 0),
                     "k": lambda p, g: feature_major(p, g, 4), "v": values, "scores": scores, "heads": heads,
                     "outputs": outputs, "proj": proj, "gate": gate})


PLAN_STEPS = 17


def flat(t):
    return t[:, :, :].rearrange("p a b -> p (a b)")


def of_expert(w_hi, w_lo, e, at, n):
    if isinstance(e, int):
        return w_hi[:, e, at:at + n], w_lo[:, e, at:at + n]
    return [w[:, bass.ds(e, 1), at:at + n].rearrange("p o n -> p (o n)") for w in (w_hi, w_lo)]


def phase_two(nc, sems, d, chosen, weight, out):
    with ExitStack() as ctx:
        def sb(name, shape, dt=F32):
            return ctx.enter_context(nc.sbuf_tensor(name, shape, dt))

        def signal(name, per=1):
            return Signal(sems.enter_context(nc.semaphore(name)), per)

        NE = E1 + 1
        RAW, ZBUFS, YBUFS, GBUFS = 4, 8, 4, 8
        ALL = ALL_TILES + SLOT_TILES
        HOMED_AT = 8
        w_raw = sb("w_raw", [P, RAW, EXPERT])
        w_hi = sb("w_hi", [P, NE, EXPERT], F32R)
        w_lo = sb("w_lo", [P, NE, EXPERT], F32R)
        z = sb("z", [P, ALL_TILES, ROW])
        res = sb("res", [P, ALL_TILES, HID])
        z_slot = sb("z_slot", [P, ZBUFS, ROW])
        zt_hi = sb("zt_hi", [P, 2, HID], F32R)
        zt_lo = sb("zt_lo", [P, 2, HID], F32R)
        silu = sb("silu", [P, 2, M1])
        unit = sb("unit", [P, 2, M1])
        at_hi = sb("at_hi", [P, 2, P], F32R)
        at_lo = sb("at_lo", [P, 2, P], F32R)
        y_slot = sb("y_slot", [P, YBUFS, HID])
        home = sb("home", [P, ALL_TILES, 2], U32)
        ident = sb("ident_2", [P, P])

        plan = sb("plan", [P, 2 * P + ALL_TILES + SLOT_TILES + E1 * ALL_TILES])
        earlier, ones = plan[:, 0:P], plan[:, P:2 * P]
        at = 2 * P
        full = plan[:, at:at + ALL_TILES]
        number = plan[:, at + ALL_TILES:at + ALL_TILES + SLOT_TILES]
        carry = plan[:, at + ALL_TILES + SLOT_TILES:]
        both = sb("both", [P, ALL_TILES, E1])
        count = sb("count", [P, E1, ALL_TILES])
        upto = sb("upto", [P, E1, ALL_TILES])
        place = sb("place", [P, E1, ALL_TILES])
        fills = sb("fills", [P, E1, ALL_TILES])
        tiles = sb("tiles", [P, 3, E1])
        before = sb("before", [P, SLOT_TILES, E1])
        owner = sb("owner", [P, SLOT_TILES])
        owner_i = sb("owner_i", [P, SLOT_TILES], U32)
        mine = sb("mine", [P, ALL_TILES, 2, E1])
        slot = sb("slot", [P, ALL_TILES, 2])
        slot_i = sb("slot_i", [P, ALL_TILES, 2], U32)

        bank_z = [ctx.enter_context(nc.psum_tensor(f"bank_z{i}", [P, GT], F32)) for i in range(2)]
        bank_gu = [ctx.enter_context(nc.psum_tensor(f"bank_gu{i}", [P, GT], F32)) for i in range(2)]
        bank_t = [ctx.enter_context(nc.psum_tensor(f"bank_t{i}", [P, GT], F32)) for i in range(2)]
        bank_y = [ctx.enter_context(nc.psum_tensor(f"bank_y{i}", [P, GT], F32)) for i in range(2)]

        plan_in, w_raw_in = signal("plan_in"), [signal(f"w_raw_in{i}") for i in range(RAW)]
        z_in, res_in = [signal(f"z_in{i}") for i in range(GROUPS)], signal("res_in")
        w_hi2, w_lo2 = signal("w_hi2"), signal("w_lo2")
        plan_v, plan_mm = signal("plan_v"), signal("plan_mm")
        scattered, z_slot_in = signal("scattered"), [signal(f"z_slot_in{i}") for i in range(ZBUFS)]
        z_turned, zt_hi_done, zt_split = signal("z_turned"), signal("zt_hi_done"), signal("zt_split")
        gu_mm, silu_done, unit_done = signal("gu_mm"), signal("silu_done"), signal("unit_done")
        a_turned, at_hi_done, at_split = signal("a_turned"), signal("at_hi_done"), signal("at_split")
        y_mm, y_out, shared_added = signal("y_mm"), signal("y_out"), signal("shared_added")
        y_stored = [signal(f"y_stored{i}") for i in range(YBUFS)]
        pair_in, homed = [signal(f"pair_in{i}") for i in range(GBUFS)], signal("homed")
        combined, stored = signal("combined"), signal("stored2")

        block = ctx.enter_context(nc.Block())

        def tokens(tensor, g):
            return tensor[:, g * TILES:(g + 1) * TILES, 0:HID]

        y_pair = flat(z)[:, 0:GBUFS * 2 * HID].rearrange("p (b k n) -> p b k n", b=GBUFS, k=2)

        @block.sync
        def _(sp):
            def load_expert(i):
                if i >= RAW:
                    sp.wait_ge(w_lo2.sem, i - RAW + 1)
                sp.dma_start(w_raw[:, i % RAW, :], d["experts"][(i - 1) % NE]).then_inc(w_raw_in[i % RAW].sem, 16)

            def load_slots(j):
                if j >= ZBUFS:
                    sp.wait_ge(y_stored[j % YBUFS].sem, 16 * ((j - ZBUFS) // YBUFS + 1))
                sp.dma_start(z_slot[:, j % ZBUFS, :], d["z_slots"][j * P:(j + 1) * P, :]).then_inc(z_slot_in[j % ZBUFS].sem, 16)

            sp.dma_start(plan[:, :], d["plan"]).then_inc(plan_in.sem, 16)
            sp.dma_start(ident[:, :], d["ident"]).then_inc(plan_in.sem, 16)
            sp.dma_start(home[:, :, :], d["home"]).then_inc(plan_in.sem, 16)
            load_expert(0)
            for g in range(GROUPS):
                sp.dma_start(tokens(z, g), d["z_mid"][g]).then_inc(z_in[g].sem, 16)
                if g == 0:
                    load_expert(1)
            for g in range(GROUPS):
                sp.dma_start(tokens(res, g), d["h_mid"][g]).then_inc(res_in.sem, 16)
            for i in range(2, NE):
                load_expert(i)
            sp.wait_ge(scattered.sem, 2 * ALL_TILES * 16)
            for j in range(SLOT_TILES):
                load_slots(j)

            def load_pair(t):
                if t >= GBUFS:
                    sp.wait_ge(combined.sem, 2 * (t - GBUFS) + 2)
                sp.dma_start(y_pair[:, t % GBUFS, :, :],
                             d["y_tok"][2 * t * P:2 * (t + 1) * P, :].rearrange("(p k) n -> p k n", k=2)).then_inc(pair_in[t % GBUFS].sem, 16)

            for b in range(YBUFS):
                sp.wait_ge(y_stored[b].sem, 16 * (SLOT_TILES // YBUFS))
            for t in range(GBUFS):
                load_pair(t)
            for t in range(ALL_TILES):
                sp.wait_ge(combined.sem, 2 * t + 2)
                sp.dma_start(out[t // TILES][:, t % TILES, :], res[:, t, :]).then_inc(stored.sem, 16)
                if t + GBUFS < ALL_TILES:
                    load_pair(t + GBUFS)
            sp.wait_ge(stored.sem, 16 * ALL_TILES)

        @block.gpsimd
        def _(pool):
            pool.wait_ge(plan_v.sem, PLAN_STEPS)
            for k in range(2):
                pool.wait_ge(homed.sem, k + 1)
                for t in range(ALL_TILES):
                    if k == 0 and t % TILES == 0:
                        pool.wait_ge(z_in[t // TILES].sem, 16)
                    pool.indirect_dma_start(d["z_slots"], bass.IndirectOffsetOnAxis(slot_i[:, t, k:k + 1], 0),
                                            z[:, t, :], None).then_inc(scattered.sem, 16)
            for j in range(SLOT_TILES):
                pool.wait_ge(y_out.sem, j + 1)
                pool.indirect_dma_start(d["y_tok"], bass.IndirectOffsetOnAxis(z_slot[:, j % ZBUFS, HID:HID + 1].bitcast(U32), 0),
                                        y_slot[:, j % YBUFS, :], None).then_inc(y_stored[j % YBUFS].sem, 16)

        @block.scalar
        def _(act):
            def split(i):
                e = (i - 1) % NE
                act.wait_ge(w_raw_in[i % RAW].sem, 16 * (i // RAW + 1))
                act.activation(w_hi[:, e, :], w_raw[:, i % RAW, :], ACT.Copy).then_inc(w_hi2.sem, 1)

            split(0)
            for s in range(ALL + 3):
                if s + 1 < NE:
                    split(s + 1)
                i = s
                if i < ALL:
                    act.wait_ge(z_turned.sem, i + 1)
                    if i >= 2:
                        act.wait_ge(gu_mm.sem, i - 1)
                    act.activation(zt_hi[:, i % 2, :], bank_z[i % 2][:, 0:HID], ACT.Copy).then_inc(zt_hi_done.sem, 1)
                i = s - 1
                if 0 <= i < ALL:
                    act.wait_ge(gu_mm.sem, i + 1)
                    if i >= 2:
                        act.wait_ge(unit_done.sem, i - 1)
                    act.activation(silu[:, i % 2, :], bank_gu[i % 2][:, 0:M1], ACT.Silu).then_inc(silu_done.sem, 1)
                i = s - 2
                if 0 <= i < ALL:
                    act.wait_ge(a_turned.sem, i + 1)
                    if i >= 2:
                        act.wait_ge(y_mm.sem, i - 1)
                    act.activation(at_hi[:, i % 2, :], bank_t[i % 2][:, 0:P], ACT.Copy).then_inc(at_hi_done.sem, 1)
                i = s - 3
                j = i - ALL_TILES
                if j >= 0:
                    act.wait_ge(y_mm.sem, i + 1)
                    if j >= YBUFS:
                        act.wait_ge(y_stored[j % YBUFS].sem, 16 * (j // YBUFS))
                    act.activation(y_slot[:, j % YBUFS, :], bank_y[i % 2][:, 0:HID], ACT.Copy).then_inc(y_out.sem, 1)

        @block.vector
        def _(dve):
            dve.wait_ge(plan_in.sem, 48)
            done = 0

            def step(inst):
                nonlocal done
                inst.then_inc(plan_v.sem, 1)
                done += 1
                dve.wait_ge(plan_v.sem, done)

            def to_experts(bank):
                return bank[:, 0:ALL_TILES * E1].rearrange("p (t e) -> p e t", e=E1)

            step(dve.tensor_tensor(both[:, :, :], chosen[:, :, 0, :], chosen[:, :, 1, :], ALU.add))
            dve.wait_ge(plan_mm.sem, 1)
            step(dve.tensor_copy(count[:, :, :], to_experts(bank_z[1])))
            step(dve.tensor_tensor_scan(flat(upto), carry, flat(count), 0.0, ALU.mult, ALU.add))
            step(dve.tensor_tensor(fills[:, :, :], upto[:, :, ALL_TILES - 1:ALL_TILES].broadcast_to([P, E1, ALL_TILES]),
                                   full[:, None, :].broadcast_to([P, E1, ALL_TILES]), ALU.is_gt))
            step(dve.tensor_reduce(tiles[:, 0, :], fills[:, :, :], AX_X, ALU.add))
            step(dve.tensor_tensor_scan(tiles[:, 1, :], ones[:, 0:E1], tiles[:, 0, :], 0.0, ALU.mult, ALU.add))
            step(dve.tensor_tensor(tiles[:, 2, :], tiles[:, 1, :], tiles[:, 0, :], ALU.subtract))
            step(dve.tensor_tensor(place[:, :, :], upto[:, :, :], count[:, :, :], ALU.subtract))
            step(dve.tensor_tensor(place[:, :, :], place[:, :, :], to_experts(bank_z[0]), ALU.add))
            step(dve.scalar_tensor_tensor(out=place[:, :, :], in0=tiles[:, 2, :, None].broadcast_to([P, E1, ALL_TILES]),
                                          scalar=float(P), in1=place[:, :, :], op0=ALU.mult, op1=ALU.add))
            for k in range(2):
                step(dve.tensor_tensor(mine[:, :, k, :], chosen[:, :, k, :], place[:, :, :].rearrange("p e t -> p t e"), ALU.mult))
            step(dve.tensor_reduce(slot[:, :, :], mine[:, :, :, :], AX_X, ALU.add))
            step(dve.tensor_copy(slot_i[:, :, :], slot[:, :, :]))
            step(dve.tensor_tensor(before[:, :, :], tiles[:, 1, None, :].broadcast_to([P, SLOT_TILES, E1]),
                                   number[:, :, None].broadcast_to([P, SLOT_TILES, E1]), ALU.is_le))
            step(dve.tensor_reduce(owner[:, :], before[:, :, :], AX_X, ALU.add))
            step(dve.tensor_copy(owner_i[:, :], owner[:, :]))
            assert done == PLAN_STEPS

            def split(i):
                e = (i - 1) % NE
                dve.wait_ge(w_hi2.sem, i + 1)
                dve.tensor_tensor(w_lo[:, e, :], w_raw[:, i % RAW, :], w_hi[:, e, :].bitcast(F32), ALU.subtract).then_inc(w_lo2.sem, 1)

            def home_rows(k):
                dve.tensor_copy(z[:, :, HID:].bitcast(U32), home[:, :, k:k + 1].broadcast_to([P, ALL_TILES, ROW - HID])).then_inc(homed.sem, 1)

            home_rows(0)
            split(0)
            for s in range(ALL + 3):
                if s == HOMED_AT:
                    dve.wait_ge(scattered.sem, 16 * ALL_TILES)
                    home_rows(1)
                if s + 1 < NE:
                    split(s + 1)
                i = s
                if i < ALL:
                    dve.wait_ge(zt_hi_done.sem, i + 1)
                    dve.tensor_tensor(zt_lo[:, i % 2, :], bank_z[i % 2][:, 0:HID], zt_hi[:, i % 2, :].bitcast(F32),
                                      ALU.subtract).then_inc(zt_split.sem, 1)
                i = s - 1
                if 0 <= i < ALL:
                    dve.wait_ge(silu_done.sem, i + 1)
                    if i >= 2:
                        dve.wait_ge(a_turned.sem, i - 1)
                    dve.tensor_tensor(unit[:, i % 2, :], silu[:, i % 2, :], bank_gu[i % 2][:, M1:2 * M1], ALU.mult).then_inc(unit_done.sem, 1)
                i = s - 2
                if 0 <= i < ALL:
                    dve.wait_ge(at_hi_done.sem, i + 1)
                    dve.tensor_tensor(at_lo[:, i % 2, :], bank_t[i % 2][:, 0:P], at_hi[:, i % 2, :].bitcast(F32),
                                      ALU.subtract).then_inc(at_split.sem, 1)
                i = s - 3
                if 0 <= i < ALL_TILES:
                    if i == 0:
                        dve.wait_ge(res_in.sem, 16 * GROUPS)
                    dve.wait_ge(y_mm.sem, i + 1)
                    dve.tensor_tensor(res[:, i, :], bank_y[i % 2][:, 0:HID], res[:, i, :], ALU.add).then_inc(shared_added.sem, 1)
            dve.wait_ge(shared_added.sem, ALL_TILES)
            for i in range(2 * ALL_TILES):
                t, k = i // 2, i % 2
                dve.wait_ge(pair_in[t % GBUFS].sem, 16 * (t // GBUFS + 1))
                if k:
                    dve.wait_ge(combined.sem, i)
                dve.scalar_tensor_tensor(out=res[:, t, :], in0=y_pair[:, t % GBUFS, k, :], scalar=weight[:, t, k:k + 1],
                                         in1=res[:, t, :], op0=ALU.mult, op1=ALU.add).then_inc(combined.sem, 1)

        @block.tensor
        def _(pe):
            pe.wait_ge(plan_in.sem, 48)
            pe.wait_ge(plan_v.sem, 1)
            pe.matmul(bank_z[0][:, 0:ALL_TILES * E1], earlier, flat(both), start=True, stop=True)
            pe.matmul(bank_z[1][:, 0:ALL_TILES * E1], ones, flat(both), start=True, stop=True).then_inc(plan_mm.sem, 1)
            pe.wait_ge(plan_v.sem, PLAN_STEPS)

            owners = {}
            for s in range(ALL + 3):
                i = s
                if i < ALL:
                    j = i - ALL_TILES
                    if j < 0:
                        owners[i] = E1
                        for o in range(3 * i, 3 * i + 3):
                            owners[ALL_TILES + o] = pe.value_load(owner_i[0:1, o:o + 1], min_val=0, max_val=E1)
                        if i % TILES == 0:
                            pe.wait_ge(z_in[i // TILES].sem, 16)
                        rows = z[:, i, :]
                    else:
                        pe.wait_ge(z_slot_in[j % ZBUFS].sem, 16 * (j // ZBUFS + 1))
                        rows = z_slot[:, j % ZBUFS, :]
                    if i >= 2:
                        pe.wait_ge(zt_split.sem, i - 1)
                    for c in range(KH):
                        mm = pe.transpose(bank_z[i % 2][:, c * P:(c + 1) * P], rows[:, c * P:(c + 1) * P], ident[:, :])
                    mm.then_inc(z_turned.sem, 1)
                i = s - 1
                if 0 <= i < ALL:
                    pe.wait_ge(zt_split.sem, i + 1)
                    pe.wait_ge(w_lo2.sem, 1 if i < ALL_TILES else NE)
                    if i >= 2:
                        pe.wait_ge(unit_done.sem, i - 1)
                    for c in range(KH):
                        cut = slice(c * P, (c + 1) * P)
                        mm = product(pe, bank_gu[i % 2][:, 0:2 * M1], (zt_hi[:, i % 2, cut], zt_lo[:, i % 2, cut]),
                                     of_expert(w_hi, w_lo, owners[i], c * 2 * M1, 2 * M1), c == 0, c == KH - 1)
                    mm.then_inc(gu_mm.sem, 1)
                i = s - 2
                if 0 <= i < ALL:
                    pe.wait_ge(unit_done.sem, i + 1)
                    if i >= 2:
                        pe.wait_ge(at_split.sem, i - 1)
                    pe.transpose(bank_t[i % 2][:, 0:P], unit[:, i % 2, :], ident[:, :]).then_inc(a_turned.sem, 1)
                i = s - 3
                if 0 <= i < ALL:
                    pe.wait_ge(at_split.sem, i + 1)
                    if 2 <= i < ALL_TILES + 2:
                        pe.wait_ge(shared_added.sem, i - 1)
                    if i >= ALL_TILES + 2:
                        pe.wait_ge(y_out.sem, i - ALL_TILES - 1)
                    product(pe, bank_y[i % 2][:, 0:HID], (at_hi[:, i % 2, :], at_lo[:, i % 2, :]),
                            of_expert(w_hi, w_lo, owners[i], KH * 2 * M1, HID), True, True).then_inc(y_mm.sem, 1)


def build(nc, d, out):
    with ExitStack() as ctx:
        chosen = ctx.enter_context(nc.sbuf_tensor("chosen", [P, ALL_TILES, 2, E1], F32))
        weight = ctx.enter_context(nc.sbuf_tensor("weight", [P, ALL_TILES, 2], F32))
        phase_one(nc, ctx, d, chosen, weight)
        phase_two(nc, ctx, d, chosen, weight, out)


def kernel(**inputs):
    import numpy as np
    from concourse import bacc
    from concourse.bass_utils import run_bass_kernel_spmd

    a = {k: np.asarray(v) for k, v in inputs.items()}

    def rows(w, k):
        return w.reshape(k, P, -1).transpose(1, 0, 2)

    def column(v):
        return v.reshape(-1, P).T

    def wide(v):
        return np.broadcast_to(v, (P, v.shape[-1]))

    side, ps = 8, 16
    x = a["x"].reshape(GROUPS, GS, 3, side, ps, side, ps).transpose(0, 4, 6, 2, 1, 3, 5)
    x = x.reshape(GROUPS, KP, P, 2, GT // 2).transpose(0, 3, 2, 1, 4)

    quarter = HID // 4
    f = (10000.0 ** (np.arange(quarter, dtype=np.float32) / quarter)).astype(np.float32)
    rr, cc = [v.reshape(-1, 1).astype(np.float32) / f for v in np.meshgrid(np.arange(side), np.arange(side), indexing="ij")]
    pos = np.concatenate([np.sin(rr), np.cos(rr), np.sin(cc), np.cos(cc)], -1).astype(np.float32)
    dist = np.arange(2 * SEQ) - (SEQ - 1)
    large = 16 + (np.log(np.maximum(dist, 1).astype(np.float32) / 16) / np.log(128 / 16) * 16).astype(np.int32)
    bucket = np.where(dist < 0, 32, np.where(dist < 16, dist, np.minimum(large, 31)))
    base = (np.arange(33)[:, None] == bucket[None]).astype(np.float32)
    member = (np.arange(GS)[:, None] == np.arange(GT)[None] // SEQ).astype(np.float32)
    earlier = (np.arange(P)[:, None] < np.arange(P)[None]).astype(np.float32)
    nobody = np.tile(np.arange(SLOT_TILES * P, dtype=np.uint32)[:, None] + 2 * BATCH * SEQ, (1, ROW - HID)).view(np.float32)
    home = (2 * (np.arange(P)[:, None, None] + P * np.arange(ALL_TILES)[None, :, None]) + np.arange(2)).astype(np.uint32)
    plan = np.concatenate([earlier, np.ones((P, P)), wide(P * np.arange(ALL_TILES)), wide(np.arange(SLOT_TILES)),
                           wide(np.tile(np.arange(ALL_TILES) > 0, E1))], 1).astype(np.float32)

    experts = [np.concatenate([
        np.concatenate([rows(g, KH), rows(u, KH)], 2).reshape(P, -1), w], 1)
        for g, u, w in zip([*a["L1_ffn_w_gate"], a["L1_ffn_ws_gate"]], [*a["L1_ffn_w_up"], a["L1_ffn_ws_up"]],
                           [*a["L1_ffn_w_down"], a["L1_ffn_ws_down"]])]
    host = {
        "x": x, "wp": rows(a["L0_tok_Wp"].T, KP), "pos": np.tile(pos, (2, 1)), "tokb": wide(a["L0_tok_b"]),
        "bo": wide(a["L1_attn_bo"]), "iota": wide(np.arange(E1, dtype=np.float32)), "ident": np.eye(P, dtype=np.float32),
        "b_dt": column(a["L0_attn_b_dt"]), "skip_d": column(a["L0_attn_D_vec"]),
        "a_log": rows(a["L0_attn_A_log"], KH), "bmat": rows(a["L0_attn_B_mat"], KH), "cmat": rows(a["L0_attn_C_mat"], KH),
        "cols": np.stack([column(a["L0_ffn_" + n]) for n in ("ln_g", "ln_b", "bn_g", "bn_b", "bn_mean", "bn_var", "bn_var", "bn_var")], 1),
        "b_down": column(a["L0_ffn_b_down"].reshape(-1)), "wr": rows(a["L0_ffn_Wr"], KH),
        "br": np.broadcast_to(a["L0_ffn_br"], (E0, E0)), "gate_w": rows(a["L1_ffn_gate_w"].T, KH), "member": member,
        "rel": a["L1_attn_rel_emb"], "base": base, "b_up": a["L0_ffn_b_up"],
        "w_dt": rows(a["L0_attn_W_dt"].T, KH), "w_down": rows(a["L0_ffn_W_down"].transpose(1, 0, 2).reshape(HID, -1), KH),
        "w_up": rows(a["L0_ffn_W_up"].reshape(E0 * H0, HID), 4),
        "w_qkv": rows(np.concatenate([a["L1_attn_Wq"], a["L1_attn_Wkv"]], 1), KH), "w_o": rows(a["L1_attn_Wo"], HP),
        "experts": np.stack(experts), "plan": plan, "home": home, "nobody": nobody,
        "blank": np.zeros((P, HID), np.float32),
    }
    nc = bacc.Bacc("TRN2", target_bir_lowering=False, num_devices=1)
    arrays, d = {}, {}
    for name, v in host.items():
        arrays["in_" + name] = np.ascontiguousarray(v)
        d[name] = nc.dram_tensor("in_" + name, v.shape, mybir.dt.from_np(v.dtype), kind="ExternalInput").ap()
    d["h_mid"] = nc.dram_tensor("h_mid", (GROUPS, P, TILES, HID), F32, kind="Internal").ap()
    d["z_mid"] = nc.dram_tensor("z_mid", (GROUPS, P, TILES, HID), F32, kind="Internal").ap()
    d["z_slots"] = nc.dram_tensor("z_slots", (SLOT_TILES * P, ROW), F32, kind="Internal").ap()
    d["y_tok"] = nc.dram_tensor("y_tok", (2 * BATCH * SEQ + SLOT_TILES * P, HID), F32, kind="Internal").ap()
    out = nc.dram_tensor("out", (GROUPS, P, TILES, HID), F32, kind="ExternalOutput").ap()
    build(nc, d, out)
    got = run_bass_kernel_spmd(nc, [arrays], core_ids=[0]).results[0]["out"]
    return got.reshape(GROUPS, P, TILES, HID).transpose(0, 2, 1, 3).reshape(BATCH, SEQ, HID)
```

```python
from contextlib import ExitStack

import concourse.bass as bass
from concourse import mybir

ALU = mybir.AluOpType
ACT = mybir.ActivationFunctionType
F32 = mybir.dt.float32
F32R = mybir.dt.float32r
U32 = mybir.dt.uint32
AX_X = mybir.AxisListType.X

P = 128
BATCH, SEQ, HID = 32, 64, 256
PATCH = 768
NSTATE = 16
GROUPS = 4
GT = BATCH * SEQ // GROUPS
TILES = GT // P
GS = GT // SEQ
KH = HID // P
KP = PATCH // P
E0, H0 = 8, 64
HEADS, DH = 8, 64
INNER = HEADS * DH
HP = HEADS // 2
E1, M1 = 16, 128
TOPK_SCALE = 2.5
EPS = 1e-5
PENALTY = float(2.0**100)
MASKED = -1e37
STEPS = KH * NSTATE
EXPERT = KH * 2 * M1 + HID
ALL_TILES = GROUPS * TILES
SLOT_TILES = 2 * ALL_TILES + E1
ROW = HID + 16


class Signal:

    def __init__(self, sem, per):
        self.sem, self.per = sem, per

    def __call__(self, g, k):
        return self.sem, g * self.per + k


def wait(engine, at):
    if not (isinstance(at[1], int) and at[1] <= 0):
        engine.wait_ge(*at)


def product(pe, out, lhs, rhs, start, stop, **kw):
    pe.matmul(out, lhs[0], rhs[0], start=start, stop=False, **kw)
    pe.matmul(out, lhs[1], rhs[0], start=False, stop=False, **kw)
    return pe.matmul(out, lhs[0], rhs[1], start=False, stop=stop, **kw)


BACK = [
    ("join", 0), ("gate", -1), ("ln2", 0), ("turn2", 0), ("pick", 0), ("route", -1), ("down", 0), ("up", 0),
    ("ln3", 0), ("turn3", 0),
    ("q", 0), ("k", 0), ("similar", 0, 0), ("similar", 0, 1), ("scores", 0, 0), ("v", 0), ("scores", 0, 1), ("probs", 0, 0),
    ("similar", 0, 2), ("heads", 0, 0), ("scores", 0, 2), ("probs", 0, 1), ("similar", 0, 3), ("heads", 0, 1),
    ("outputs", 0, 0), ("scores", 0, 3), ("probs", 0, 2), ("outputs", 0, 1),
    ("heads", 0, 2), ("proj", 0, 0), ("probs", 0, 3), ("outputs", 0, 2), ("heads", 0, 3), ("outputs", 0, 3), ("proj", 0, 1),
    ("ln4", 0),
]
FRONT = [("patch", 2, 0), ("patch", 2, 1), ("ln1", 2), ("turn1", 2), ("dt", 2), ("soft", 2)]
STEP = [("step", 1, i) for i in range(STEPS)]
for at, piece in ((24, ("relative", 1)), (20, ("split", 1, 4)), (15, ("split", 1, 3)), (10, ("split", 1, 2)), (5, ("split", 1, 1))):
    STEP.insert(at, piece)
MERGED = {
    "sync": "sbssssbbssfsbsfbfbbbbfbbsssssfsssssbbbbsfsbbssbsbbbbsssbbbbsbbbbbsbsbssbssssbsb",
    "gpsimd": "ssssssssssbbbsssfsssbbbbsbbbbssfbsffsbbsbbbbbbbbfssbbbsbbbsbbssbssbfsbssbsssbsb",
    "scalar": "sbfsbbsfsbsbbsssbbsfsssfbssbssssfsbbssbfssbsbbbbbsbsbbbbsbsbssbbssbbsbsbbssbsbb",
    "vector": "sbbbsfssbsbsbbssfsfbsssbsfsbsssssbfbssbbfbbbbssbsbbbbsssbbbbssbsbssbbssbssbbsbb",
    "tensor": "sbbfsbssssbfbfbbsbfbssssssbsssfbsbssbsbsbbbsbbbbbssbbbsbbbbbbsssfsssssssbbbbsbs",
}


RAW = 9
RAW_SIZE = KP * GT + 4 * KH * GT


def expert_order(i):
    return (i - 1) % (E1 + 1)


def phase_one(nc, sems, d, chosen, weight, raw_store, w_raw_in):
    with ExitStack() as ctx:
        def sb(name, shape, dt=F32):
            return ctx.enter_context(nc.sbuf_tensor(name, shape, dt))

        def signal(name, per=1):
            return Signal(sems.enter_context(nc.semaphore(name)), per)

        ident = sb("ident", [P, P])
        posb = sb("posb", [P, HID])
        bo = sb("bo", [P, HID])
        iota = sb("iota", [P, E1])
        eps = sb("eps", [P, 1])
        one = sb("one", [P, 1])
        b_dt = sb("b_dt", [P, KH])
        skip_d = sb("skip_d", [P, KH])
        decay = sb("decay", [P, KH, NSTATE])
        bmat = sb("bmat", [P, KH, NSTATE])
        cmat = sb("cmat", [P, KH, NSTATE])
        cols = sb("cols", [P, 8, KH])
        bn_a = sb("bn_a", [P, KH])
        bn_c = sb("bn_c", [P, KH])
        b_down = sb("b_down", [P, E0 // 2])
        wr = sb("wr", [P, KH, E0])
        br = sb("br", [E0, E0])
        gate_w = sb("gate_w", [P, KH, E1])
        member_r = sb("member_r", [GS, GT], F32R)
        rel = sb("rel", [33, HEADS])
        base = sb("base", [33, 2 * SEQ])
        rel_bias = sb("rel_bias", [P, HP, SEQ])

        wp = sb("wp", [P, KP, HID])
        w_dt = [sb(f"w_dt{s}", [P, KH, HID], F32R) for s in "hl"]
        w_down = [sb(f"w_down{s}", [P, KH, E0 * H0], F32R) for s in "hl"]
        w_up = [sb(f"w_up{s}", [P, E0 * H0 // P, HID], F32R) for s in "hl"]
        w_qkv = [sb(f"w_qkv{s}", [P, KH, 3 * INNER], F32R) for s in "hl"]
        w_o = [sb(f"w_o{s}", [P, HP, HID], F32R) for s in "hl"]
        b_up = [sb(f"b_up{s}", [E0, HID], F32R) for s in "hl"]

        patches = raw_store[:, 0:KP * GT].rearrange("p (b k n) -> p b k n", b=2, k=KP)

        def stored(i):
            at = KP * GT + i * KH * GT
            return raw_store[:, at:at + KH * GT].rearrange("p (c n) -> p c n", c=KH)

        h = [sb(f"h_{i}", [P, TILES, HID]) for i in range(3)]
        tok_a = sb("tok_a", [P, TILES, HID])
        u_hi = sb("u_hi", [P, KH, GT], F32R)
        u_lo = sb("u_lo", [P, KH, GT], F32R)
        u_t = sb("u_t", [P, KH, GT])
        dt = [stored(i) for i in range(2)]
        drive = [sb(f"drive_{i}", [P, KH, GT]) for i in range(2)]
        y_t = stored(2)
        state = stored(3)
        feed = sb("feed", [P, 2, GT])
        stats_a = sb("stats_a", [P, TILES, 6])
        mv_a = sb("mv_a", [P, TILES, 2])
        ln_a = sb("ln_a", [P, TILES, 2])

        tok_b = sb("tok_b", [P, TILES, HID])
        z_hi = sb("z_hi", [P, KH, GT], F32R)
        z_lo = sb("z_lo", [P, KH, GT], F32R)
        z_t = sb("z_t", [P, KH, GT])
        mid_hi = sb("mid_hi", [P, 4, GT], F32R)
        mid_lo = sb("mid_lo", [P, 4, GT], F32R)
        qkv = sb("qkv", [P, 12, GT])
        score = sb("score", [P, 2, GT])
        probs_t = sb("probs_t", [P, 2, GT])
        stats_b = sb("stats_b", [P, TILES, 6])
        mv_b = sb("mv_b", [P, TILES, 2])
        ln_b = sb("ln_b", [P, TILES, 6])
        zsum = sb("zsum", [P, KH, GS])
        zbn = sb("zbn", [P, KH, GS])
        pick = sb("pick", [E0, 8, E0])
        pick_i = sb("pick_i", [E0, E0], U32)
        pen = sb("pen", [E0, E0, H0], F32R)
        oneh_r = sb("oneh_r", [E0, E0], F32R)
        oneh_t = sb("oneh_t", [E0, GT], F32R)
        gtok = sb("gtok", [P, TILES])
        srow = sb("srow", [P, 2, 3, 8])
        rsc = sb("rsc", [P, TILES, E1])
        rtop = sb("rtop", [P, TILES, 8])
        ridx = sb("ridx", [P, TILES, 8], U32)
        ridf = sb("ridf", [P, TILES, 8])
        rw = sb("rw", [P, TILES, 2])
        blank = sb("blank", [P, HID])

        bank_x = [ctx.enter_context(nc.psum_tensor(f"bank_x{i}", [P, GT], F32)) for i in range(2)]
        bank_a = [ctx.enter_context(nc.psum_tensor(f"bank_a{i}", [P, GT], F32)) for i in range(2)]
        bank_b = [ctx.enter_context(nc.psum_tensor(f"bank_b{i}", [P, GT], F32)) for i in range(4)]

        blank_in, zeroed = signal("blank_in"), signal("zeroed")
        const_in, wp_in, w_dt_in, w_in = signal("const_in"), signal("wp_in"), signal("w_dt_in"), signal("w_in")
        setup_v, setup_a, setup_p = signal("setup_v"), signal("setup_a"), signal("setup_p")
        w_hi_done, w_lo_done, small_split = signal("w_hi_done"), signal("w_lo_done"), signal("small_split")
        bias_mm, bias_out = signal("bias_mm"), signal("bias_out")
        x_in = [signal(f"x_in{i}", 16) for i in range(2)]
        patch_mm, patch_add = signal("patch_mm", 2), signal("patch_add", 2)
        stat_a, mean_a, rstd_a = signal("stat_a", 4), signal("mean_a", 4), signal("rstd_a", 2)
        u_tok, u_turned, u_copied = signal("u_tok", 4), signal("u_turned", 2), signal("u_copied", 4)
        u_split, dt_mm, dt_in = signal("u_split", 2), signal("dt_mm", 2), signal("dt_in", 2)
        sp_v, sp_a = signal("sp_v", 6), signal("sp_a", 2)
        decay_in, feed_in, scanned, y_sum = signal("decay_in", STEPS), signal("feed_in", STEPS), signal("scanned", STEPS), signal("y_sum", 2 + STEPS)
        y_turned, joined = signal("y_turned", 2), signal("joined", 2)
        stat_b, mean_b = signal("stat_b", 12), signal("mean_b", 12)
        ln2_a, ln2_v = signal("ln2_a", 4), signal("ln2_v", 2)
        rstd_b = signal("rstd_b", 4)
        z_tok, z2_turned, z2_copied, z2_split = signal("z_tok", 12), signal("z2_turned", 2), signal("z2_copied", 4), signal("z2_split", 2)
        pick_v, pick_mm, pick_exp = signal("pick_v", 16), signal("pick_mm", 3), signal("pick_exp", 1)
        down_mm, hid_copied, hid_split = signal("down_mm", 4), signal("hid_copied", 8), signal("hid_split", 4)
        up_mm, h_ffn = signal("up_mm", 2), signal("h_ffn", 4)
        z3_turned, z3_hi, z3_split = signal("z3_turned", 2), signal("z3_hi", 2), signal("z3_split", 2)
        qkv_mm, q_out, k_out, v_out = signal("qkv_mm", 12), signal("q_out", 4), signal("k_out", 4), signal("v_out", 4)
        bo_added = signal("bo_added", 1)
        s_bias, s_mm, s_max, s_sub = signal("s_bias", 4), signal("s_mm", 4), signal("s_max", 4), signal("s_sub", 4)
        s_exp, s_sum, s_rcp, s_norm = signal("s_exp", 4), signal("s_sum", 4), signal("s_rcp", 4), signal("s_norm", 4)
        pt_mm, pt_out, o_half, o_mm = signal("pt_mm", 4), signal("pt_out", 4), signal("o_half", 4), signal("o_mm", 4)
        o_hi, o_split, proj_mm, h_attn = signal("o_hi", 4), signal("o_split", 4), signal("proj_mm", 2), signal("h_attn", 2)
        h_stored, z_stored = signal("h_stored", 16), signal("z_stored", 16)
        z4_turned, z4_out = signal("z4_turned", 2), signal("z4_out", 2)
        gate_mm, gate_exp, gate_v = signal("gate_mm", 1), signal("gate_exp", 1), signal("gate_v", 14 + 2 * TILES)

        block = ctx.enter_context(nc.Block())

        raw = qkv[:, :, :].rearrange("p a b -> p (a b)")
        raw_b = tok_b[:, :, :].rearrange("p a b -> p (a b)")
        at, staged = 0, []
        for name, pair in (("w_down", w_down), ("w_up", w_up), ("w_qkv", w_qkv), ("w_o", w_o)):
            n = pair[0].shape[1] * pair[0].shape[2]
            staged.append((name, pair, raw[:, at:at + n]))
            at += n
        staged.insert(0, ("w_dt", w_dt, raw_b[:, 0:KH * HID]))
        tokb = raw_b[:, 768:1024]
        raw_member = score[0:GS, 0, :]
        small = [("pos", posb[:, :]), ("tokb", tokb), ("bo", bo[:, :]), ("iota", iota[:, :]),
                 ("ident", ident[:, :]), ("b_dt", b_dt[:, :]), ("skip_d", skip_d[:, :]),
                 ("a_log", decay[:, :, :]), ("bmat", bmat[:, :, :]), ("cmat", cmat[:, :, :]),
                 ("cols", cols[:, :, :]), ("b_down", b_down[:, :]), ("wr", wr[:, :, :]), ("br", br[:, :]),
                 ("gate_w", gate_w[:, :, :]), ("member", raw_member), ("rel", rel[0:32, :]),
                 ("base", base[:, :]), ("b_up", raw_b[0:E0, 512:768])]

        def run(who, engine, own):
            for n in range(-2, GROUPS + 1):
                chains = {"b": iter(BACK), "f": iter(FRONT), "s": iter(STEP)}
                for chain in MERGED[who]:
                    piece, ahead, *args = next(chains[chain])
                    if piece in own and 0 <= n + ahead < GROUPS:
                        own[piece](engine, n + ahead, *args)

        def by_sample(tiles, t):
            return tiles[:, :, t * P:(t + 1) * P].rearrange("p j (y q) -> p j y q", q=SEQ)

        def heads_out(t):
            return bank_b[2 + t % 2][:, :].rearrange("p (y j q) -> p j y q", j=HP, q=SEQ)

        def load_patches(sp, g, b):
            wait(sp, patch_mm(g - 1, b + 1))
            sp.dma_start(patches[:, b, :, :], d["x"][g, b]).then_inc(x_in[b].sem, 16)

        def store_h(sp, g, b):
            if b == 1:
                wait(sp, h_attn(g, 2))
                sp.dma_start(d["h_mid"][g], h[g % 3][:, :, :]).then_inc(h_stored.sem, 16)

        def store_z(sp, g):
            wait(sp, z_tok(g, 12))
            sp.dma_start(d["z_mid"][g], tok_b[:, :, :]).then_inc(z_stored.sem, 16)

        @block.sync
        def _(sp):
            sp.dma_start(wp[:, :, :], d["wp"]).then_inc(wp_in.sem, 16)
            load_patches(sp, 0, 0)
            load_patches(sp, 0, 1)
            for name, to in small:
                sp.dma_start(to, d[name]).then_inc(const_in.sem, 16)
            for name, _, to in staged:
                sp.dma_start(to, d[name].rearrange("p a b -> p (a b)")).then_inc((w_dt_in if name == "w_dt" else w_in).sem, 16)

            sp.dma_start(blank[:, :], d["blank"]).then_inc(blank_in.sem, 16)
            sp.wait_ge(blank_in.sem, 16)
            sp.dma_start(d["z_slots"].rearrange("(j p) n -> p j n", p=P)[:, :, 0:HID],
                         blank[:, None, :].broadcast_to([P, SLOT_TILES, HID])).then_inc(zeroed.sem, 16)
            sp.dma_start(d["z_slots"][:, HID:], d["nobody"]).then_inc(zeroed.sem, 16)

            def first_experts(sp, g):
                if g == GROUPS - 1:
                    wait(sp, y_turned(GROUPS, 0))
                    for i in range(RAW):
                        sp.dma_start(raw_store[:, i * EXPERT:(i + 1) * EXPERT], d["experts"][expert_order(i)]).then_inc(w_raw_in[i].sem, 16)

            def next_patches(sp, g, b):
                if g + 1 < GROUPS:
                    load_patches(sp, g + 1, b)

            run("sync", sp, {"patch": next_patches, "proj": store_h, "ln4": store_z, "join": first_experts})
            sp.wait_ge(zeroed.sem, 32)
            wait(sp, h_stored(GROUPS, 0))
            wait(sp, z_stored(GROUPS, 0))

        @block.gpsimd
        def _(pool):
            pool.wait_ge(const_in.sem, 16 * len(small))
            pool.tensor_tensor(posb[:, :], posb[:, :], tokb, ALU.add).then_inc(setup_p.sem, 1)
            pool.tensor_tensor(cmat[:, :, :], cmat[:, :, :], bmat[:, :, :], ALU.mult).then_inc(setup_p.sem, 1)

            def step(pool, g, i):
                if i == 0:
                    wait(pool, u_copied(g, 4))
                    wait(pool, y_turned(g, 0))
                    for c in range(KH):
                        pool.tensor_scalar(y_t[:, c, :], u_t[:, c, :], skip_d[:, c:c + 1], None, ALU.mult).then_inc(y_sum.sem, 1)
                c = i // NSTATE
                wait(pool, scanned(g, i + 1))
                wait(pool, y_sum(g, 2 + i))
                pool.tensor_tensor(y_t[:, c, :], state[:, i % 2, :], y_t[:, c, :], ALU.add).then_inc(y_sum.sem, 1)

            def add_output_bias(pool, g):
                wait(pool, z_tok(g, 8))
                pool.tensor_tensor(h[g % 3][:, :, :], h[g % 3][:, :, :], bo[:, None, :].broadcast_to([P, TILES, HID]),
                                   ALU.add).then_inc(bo_added.sem, 1)

            run("gpsimd", pool, {"step": step, "ln3": add_output_bias})

        def rstd(act, g, k):
            wait(act, mean_b(g, 4 * (k + 1)))
            act.activation(ln_b[:, :, 0], mv_b[:, :, 1], ACT.Ln, bias=eps[:, 0:1]).then_inc(rstd_b.sem, 1)
            wait(act, rstd_b(g, 2 * k - 1))
            act.activation(ln_b[:, :, 5], ln_b[:, :, 0], ACT.Exp, scale=-0.5).then_inc(rstd_b.sem, 1)

        @block.scalar
        def _(act):
            act.preload_act_table_set("natural_log_exp_and_others")
            act.wait_ge(setup_v.sem, 5)
            act.wait_ge(const_in.sem, 16 * len(small))
            act.activation(decay[:, :, :], decay[:, :, :], ACT.Exp).then_inc(setup_a.sem, 1)
            act.activation(bn_a[:, :], cols[:, 5, :], ACT.Ln, bias=eps[:, 0:1]).then_inc(setup_a.sem, 1)
            act.wait_ge(setup_a.sem, 2)
            act.activation(bn_a[:, :], bn_a[:, :], ACT.Exp, scale=-0.5).then_inc(setup_a.sem, 1)

            def ln1(act, g):
                wait(act, mean_a(g, 4))
                act.activation(ln_a[:, :, 0], mv_a[:, :, 1], ACT.Ln, bias=eps[:, 0:1]).then_inc(rstd_a.sem, 1)
                wait(act, rstd_a(g, 1))
                act.activation(ln_a[:, :, 1], ln_a[:, :, 0], ACT.Exp, scale=-0.5).then_inc(rstd_a.sem, 1)

            def turn1(act, g):
                for c in range(KH):
                    wait(act, u_turned(g, c + 1))
                    act.activation(u_hi[:, c, :], bank_a[c][:, :], ACT.Copy).then_inc(u_copied.sem, 1)
                    if c == 0:
                        wait(act, y_sum(g - 1, 2))
                        wait(act, sp_v(g, 0))
                    act.activation(u_t[:, c, :], bank_a[c][:, :], ACT.Copy).then_inc(u_copied.sem, 1)

            def dt_bias(act, g):
                wait(act, scanned(g - 1, 0))
                for c in range(KH):
                    wait(act, dt_mm(g, c + 1))
                    act.activation(dt[g % 2][:, c, :], bank_a[c][:, :], ACT.Identity, bias=b_dt[:, c:c + 1]).then_inc(dt_in.sem, 1)

            def soft(act, g):
                wait(act, sp_v(g, 1))
                act.activation(drive[g % 2][:, :, :], drive[g % 2][:, :, :], ACT.Exp).then_inc(sp_a.sem, 1)
                wait(act, sp_v(g, 3))
                act.activation(drive[g % 2][:, :, :], drive[g % 2][:, :, :], ACT.Ln, bias=one[:, 0:1]).then_inc(sp_a.sem, 1)

            def step(act, g, i):
                if i == 0:
                    wait(act, sp_v(g, 6))
                    act.wait_ge(setup_v.sem, 6)
                c, n = divmod(i, NSTATE)
                wait(act, scanned(g, i - 1))
                act.activation(bank_x[i % 2][:, :].rearrange("p (b t) -> p b t", t=SEQ)[:, :, 1:SEQ],
                               dt[g % 2][:, c, :].rearrange("p (b t) -> p b t", t=SEQ)[:, :, 1:SEQ],
                               ACT.Exp, scale=decay[:, c, n:n + 1]).then_inc(decay_in.sem, 1)
                act.activation(feed[:, i % 2, :], drive[g % 2][:, c, :], ACT.Copy, scale=cmat[:, c, n:n + 1]).then_inc(feed_in.sem, 1)

            def ln2(act, g):
                wait(act, mean_b(g, 4))
                act.activation(ln_b[:, :, 0], mv_b[:, :, 1], ACT.Ln, bias=eps[:, 0:1]).then_inc(ln2_a.sem, 1)
                wait(act, ln2_a(g, 1))
                act.activation(ln_b[:, :, 1], ln_b[:, :, 0], ACT.Exp, scale=-1.0).then_inc(ln2_a.sem, 1)
                wait(act, ln2_v(g, 1))
                act.activation(ln_b[:, :, 3], ln_b[:, :, 2], ACT.Ln, bias=eps[:, 0:1]).then_inc(ln2_a.sem, 1)
                wait(act, ln2_v(g, 2))
                act.activation(ln_b[:, :, 5], ln_b[:, :, 4], ACT.Exp, scale=-0.5).then_inc(ln2_a.sem, 1)

            def turn2(act, g):
                for c in range(KH):
                    wait(act, z2_turned(g, c + 1))
                    act.activation(z_hi[:, c, :], bank_b[c][:, :], ACT.Identity, bias=cols[:, 1, c:c + 1],
                                   scale=cols[:, 0, c:c + 1]).then_inc(z2_copied.sem, 1)
                    act.activation(z_t[:, c, :], bank_b[c][:, :], ACT.Identity, bias=cols[:, 1, c:c + 1],
                                   scale=cols[:, 0, c:c + 1]).then_inc(z2_copied.sem, 1)

            def pick_one(act, g):
                wait(act, pick_v(g, 6))
                act.activation(pick[:, 1, :], pick[:, 0, :], ACT.Exp, bias=pick[:, 3, 0:1],
                               accum_out=pick[:, 3, 1:2]).then_inc(pick_exp.sem, 1)

            def down(act, g):
                for e in range(4):
                    wait(act, down_mm(g, e + 1))
                    act.activation(mid_hi[:, e, :], bank_b[e][:, :], ACT.Relu, bias=b_down[:, e:e + 1]).then_inc(hid_copied.sem, 1)
                    act.activation(qkv[:, e, :], bank_b[e][:, :], ACT.Relu, bias=b_down[:, e:e + 1]).then_inc(hid_copied.sem, 1)

            def turn3(act, g):
                for c in range(KH):
                    wait(act, z3_turned(g, c + 1))
                    act.activation(z_hi[:, c, :], bank_b[2 + c][:, :], ACT.Copy).then_inc(z3_hi.sem, 1)

            def queries(act, g):
                for m in range(4):
                    wait(act, qkv_mm(g, m + 1))
                    act.activation(qkv[:, m, :], bank_b[m][:, :], ACT.Copy, scale=DH**-0.5).then_inc(q_out.sem, 1)

            def keys(act, g):
                for m in range(4):
                    wait(act, qkv_mm(g, 4 + m + 1))
                    act.activation(qkv[:, 4 + m, :], bank_b[m][:, :], ACT.Copy).then_inc(k_out.sem, 1)

            def values(act, g):
                for m in range(4):
                    wait(act, qkv_mm(g, 8 + m + 1))
                    if m == 2:
                        wait(act, gate_mm(g, 0))
                    act.activation(qkv[:, 8 + m, :], bank_b[m][:, :], ACT.Copy).then_inc(v_out.sem, 1)

            def scores(act, g, t):
                wait(act, s_sub(g, t + 1))
                act.activation(score[:, t % 2, :], score[:, t % 2, :], ACT.Exp).then_inc(s_exp.sem, 1)

            def heads(act, g, t):
                wait(act, pt_mm(g, t + 1))
                wait(act, o_mm(g, t - 1) if t >= 2 else o_mm(g, 0))
                act.activation(probs_t[:, t % 2, :], bank_b[t % 2][:, :], ACT.Copy).then_inc(pt_out.sem, 1)

            def outputs(act, g, t):
                wait(act, o_mm(g, t + 1))
                act.activation(by_sample(mid_hi, t), heads_out(t), ACT.Copy).then_inc(o_hi.sem, 1)

            def gate(act, g):
                for c in range(KH):
                    wait(act, z4_turned(g, c + 1))
                    act.activation(qkv[:, 10 + c, :], bank_b[2 + c][:, :], ACT.Copy).then_inc(z4_out.sem, 1)
                wait(act, gate_mm(g, 1))
                wait(act, gate_v(g, 0))
                act.activation(rsc[:, :, :], bank_b[0][:, 0:TILES * E1].rearrange("p (t e) -> p t e", e=E1),
                               ACT.Exp, scale=-1.0).then_inc(gate_exp.sem, 1)

            run("scalar", act, {"ln1": ln1, "turn1": turn1, "dt": dt_bias, "soft": soft, "step": step, "ln2": ln2,
                      "turn2": turn2, "pick": pick_one, "down": down, "ln3": lambda a, g: rstd(a, g, 1), "turn3": turn3,
                      "q": queries, "k": keys, "v": values, "scores": scores, "heads": heads, "outputs": outputs,
                      "ln4": lambda a, g: rstd(a, g, 2), "gate": gate})

        def norm_stats(dve, src, stats, mv, stat, mean, g, k, ready, tiles=range(TILES)):
            for t in tiles:
                ready(t)
                dve.bn_stats(stats[:, t, :], src[:, t, :]).then_inc(stat.sem, 1)
            for t in tiles:
                wait(dve, stat(g, 4 * k + t + 1))
                dve.bn_aggr(mv[:, t, :], stats[:, t, :]).then_inc(mean.sem, 1)

        def normalise(dve, g):
            for t in range(TILES):
                dve.tensor_scalar(tok_b[:, t, :], h[g % 3][:, t, :], mv_b[:, t, 0:1], ln_b[:, t, 5:6],
                                  ALU.subtract, ALU.mult).then_inc(z_tok.sem, 1)

        @block.vector
        def _(dve):
            dve.memset(eps[:, :], EPS).then_inc(setup_v.sem, 1)
            dve.memset(one[:, :], 1.0).then_inc(setup_v.sem, 1)
            dve.memset(rel[32:33, :], MASKED).then_inc(setup_v.sem, 1)
            for i in range(2):
                dve.memset(bank_x[i][:, :], 0.0).then_inc(setup_v.sem, 1)
            dve.wait_ge(const_in.sem, 16 * len(small))
            dve.tensor_copy(b_up[0][:, :], raw_b[0:E0, 512:768]).then_inc(w_hi_done.sem, 1)
            dve.wait_ge(w_dt_in.sem, 16)

            def split(i):
                name, pair, src = staged[i]
                hi, lo = (w[:, :, :].rearrange("p a b -> p (a b)") for w in pair)
                dve.tensor_copy(hi, src).then_inc(w_hi_done.sem, 1)
                dve.wait_ge(w_hi_done.sem, i + 2)
                dve.tensor_tensor(lo, src, hi.bitcast(F32), ALU.subtract).then_inc(w_lo_done.sem, 1)

            split(0)
            dve.tensor_tensor(b_up[1][:, :], raw_b[0:E0, 512:768], b_up[0][:, :].bitcast(F32), ALU.subtract).then_inc(small_split.sem, 1)
            dve.tensor_copy(member_r[:, :], raw_member).then_inc(small_split.sem, 1)
            dve.tensor_scalar(rel[0:32, :], rel[0:32, :], DH**0.5, None, ALU.mult).then_inc(small_split.sem, 1)
            dve.wait_ge(setup_a.sem, 3)
            dve.tensor_scalar(decay[:, :, :], decay[:, :, :], -1.0, None, ALU.mult).then_inc(setup_v.sem, 1)
            dve.tensor_tensor(bn_a[:, :], bn_a[:, :], cols[:, 2, :], ALU.mult).then_inc(setup_v.sem, 1)
            dve.wait_ge(setup_v.sem, 7)
            dve.tensor_tensor(bn_c[:, :], bn_a[:, :], cols[:, 4, :], ALU.mult).then_inc(setup_v.sem, 1)
            dve.wait_ge(setup_v.sem, 8)
            dve.tensor_tensor(bn_c[:, :], cols[:, 3, :], bn_c[:, :], ALU.subtract).then_inc(setup_v.sem, 1)
            dve.tensor_scalar(bn_a[:, :], bn_a[:, :], 1.0 / SEQ, None, ALU.mult).then_inc(setup_v.sem, 1)
            dve.wait_ge(setup_p.sem, 2)

            def patch(dve, g, b):
                wait(dve, patch_mm(g, b + 1))
                wait(dve, z_tok(g - 2, 0))
                wait(dve, h_stored(g - 2, 0))
                dve.tensor_tensor(h[g % 3][:, 2 * b:2 * b + 2, :], bank_a[b][:, :].rearrange("p (t n) -> p t n", t=2),
                                  posb[:, None, :].broadcast_to([P, 2, HID]), ALU.add).then_inc(patch_add.sem, 1)
                norm_stats(dve, h[g % 3], stats_a, mv_a, stat_a, mean_a, g, 0, lambda t: wait(dve, patch_add(g, b + 1)),
                           range(2 * b, 2 * b + 2))

            def ln1(dve, g):
                wait(dve, rstd_a(g, 2))
                wait(dve, sp_v(g, 0))
                for t in range(TILES):
                    dve.tensor_scalar(tok_a[:, t, :], h[g % 3][:, t, :], mv_a[:, t, 0:1], ln_a[:, t, 1:2],
                                      ALU.subtract, ALU.mult).then_inc(u_tok.sem, 1)

            def turn1(dve, g):
                for c in range(KH):
                    wait(dve, u_copied(g, 2 * c + 2))
                    dve.tensor_tensor(u_lo[:, c, :], bank_a[c][:, :], u_hi[:, c, :].bitcast(F32), ALU.subtract).then_inc(u_split.sem, 1)

            def dt_bias(dve, g):
                wait(dve, dt_in(g, 2))
                wait(dve, scanned(g - 1, 0))
                dve.scalar_tensor_tensor(out=drive[g % 2][:, :, :], in0=dt[g % 2][:, :, :], scalar=-1.0, in1=dt[g % 2][:, :, :],
                                         op0=ALU.mult, op1=ALU.min).then_inc(sp_v.sem, 1)

            def soft(dve, g):
                rest = tok_a[:, :, :].rearrange("p a b -> p (a b)").rearrange("p (c t) -> p c t", c=KH)
                wait(dve, sp_a(g, 1))
                dve.tensor_scalar(rest, drive[g % 2][:, :, :], 1.0, -1.0, ALU.add, ALU.add).then_inc(sp_v.sem, 1)
                wait(dve, sp_v(g, 2))
                dve.tensor_tensor(rest, drive[g % 2][:, :, :], rest, ALU.subtract).then_inc(sp_v.sem, 1)
                wait(dve, sp_v(g, 3))
                dve.scalar_tensor_tensor(out=dt[g % 2][:, :, :], in0=dt[g % 2][:, :, :], scalar=0.0, in1=rest,
                                         op0=ALU.max, op1=ALU.add).then_inc(sp_v.sem, 1)
                wait(dve, sp_a(g, 2))
                wait(dve, sp_v(g, 4))
                dve.tensor_tensor(dt[g % 2][:, :, :], dt[g % 2][:, :, :], drive[g % 2][:, :, :], ALU.add).then_inc(sp_v.sem, 1)
                wait(dve, sp_v(g, 5))
                dve.tensor_tensor(drive[g % 2][:, :, :], dt[g % 2][:, :, :], u_t[:, :, :], ALU.mult).then_inc(sp_v.sem, 1)

            def step(dve, g, i):
                wait(dve, feed_in(g, i + 1))
                wait(dve, y_sum(g, i + 1 if i >= 2 else i - 1))
                dve.tensor_tensor_scan(state[:, i % 2, :], bank_x[i % 2][:, :], feed[:, i % 2, :], 0.0,
                                       ALU.mult, ALU.add).then_inc(scanned.sem, 1)

            def join(dve, g):
                wait(dve, u_tok(g, 4))
                for b in range(2):
                    wait(dve, y_turned(g, b + 1))
                    dve.tensor_tensor(h[g % 3][:, 2 * b:2 * b + 2, :], h[g % 3][:, 2 * b:2 * b + 2, :],
                                      bank_a[b][:, :].rearrange("p (t n) -> p t n", t=2), ALU.add).then_inc(joined.sem, 1)
                norm_stats(dve, h[g % 3], stats_b, mv_b, stat_b, mean_b, g, 0, lambda t: wait(dve, joined(g, t // 2 + 1)))

            def ln2(dve, g):
                wait(dve, ln2_a(g, 2))
                dve.tensor_tensor(ln_b[:, :, 2], mv_b[:, :, 1], ln_b[:, :, 1], ALU.mult).then_inc(ln2_v.sem, 1)
                wait(dve, ln2_a(g, 3))
                dve.tensor_tensor(ln_b[:, :, 4], ln_b[:, :, 0], ln_b[:, :, 3], ALU.add).then_inc(ln2_v.sem, 1)
                wait(dve, ln2_a(g, 4))
                dve.wait_ge(w_lo_done.sem, len(staged))
                wait(dve, z_stored(g, 0))
                normalise(dve, g)

            def turn2(dve, g):
                for c in range(KH):
                    wait(dve, z2_copied(g, 2 * c + 2))
                    dve.tensor_tensor(z_lo[:, c, :], z_t[:, c, :], z_hi[:, c, :].bitcast(F32), ALU.subtract).then_inc(z2_split.sem, 1)
                dve.tensor_reduce(zsum[:, :, :], z_t[:, :, :].rearrange("p c (b t) -> p c b t", t=SEQ), AX_X, ALU.add).then_inc(pick_v.sem, 1)
                wait(dve, pick_v(g, 1))
                for c in range(KH):
                    dve.tensor_scalar(zbn[:, c, :], zsum[:, c, :], bn_a[:, c:c + 1], bn_c[:, c:c + 1],
                                      ALU.mult, ALU.add).then_inc(pick_v.sem, 1)

            def pick_one(dve, g):
                wait(dve, pick_mm(g, 1))
                dve.tensor_tensor(pick[:, 0, :], bank_b[2][0:GS, 0:E0], br[:, :], ALU.add).then_inc(pick_v.sem, 1)
                wait(dve, pick_v(g, 4))
                dve.tensor_reduce(pick[:, 3, 2:3], pick[:, 0, :], AX_X, ALU.max).then_inc(pick_v.sem, 1)
                wait(dve, pick_v(g, 5))
                dve.tensor_scalar(pick[:, 3, 0:1], pick[:, 3, 2:3], -1.0, None, ALU.mult).then_inc(pick_v.sem, 1)
                wait(dve, pick_exp(g, 1))
                dve.reciprocal(pick[:, 3, 3:4], pick[:, 3, 1:2]).then_inc(pick_v.sem, 1)
                wait(dve, pick_v(g, 7))
                dve.tensor_scalar(pick[:, 2, :], pick[:, 1, :], pick[:, 3, 3:4], None, ALU.mult).then_inc(pick_v.sem, 1)
                wait(dve, pick_v(g, 8))
                dve.max(pick[:, 4, :], pick[:, 2, :]).then_inc(pick_v.sem, 1)
                wait(dve, pick_v(g, 9))
                dve.max_index(pick_i[:, :], pick[:, 4, :], pick[:, 2, :]).then_inc(pick_v.sem, 1)
                wait(dve, pick_v(g, 10))
                dve.tensor_copy(pick[:, 5, :], pick_i[:, :]).then_inc(pick_v.sem, 1)
                wait(dve, pick_v(g, 11))
                dve.tensor_scalar(pick[:, 6, :], iota[0:GS, 0:E0], pick[:, 5, 0:1], None, ALU.is_equal).then_inc(pick_v.sem, 1)
                wait(dve, pick_v(g, 12))
                dve.tensor_scalar(pen[:, :, :], pick[:, 6, :, None].broadcast_to([GS, E0, H0]), 1.0, PENALTY,
                                  ALU.subtract, ALU.mult).then_inc(pick_v.sem, 1)
                dve.tensor_copy(oneh_r[:, :], pick[:, 6, :]).then_inc(pick_v.sem, 1)

            def down(dve, g):
                wait(dve, pick_mm(g, 3))
                dve.tensor_copy(oneh_t[:, :], bank_b[3][0:E0, :]).then_inc(pick_v.sem, 1)
                dve.tensor_copy(gtok[:, :], bank_b[2][:, 0:TILES]).then_inc(pick_v.sem, 1)
                for e in range(4):
                    wait(dve, hid_copied(g, 2 * e + 2))
                    dve.tensor_tensor(mid_lo[:, e, :], qkv[:, e, :], mid_hi[:, e, :].bitcast(F32), ALU.subtract).then_inc(hid_split.sem, 1)

            def up(dve, g):
                for t in range(TILES):
                    wait(dve, up_mm(g, t // 2 + 1))
                    dve.scalar_tensor_tensor(out=h[g % 3][:, t, :], in0=bank_b[t // 2][:, (t % 2) * HID:(t % 2 + 1) * HID],
                                             scalar=gtok[:, t:t + 1], in1=h[g % 3][:, t, :], op0=ALU.mult,
                                             op1=ALU.add).then_inc(h_ffn.sem, 1)
                norm_stats(dve, h[g % 3], stats_b, mv_b, stat_b, mean_b, g, 1, lambda t: wait(dve, h_ffn(g, t + 1)))

            def ln3(dve, g):
                wait(dve, rstd_b(g, 2))
                wait(dve, z2_turned(g, 2))
                normalise(dve, g)

            def turn3(dve, g):
                for c in range(KH):
                    wait(dve, z3_hi(g, c + 1))
                    dve.tensor_tensor(z_lo[:, c, :], bank_b[2 + c][:, :], z_hi[:, c, :].bitcast(F32), ALU.subtract).then_inc(z3_split.sem, 1)

            def by_head(t):
                return score[:, t % 2, :].rearrange("p (a k) -> p a k", k=SEQ)

            def scores(dve, g, t):
                r = srow[:, t % 2]
                wait(dve, s_mm(g, t + 1))
                wait(dve, pt_mm(g, t - 1) if t >= 2 else pt_mm(g, 0))
                dve.tensor_reduce(r[:, 0, :], bank_a[t % 2][:, :].rearrange("p (a k) -> p a k", k=SEQ), AX_X, ALU.max).then_inc(s_max.sem, 1)
                wait(dve, s_max(g, t + 1))
                dve.tensor_tensor(by_head(t), bank_a[t % 2][:, :].rearrange("p (a k) -> p a k", k=SEQ),
                                  r[:, 0, :, None].broadcast_to([P, 8, SEQ]), ALU.subtract).then_inc(s_sub.sem, 1)

            def probs(dve, g, t):
                r = srow[:, t % 2]
                wait(dve, s_exp(g, t + 1))
                dve.tensor_reduce(r[:, 1, :], by_head(t), AX_X, ALU.add).then_inc(s_sum.sem, 1)
                wait(dve, s_sum(g, t + 1))
                dve.reciprocal(r[:, 2, :], r[:, 1, :]).then_inc(s_rcp.sem, 1)
                wait(dve, s_rcp(g, t + 1))
                dve.tensor_tensor(by_head(t), by_head(t), r[:, 2, :, None].broadcast_to([P, 8, SEQ]), ALU.mult).then_inc(s_norm.sem, 1)

            def outputs(dve, g, t):
                wait(dve, o_hi(g, t + 1))
                dve.tensor_tensor(by_sample(mid_lo, t), heads_out(t), by_sample(mid_hi, t).bitcast(F32),
                                  ALU.subtract).then_inc(o_split.sem, 1)

            def proj(dve, g, b):
                wait(dve, bo_added(g, 1))
                wait(dve, proj_mm(g, b + 1))
                dve.tensor_tensor(h[g % 3][:, 2 * b:2 * b + 2, :], bank_a[b][:, :].rearrange("p (t n) -> p t n", t=2),
                                  h[g % 3][:, 2 * b:2 * b + 2, :], ALU.add).then_inc(h_attn.sem, 1)
                norm_stats(dve, h[g % 3], stats_b, mv_b, stat_b, mean_b, g, 2, lambda t: wait(dve, h_attn(g, b + 1)),
                           range(2 * b, 2 * b + 2))

            def ln4(dve, g):
                wait(dve, rstd_b(g, 4))
                wait(dve, z3_turned(g, 2))
                normalise(dve, g)

            def route(dve, g):
                wait(dve, gate_exp(g, 1))
                dve.tensor_scalar(rsc[:, :, :], rsc[:, :, :], 1.0, None, ALU.add).then_inc(gate_v.sem, 1)
                wait(dve, gate_v(g, 1))
                dve.reciprocal(rsc[:, :, :], rsc[:, :, :]).then_inc(gate_v.sem, 1)
                wait(dve, gate_v(g, 2))
                for t in range(TILES):
                    dve.max(rtop[:, t, :], rsc[:, t, :]).then_inc(gate_v.sem, 1)
                for t in range(TILES):
                    wait(dve, gate_v(g, 3 + t))
                    dve.max_index(ridx[:, t, :], rtop[:, t, :], rsc[:, t, :]).then_inc(gate_v.sem, 1)
                wait(dve, gate_v(g, 10))
                dve.tensor_copy(ridf[:, :, :], ridx[:, :, :]).then_inc(gate_v.sem, 1)
                dve.scalar_tensor_tensor(out=rw[:, :, 0:1], in0=rtop[:, :, 0:1], scalar=1e-20, in1=rtop[:, :, 1:2],
                                         op0=ALU.add, op1=ALU.add).then_inc(gate_v.sem, 1)
                wait(dve, gate_v(g, 12))
                dve.reciprocal(rw[:, :, 1:2], rw[:, :, 0:1]).then_inc(gate_v.sem, 1)
                wait(dve, gate_v(g, 13))
                dve.scalar_tensor_tensor(out=weight[:, g * TILES:(g + 1) * TILES, :], in0=rtop[:, :, 0:2], scalar=TOPK_SCALE,
                                         in1=rw[:, :, 1:2].broadcast_to([P, TILES, 2]), op0=ALU.mult, op1=ALU.mult).then_inc(gate_v.sem, 1)
                wait(dve, gate_v(g, 14))
                for t in range(TILES):
                    for k in range(2):
                        dve.tensor_scalar(chosen[:, g * TILES + t, k, :], iota[:, :], ridf[:, t, k:k + 1], None,
                                          ALU.is_equal).then_inc(gate_v.sem, 1)

            def split_weight(dve, g, i):
                if g == 0:
                    dve.wait_ge(w_in.sem, 16 * (len(staged) - 1))
                    split(i)

            def relative(dve, g):
                if g == 0:
                    dve.wait_ge(bias_mm.sem, 1)
                    dve.tensor_copy(rel_bias[:, :, :], bank_b[0][:, 0:SEQ * HP].rearrange("p (k j) -> p j k", j=HP)).then_inc(bias_out.sem, 1)

            run("vector", dve, {"split": split_weight, "relative": relative, "patch": patch, "ln1": ln1, "turn1": turn1, "dt": dt_bias, "soft": soft,
                      "step": step, "join": join, "ln2": ln2, "turn2": turn2, "pick": pick_one, "down": down, "up": up,
                      "ln3": ln3, "turn3": turn3, "scores": scores, "probs": probs, "outputs": outputs,
                      "proj": proj, "ln4": ln4, "route": route})

        def turn(pe, tok, banks, ready, done):
            for t in range(TILES):
                ready(t)
                for c in range(KH):
                    mm = pe.transpose(banks[c][:, t * P:(t + 1) * P], tok[:, t, c * P:(c + 1) * P], ident[:, :])
                    if t == TILES - 1:
                        mm.then_inc(done.sem, 1)

        @block.tensor
        def _(pe):
            pe.wait_ge(wp_in.sem, 16)
            pe.wait_ge(const_in.sem, 16 * len(small))

            def patch(pe, g, b):
                wait(pe, joined(g - 1, 0))
                wait(pe, dt_in(g, 0))
                wait(pe, x_in[b](g, 16))
                for t in range(2 * b, 2 * b + 2):
                    for k in range(KP):
                        mm = pe.matmul(bank_a[b][:, (t % 2) * HID:(t % 2 + 1) * HID], patches[:, b, k, (t % 2) * P:(t % 2 + 1) * P],
                                       wp[:, k, :], start=(k == 0), stop=(k == KP - 1))
                mm.then_inc(patch_mm.sem, 1)

            def turn1(pe, g):
                turn(pe, tok_a, bank_a, lambda t: wait(pe, u_tok(g, t + 1)), u_turned)

            def dt_products(pe, g):
                pe.wait_ge(w_lo_done.sem, 1)
                wait(pe, u_split(g, 2))
                for m in range(KH):
                    for c in range(KH):
                        mm = product(pe, bank_a[m][:, :], [w[:, c, m * P:(m + 1) * P] for w in w_dt],
                                     (u_hi[:, c, :], u_lo[:, c, :]), c == 0, c == KH - 1)
                    mm.then_inc(dt_mm.sem, 1)

            def relative(pe, g):
                if g == 0:
                    pe.wait_ge(small_split.sem, 3)
                    pe.wait_ge(setup_v.sem, 3)
                    for k in range(SEQ):
                        for x in range(2):
                            mm = pe.matmul(bank_b[0][x * SEQ:(x + 1) * SEQ, k * HP:(k + 1) * HP],
                                           base[:, SEQ - 1 - k:2 * SEQ - 1 - k], rel[:, x:HEADS:2], start=True, stop=True)
                    mm.then_inc(bias_mm.sem, 1)

            def join(pe, g):
                wait(pe, y_sum(g, 2 + STEPS))
                if g + 1 < GROUPS:
                    wait(pe, dt_in(g + 1, 2))
                wait(pe, h_attn(g, 0))
                for b in range(2):
                    for t in range(2 * b, 2 * b + 2):
                        for c in range(KH):
                            at = (t % 2) * HID + c * P
                            mm = pe.transpose(bank_a[b][:, at:at + P], y_t[:, c, t * P:(t + 1) * P], ident[:, :])
                    mm.then_inc(y_turned.sem, 1)

            def turn2(pe, g):
                wait(pe, gate_exp(g, 0))
                pe.wait_ge(bias_out.sem, 1)
                turn(pe, tok_b, bank_b[0:2], lambda t: wait(pe, z_tok(g, t + 1)), z2_turned)

            def pick_one(pe, g):
                wait(pe, pick_v(g, 3))
                wait(pe, z4_out(g, 0))
                for c in range(KH):
                    mm = pe.matmul(bank_b[2][0:GS, 0:E0], zbn[:, c, :], wr[:, c, :], start=(c == 0), stop=(c == KH - 1))
                mm.then_inc(pick_mm.sem, 1)

            def down(pe, g):
                def units(e):
                    for c in range(KH):
                        product(pe, bank_b[e][:, :], [w[:, c, e * P:(e + 1) * P] for w in w_down],
                                (z_hi[:, c, :], z_lo[:, c, :]), c == 0, False)

                def penalise(e):
                    pe.matmul(bank_b[e][:, :], pen[:, 2 * e:2 * e + 2, :].rearrange("b e j -> b (e j)"), member_r[:, :],
                              start=False, stop=True).then_inc(down_mm.sem, 1)

                pe.wait_ge(w_lo_done.sem, len(staged))
                wait(pe, z2_split(g, 2))
                units(0)
                units(1)
                wait(pe, pick_v(g, 14))
                for t in range(TILES):
                    mm = pe.matmul(bank_b[2][:, t:t + 1], member_r[:, t * P:(t + 1) * P].bitcast(F32), pick[:, 4, 0:1], start=True, stop=True)
                mm.then_inc(pick_mm.sem, 1)
                pe.matmul(bank_b[3][0:E0, :], oneh_r[:, :], member_r[:, :], start=True, stop=True).then_inc(pick_mm.sem, 1)
                penalise(0)
                penalise(1)
                wait(pe, pick_v(g, 16))
                for e in (2, 3):
                    units(e)
                    penalise(e)

            def up(pe, g):
                def out(t):
                    return bank_b[t // 2][:, (t % 2) * HID:(t % 2 + 1) * HID]

                for e in range(4):
                    for t in range(TILES):
                        wait(pe, hid_split(g, max(e, t // 2) + 1))
                        product(pe, out(t), (mid_hi[:, e, t * P:(t + 1) * P], mid_lo[:, e, t * P:(t + 1) * P]),
                                [w[:, e, :] for w in w_up], e == 0 and t % 2 == 0, False, skip_group_check=True)
                for t in range(TILES):
                    for s in range(2):
                        mm = pe.matmul(out(t), oneh_t[:, t * P:(t + 1) * P], b_up[s][:, :], start=False, stop=(s == 1), skip_group_check=True)
                    if t % 2:
                        mm.then_inc(up_mm.sem, 1)

            def turn3(pe, g):
                turn(pe, tok_b, bank_b[2:4], lambda t: wait(pe, z_tok(g, 5 + t)), z3_turned)

            def feature_major(pe, g, first):
                wait(pe, z3_split(g, 2))
                for m in range(first, first + 4):
                    wait(pe, h_ffn(g, 4) if m < 4 else q_out(g, m - 3))
                    for c in range(KH):
                        mm = product(pe, bank_b[m % 4][:, :], [w[:, c, m * P:(m + 1) * P] for w in w_qkv],
                                     (z_hi[:, c, :], z_lo[:, c, :]), c == 0, c == KH - 1)
                    mm.then_inc(qkv_mm.sem, 1)

            def values(pe, g):
                for t in range(TILES):
                    wait(pe, k_out(g, t + 1))
                    for c in range(KH):
                        mm = product(pe, bank_b[t][:, :], (z_hi[:, c, t * P:(t + 1) * P], z_lo[:, c, t * P:(t + 1) * P]),
                                     [w[:, c, 2 * INNER:3 * INNER] for w in w_qkv], c == 0, c == KH - 1)
                    mm.then_inc(qkv_mm.sem, 1)

            def similar(pe, g, t):
                if t == 0:
                    wait(pe, q_out(g, 4))
                    wait(pe, k_out(g, 4))
                if t < 2:
                    wait(pe, dt_in(min(g + 3, GROUPS), 0))
                    wait(pe, joined(g, 2))
                else:
                    wait(pe, s_sub(g, t - 1))
                pe.matmul(bank_a[t % 2][:, :].rearrange("p (j y k) -> p j y k", j=HP, y=2), ident[:, :],
                          rel_bias[:, :, None, :].broadcast_to([P, HP, 2, SEQ]), start=True, stop=False,
                          skip_group_check=True).then_inc(s_bias.sem, 1)
                wait(pe, s_bias(g, t + 1))
                for j in range(HP):
                    for y in range(2):
                        for x in range(2):
                            rows, tok = slice(x * DH, (x + 1) * DH), slice(t * P + y * SEQ, t * P + (y + 1) * SEQ)
                            mm = pe.matmul(bank_a[t % 2][x * SEQ:(x + 1) * SEQ, (2 * j + y) * SEQ:(2 * j + y + 1) * SEQ],
                                           qkv[rows, j, tok], qkv[rows, 4 + j, tok], start=False, stop=True,
                                           skip_group_check=True)
                mm.then_inc(s_mm.sem, 1)

            def heads(pe, g, t):
                wait(pe, s_norm(g, t + 1))
                wait(pe, v_out(g, 2) if t < 2 else pt_out(g, t - 1))
                for j in range(HP):
                    mm = pe.transpose(bank_b[t % 2][:, j * P:(j + 1) * P], score[:, t % 2, j * P:(j + 1) * P], ident[:, :])
                mm.then_inc(pt_mm.sem, 1)

            def outputs(pe, g, t):
                wait(pe, pt_out(g, t + 1))
                if t == 0:
                    wait(pe, v_out(g, 4))
                if t >= 2:
                    wait(pe, o_split(g, t - 1))
                for y in range(2):
                    for j in range(HP):
                        for x in range(2):
                            rows = slice(y * SEQ, (y + 1) * SEQ)
                            if y == 1 and j == 0 and x == 0:
                                wait(pe, o_half(g, t + 1))
                            mm = pe.matmul(bank_b[2 + t % 2][x * DH:(x + 1) * DH, (y * HP + j) * SEQ:(y * HP + j + 1) * SEQ],
                                           qkv[rows, 8 + t, (2 * j + x) * DH:(2 * j + x + 1) * DH],
                                           probs_t[rows, t % 2, (2 * j + x) * SEQ:(2 * j + x + 1) * SEQ],
                                           start=True, stop=True)
                    mm.then_inc((o_half, o_mm)[y].sem, 1)

            def proj(pe, g, b):
                wait(pe, s_sub(g, 3 + b))
                for t in range(2 * b, 2 * b + 2):
                    wait(pe, o_split(g, t + 1))
                    for j in range(HP):
                        mm = product(pe, bank_a[b][:, (t % 2) * HID:(t % 2 + 1) * HID],
                                     (mid_hi[:, j, t * P:(t + 1) * P], mid_lo[:, j, t * P:(t + 1) * P]),
                                     [w[:, j, :] for w in w_o], j == 0, j == HP - 1)
                    if t % 2:
                        mm.then_inc(proj_mm.sem, 1)

            def gate(pe, g):
                turn(pe, tok_b, bank_b[2:4], lambda t: wait(pe, z_tok(g, 9 + t)), z4_turned)
                wait(pe, z4_out(g, 2))
                for t in range(TILES):
                    for c in range(KH):
                        mm = pe.matmul(bank_b[0][:, t * E1:(t + 1) * E1], qkv[:, 10 + c, t * P:(t + 1) * P], gate_w[:, c, :],
                                       start=(c == 0), stop=(c == KH - 1))
                mm.then_inc(gate_mm.sem, 1)

            run("tensor", pe, {"relative": relative, "patch": patch, "turn1": turn1, "dt": dt_products, "join": join, "turn2": turn2,
                     "pick": pick_one, "down": down, "up": up, "turn3": turn3, "q": lambda p, g: feature_major(p, g, 0),
                     "k": lambda p, g: feature_major(p, g, 4), "v": values, "similar": similar, "heads": heads,
                     "outputs": outputs, "proj": proj, "gate": gate})


PLAN_STEPS = 17
SLOT_STEPS = 14


def flat(t):
    return t[:, :, :].rearrange("p a b -> p (a b)")


def of_expert(w_hi, w_lo, e, at, n):
    if isinstance(e, int):
        return w_hi[:, e, at:at + n], w_lo[:, e, at:at + n]
    return [w[:, bass.ds(e, 1), at:at + n].rearrange("p o n -> p (o n)") for w in (w_hi, w_lo)]


def phase_two(nc, sems, d, chosen, weight, raw_store, w_raw_in, out):
    with ExitStack() as ctx:
        def sb(name, shape, dt=F32):
            return ctx.enter_context(nc.sbuf_tensor(name, shape, dt))

        def signal(name, per=1):
            return Signal(sems.enter_context(nc.semaphore(name)), per)

        NE = E1 + 1
        ZBUFS, YBUFS, GBUFS = 8, 4, 8
        ALL = ALL_TILES + SLOT_TILES
        HALF = ALL_TILES // 2
        EARLY = 4
        w_raw = raw_store[:, 0:RAW * EXPERT].rearrange("p (b n) -> p b n", b=RAW)
        w_hi = sb("w_hi", [P, NE, EXPERT], F32R)
        w_lo = sb("w_lo", [P, NE, EXPERT], F32R)
        z = sb("z", [P, ALL_TILES, ROW])
        res = sb("res", [P, ALL_TILES, HID])
        z_slot = sb("z_slot", [P, ZBUFS, ROW])
        zt_hi = sb("zt_hi", [P, 2, HID], F32R)
        zt_lo = sb("zt_lo", [P, 2, HID], F32R)
        silu = sb("silu", [P, 2, M1])
        unit = sb("unit", [P, 2, M1])
        at_hi = sb("at_hi", [P, 2, P], F32R)
        at_lo = sb("at_lo", [P, 2, P], F32R)
        y_slot = sb("y_slot", [P, YBUFS, HID])
        home = sb("home", [P, ALL_TILES, 2], U32)
        ident = sb("ident_2", [P, P])

        plan = sb("plan", [P, 2 * P + ALL_TILES + SLOT_TILES + E1 * ALL_TILES])
        earlier, ones = plan[:, 0:P], plan[:, P:2 * P]
        at = 2 * P
        full = plan[:, at:at + ALL_TILES]
        number = plan[:, at + ALL_TILES:at + ALL_TILES + SLOT_TILES]
        carry = plan[:, at + ALL_TILES + SLOT_TILES:]
        both = sb("both", [P, ALL_TILES, E1])
        count = sb("count", [P, E1, ALL_TILES])
        upto = sb("upto", [P, E1, ALL_TILES])
        place = sb("place", [P, E1, ALL_TILES])
        fills = sb("fills", [P, E1, ALL_TILES])
        tiles = sb("tiles", [P, 3, E1])
        before = sb("before", [P, SLOT_TILES, E1])
        owner = sb("owner", [P, SLOT_TILES])
        owner_i = sb("owner_i", [P, SLOT_TILES], U32)
        mine = sb("mine", [P, ALL_TILES, 2, E1])
        slot = sb("slot", [P, ALL_TILES, 2])
        slot_i = sb("slot_i", [P, ALL_TILES, 2], U32)

        bank_z = [ctx.enter_context(nc.psum_tensor(f"bank_z{i}", [P, GT], F32)) for i in range(2)]
        bank_gu = [ctx.enter_context(nc.psum_tensor(f"bank_gu{i}", [P, GT], F32)) for i in range(2)]
        bank_t = [ctx.enter_context(nc.psum_tensor(f"bank_t{i}", [P, GT], F32)) for i in range(2)]
        bank_y = [ctx.enter_context(nc.psum_tensor(f"bank_y{i}", [P, GT], F32)) for i in range(2)]

        plan_in = signal("plan_in")
        z_in, res_in = [signal(f"z_in{i}") for i in range(GROUPS)], signal("res_in")
        w_hi2, w_lo_early, w_lo2 = signal("w_hi2"), signal("w_lo_early"), signal("w_lo2")
        plan_v, plan_mm = signal("plan_v"), signal("plan_mm")
        scattered, z_slot_in = [signal(f"scattered{i}") for i in range(2)], [signal(f"z_slot_in{i}") for i in range(ZBUFS)]
        z_turned, zt_hi_done, zt_split = signal("z_turned"), signal("zt_hi_done"), signal("zt_split")
        gu_mm, silu_done, unit_done = signal("gu_mm"), signal("silu_done"), signal("unit_done")
        a_turned, at_hi_done, at_split = signal("a_turned"), signal("at_hi_done"), signal("at_split")
        y_mm, y_out, shared_added = signal("y_mm"), signal("y_out"), signal("shared_added")
        y_stored = [signal(f"y_stored{i}") for i in range(YBUFS)]
        pair_in, homed = [signal(f"pair_in{i}") for i in range(GBUFS)], signal("homed")
        combined, stored = signal("combined"), signal("stored2")

        block = ctx.enter_context(nc.Block())

        def lo_done(i):
            return (w_lo_early.sem, i + 1) if i < EARLY else (w_lo2.sem, i - EARLY + 1)

        def tokens(tensor, g):
            return tensor[:, g * TILES:(g + 1) * TILES, 0:HID]

        y_pair = flat(z)[:, 0:GBUFS * 2 * HID].rearrange("p (b k n) -> p b k n", b=GBUFS, k=2)

        @block.sync
        def _(sp):
            def load_expert(i):
                sp.wait_ge(*lo_done(i - RAW))
                sp.dma_start(w_raw[:, i % RAW, :], d["experts"][expert_order(i)]).then_inc(w_raw_in[i % RAW].sem, 16)

            def load_slots(j):
                if j >= ZBUFS:
                    sp.wait_ge(y_stored[j % YBUFS].sem, 16 * ((j - ZBUFS) // YBUFS + 1))
                sp.dma_start(z_slot[:, j % ZBUFS, :], d["z_slots"][j * P:(j + 1) * P, :]).then_inc(z_slot_in[j % ZBUFS].sem, 16)

            sp.dma_start(plan[:, :], d["plan"]).then_inc(plan_in.sem, 16)
            sp.dma_start(ident[:, :], d["ident"]).then_inc(plan_in.sem, 16)
            sp.dma_start(home[:, :, :], d["home"]).then_inc(plan_in.sem, 16)
            for g in range(GROUPS):
                sp.dma_start(tokens(z, g), d["z_mid"][g]).then_inc(z_in[g].sem, 16)
            for g in range(GROUPS):
                sp.dma_start(tokens(res, g), d["h_mid"][g]).then_inc(res_in.sem, 16)
            for i in range(RAW, NE):
                load_expert(i)
            for i in range(2):
                sp.wait_ge(scattered[i].sem, 2 * HALF * 16)
            for j in range(SLOT_TILES):
                load_slots(j)

            def load_pair(t):
                if t >= GBUFS:
                    sp.wait_ge(combined.sem, 2 * (t - GBUFS) + 2)
                sp.dma_start(y_pair[:, t % GBUFS, :, :],
                             d["y_tok"][2 * t * P:2 * (t + 1) * P, :].rearrange("(p k) n -> p k n", k=2)).then_inc(pair_in[t % GBUFS].sem, 16)

            for b in range(YBUFS):
                sp.wait_ge(y_stored[b].sem, 16 * (SLOT_TILES // YBUFS))
            for t in range(GBUFS):
                load_pair(t)
            for t in range(ALL_TILES):
                sp.wait_ge(combined.sem, 2 * t + 2)
                sp.dma_start(out[t // TILES][:, t % TILES, :], res[:, t, :]).then_inc(stored.sem, 16)
                if t + GBUFS < ALL_TILES:
                    load_pair(t + GBUFS)
            sp.wait_ge(stored.sem, 16 * ALL_TILES)

        @block.gpsimd
        def _(pool):
            for i in range(EARLY):
                e = expert_order(i)
                pool.wait_ge(w_hi2.sem, i + 1)
                pool.tensor_tensor(w_lo[:, e, :], w_raw[:, i % RAW, :], w_hi[:, e, :].bitcast(F32), ALU.subtract).then_inc(w_lo_early.sem, 1)
            pool.wait_ge(plan_v.sem, SLOT_STEPS)
            for k in range(2):
                for t in range(ALL_TILES):
                    if t % HALF == 0:
                        pool.wait_ge(homed.sem, 1 if k == 0 else 2 + t // HALF)
                    if k == 0 and t % TILES == 0:
                        pool.wait_ge(z_in[t // TILES].sem, 16)
                    pool.indirect_dma_start(d["z_slots"], bass.IndirectOffsetOnAxis(slot_i[:, t, k:k + 1], 0),
                                            z[:, t, :], None).then_inc(scattered[t // HALF].sem, 16)
            for j in range(SLOT_TILES):
                pool.wait_ge(y_out.sem, j + 1)
                pool.indirect_dma_start(d["y_tok"], bass.IndirectOffsetOnAxis(z_slot[:, j % ZBUFS, HID:HID + 1].bitcast(U32), 0),
                                        y_slot[:, j % YBUFS, :], None).then_inc(y_stored[j % YBUFS].sem, 16)

        @block.scalar
        def _(act):
            def split(i):
                e = expert_order(i)
                act.wait_ge(w_raw_in[i % RAW].sem, 16 * (i // RAW + 1))
                act.activation(w_hi[:, e, :], w_raw[:, i % RAW, :], ACT.Copy).then_inc(w_hi2.sem, 1)

            for i in range(EARLY):
                split(i)
            for s in range(ALL + 3):
                i = s
                if i < ALL:
                    act.wait_ge(z_turned.sem, i + 1)
                    if i >= 2:
                        act.wait_ge(gu_mm.sem, i - 1)
                    act.activation(zt_hi[:, i % 2, :], bank_z[i % 2][:, 0:HID], ACT.Copy).then_inc(zt_hi_done.sem, 1)
                i = s - 1
                if 0 <= i < ALL:
                    act.wait_ge(gu_mm.sem, i + 1)
                    if i >= 2:
                        act.wait_ge(unit_done.sem, i - 1)
                    act.activation(silu[:, i % 2, :], bank_gu[i % 2][:, 0:M1], ACT.Silu).then_inc(silu_done.sem, 1)
                i = s - 2
                if 0 <= i < ALL:
                    act.wait_ge(a_turned.sem, i + 1)
                    if i >= 2:
                        act.wait_ge(y_mm.sem, i - 1)
                    act.activation(at_hi[:, i % 2, :], bank_t[i % 2][:, 0:P], ACT.Copy).then_inc(at_hi_done.sem, 1)
                i = s - 3
                j = i - ALL_TILES
                if j >= 0:
                    act.wait_ge(y_mm.sem, i + 1)
                    if j >= YBUFS:
                        act.wait_ge(y_stored[j % YBUFS].sem, 16 * (j // YBUFS))
                    act.activation(y_slot[:, j % YBUFS, :], bank_y[i % 2][:, 0:HID], ACT.Copy).then_inc(y_out.sem, 1)
                if s + EARLY < NE:
                    split(s + EARLY)

        @block.vector
        def _(dve):
            dve.wait_ge(plan_in.sem, 48)
            done = 0

            def step(inst):
                nonlocal done
                inst.then_inc(plan_v.sem, 1)
                done += 1
                dve.wait_ge(plan_v.sem, done)

            def to_experts(bank):
                return bank[:, 0:ALL_TILES * E1].rearrange("p (t e) -> p e t", e=E1)

            def home_rows(k, some, n):
                dve.tensor_copy(z[:, some, HID:].bitcast(U32), home[:, some, k:k + 1].broadcast_to([P, n, ROW - HID])).then_inc(homed.sem, 1)

            home_rows(0, slice(0, ALL_TILES), ALL_TILES)
            step(dve.tensor_tensor(both[:, :, :], chosen[:, :, 0, :], chosen[:, :, 1, :], ALU.add))
            dve.wait_ge(plan_mm.sem, 1)
            step(dve.tensor_copy(count[:, :, :], to_experts(bank_z[1])))
            step(dve.tensor_tensor_scan(flat(upto), carry, flat(count), 0.0, ALU.mult, ALU.add))
            step(dve.tensor_tensor(fills[:, :, :], upto[:, :, ALL_TILES - 1:ALL_TILES].broadcast_to([P, E1, ALL_TILES]),
                                   full[:, None, :].broadcast_to([P, E1, ALL_TILES]), ALU.is_gt))
            step(dve.tensor_reduce(tiles[:, 0, :], fills[:, :, :], AX_X, ALU.add))
            step(dve.tensor_tensor_scan(tiles[:, 1, :], ones[:, 0:E1], tiles[:, 0, :], 0.0, ALU.mult, ALU.add))
            step(dve.tensor_tensor(tiles[:, 2, :], tiles[:, 1, :], tiles[:, 0, :], ALU.subtract))
            step(dve.tensor_tensor(place[:, :, :], upto[:, :, :], count[:, :, :], ALU.subtract))
            step(dve.tensor_tensor(place[:, :, :], place[:, :, :], to_experts(bank_z[0]), ALU.add))
            step(dve.scalar_tensor_tensor(out=place[:, :, :], in0=tiles[:, 2, :, None].broadcast_to([P, E1, ALL_TILES]),
                                          scalar=float(P), in1=place[:, :, :], op0=ALU.mult, op1=ALU.add))
            for k in range(2):
                step(dve.tensor_tensor(mine[:, :, k, :], chosen[:, :, k, :], place[:, :, :].rearrange("p e t -> p t e"), ALU.mult))
            step(dve.tensor_reduce(slot[:, :, :], mine[:, :, :, :], AX_X, ALU.add))
            step(dve.tensor_copy(slot_i[:, :, :], slot[:, :, :]))
            step(dve.tensor_tensor(before[:, :, :], tiles[:, 1, None, :].broadcast_to([P, SLOT_TILES, E1]),
                                   number[:, :, None].broadcast_to([P, SLOT_TILES, E1]), ALU.is_le))
            step(dve.tensor_reduce(owner[:, :], before[:, :, :], AX_X, ALU.add))
            step(dve.tensor_copy(owner_i[:, :], owner[:, :]))
            assert done == PLAN_STEPS

            def split(i):
                e = expert_order(i)
                dve.wait_ge(w_hi2.sem, i + 1)
                dve.tensor_tensor(w_lo[:, e, :], w_raw[:, i % RAW, :], w_hi[:, e, :].bitcast(F32), ALU.subtract).then_inc(w_lo2.sem, 1)

            for s in range(ALL + 3):
                for i in range(2):
                    if s == (4, 8)[i]:
                        dve.wait_ge(scattered[i].sem, 16 * HALF)
                        home_rows(1, slice(i * HALF, (i + 1) * HALF), HALF)
                i = s
                if i < ALL:
                    dve.wait_ge(zt_hi_done.sem, i + 1)
                    dve.tensor_tensor(zt_lo[:, i % 2, :], bank_z[i % 2][:, 0:HID], zt_hi[:, i % 2, :].bitcast(F32),
                                      ALU.subtract).then_inc(zt_split.sem, 1)
                i = s - 1
                if 0 <= i < ALL:
                    dve.wait_ge(silu_done.sem, i + 1)
                    if i >= 2:
                        dve.wait_ge(a_turned.sem, i - 1)
                    dve.tensor_tensor(unit[:, i % 2, :], silu[:, i % 2, :], bank_gu[i % 2][:, M1:2 * M1], ALU.mult).then_inc(unit_done.sem, 1)
                i = s - 2
                if 0 <= i < ALL:
                    dve.wait_ge(at_hi_done.sem, i + 1)
                    dve.tensor_tensor(at_lo[:, i % 2, :], bank_t[i % 2][:, 0:P], at_hi[:, i % 2, :].bitcast(F32),
                                      ALU.subtract).then_inc(at_split.sem, 1)
                if EARLY <= s + EARLY - 1 < NE:
                    split(s + EARLY - 1)
                i = s - 3
                if 0 <= i < ALL_TILES:
                    if i == 0:
                        dve.wait_ge(res_in.sem, 16 * GROUPS)
                    dve.wait_ge(y_mm.sem, i + 1)
                    dve.tensor_tensor(res[:, i, :], bank_y[i % 2][:, 0:HID], res[:, i, :], ALU.add).then_inc(shared_added.sem, 1)
            dve.wait_ge(shared_added.sem, ALL_TILES)
            for i in range(2 * ALL_TILES):
                t, k = i // 2, i % 2
                dve.wait_ge(pair_in[t % GBUFS].sem, 16 * (t // GBUFS + 1))
                if k:
                    dve.wait_ge(combined.sem, i)
                dve.scalar_tensor_tensor(out=res[:, t, :], in0=y_pair[:, t % GBUFS, k, :], scalar=weight[:, t, k:k + 1],
                                         in1=res[:, t, :], op0=ALU.mult, op1=ALU.add).then_inc(combined.sem, 1)

        @block.tensor
        def _(pe):
            pe.wait_ge(plan_in.sem, 48)
            pe.wait_ge(plan_v.sem, 1)
            pe.matmul(bank_z[0][:, 0:ALL_TILES * E1], earlier, flat(both), start=True, stop=True)
            pe.matmul(bank_z[1][:, 0:ALL_TILES * E1], ones, flat(both), start=True, stop=True).then_inc(plan_mm.sem, 1)
            pe.wait_ge(plan_v.sem, SLOT_STEPS)

            owners = {}
            for s in range(ALL + 3):
                i = s
                if i < ALL:
                    j = i - ALL_TILES
                    if j < 0:
                        owners[i] = E1
                        if i == 0:
                            pe.wait_ge(plan_v.sem, PLAN_STEPS)
                        for o in range(3 * i, 3 * i + 3):
                            owners[ALL_TILES + o] = pe.value_load(owner_i[0:1, o:o + 1], min_val=0, max_val=E1)
                        if i % TILES == 0:
                            pe.wait_ge(z_in[i // TILES].sem, 16)
                        rows = z[:, i, :]
                    else:
                        pe.wait_ge(z_slot_in[j % ZBUFS].sem, 16 * (j // ZBUFS + 1))
                        rows = z_slot[:, j % ZBUFS, :]
                    if i >= 2:
                        pe.wait_ge(zt_split.sem, i - 1)
                    for c in range(KH):
                        mm = pe.transpose(bank_z[i % 2][:, c * P:(c + 1) * P], rows[:, c * P:(c + 1) * P], ident[:, :])
                    mm.then_inc(z_turned.sem, 1)
                i = s - 1
                if 0 <= i < ALL:
                    pe.wait_ge(zt_split.sem, i + 1)
                    pe.wait_ge(w_lo_early.sem, 1 if i < ALL_TILES else EARLY)
                    if i >= ALL_TILES:
                        pe.wait_ge(*lo_done(NE - 1))
                    if i >= 2:
                        pe.wait_ge(unit_done.sem, i - 1)
                    for c in range(KH):
                        cut = slice(c * P, (c + 1) * P)
                        mm = product(pe, bank_gu[i % 2][:, 0:2 * M1], (zt_hi[:, i % 2, cut], zt_lo[:, i % 2, cut]),
                                     of_expert(w_hi, w_lo, owners[i], c * 2 * M1, 2 * M1), c == 0, c == KH - 1)
                    mm.then_inc(gu_mm.sem, 1)
                i = s - 2
                if 0 <= i < ALL:
                    pe.wait_ge(unit_done.sem, i + 1)
                    if i >= 2:
                        pe.wait_ge(at_split.sem, i - 1)
                    pe.transpose(bank_t[i % 2][:, 0:P], unit[:, i % 2, :], ident[:, :]).then_inc(a_turned.sem, 1)
                i = s - 3
                if 0 <= i < ALL:
                    pe.wait_ge(at_split.sem, i + 1)
                    if 2 <= i < ALL_TILES + 2:
                        pe.wait_ge(shared_added.sem, i - 1)
                    if i >= ALL_TILES + 2:
                        pe.wait_ge(y_out.sem, i - ALL_TILES - 1)
                    product(pe, bank_y[i % 2][:, 0:HID], (at_hi[:, i % 2, :], at_lo[:, i % 2, :]),
                            of_expert(w_hi, w_lo, owners[i], KH * 2 * M1, HID), True, True).then_inc(y_mm.sem, 1)


def build(nc, d, out):
    with ExitStack() as ctx:
        chosen = ctx.enter_context(nc.sbuf_tensor("chosen", [P, ALL_TILES, 2, E1], F32))
        weight = ctx.enter_context(nc.sbuf_tensor("weight", [P, ALL_TILES, 2], F32))
        raw_store = ctx.enter_context(nc.sbuf_tensor("raw_store", [P, RAW_SIZE], F32))
        w_raw_in = [Signal(ctx.enter_context(nc.semaphore(f"w_raw_in{i}")), 1) for i in range(RAW)]
        phase_one(nc, ctx, d, chosen, weight, raw_store, w_raw_in)
        phase_two(nc, ctx, d, chosen, weight, raw_store, w_raw_in, out)


def kernel(**inputs):
    import numpy as np
    from concourse import bacc
    from concourse.bass_utils import run_bass_kernel_spmd

    a = {k: np.asarray(v) for k, v in inputs.items()}

    def rows(w, k):
        return w.reshape(k, P, -1).transpose(1, 0, 2)

    def column(v):
        return v.reshape(-1, P).T

    def wide(v):
        return np.broadcast_to(v, (P, v.shape[-1]))

    side, ps = 8, 16
    x = a["x"].reshape(GROUPS, GS, 3, side, ps, side, ps).transpose(0, 4, 6, 2, 1, 3, 5)
    x = x.reshape(GROUPS, KP, P, 2, GT // 2).transpose(0, 3, 2, 1, 4)

    quarter = HID // 4
    f = (10000.0 ** (np.arange(quarter, dtype=np.float32) / quarter)).astype(np.float32)
    rr, cc = [v.reshape(-1, 1).astype(np.float32) / f for v in np.meshgrid(np.arange(side), np.arange(side), indexing="ij")]
    pos = np.concatenate([np.sin(rr), np.cos(rr), np.sin(cc), np.cos(cc)], -1).astype(np.float32)
    dist = np.arange(2 * SEQ) - (SEQ - 1)
    large = 16 + (np.log(np.maximum(dist, 1).astype(np.float32) / 16) / np.log(128 / 16) * 16).astype(np.int32)
    bucket = np.where(dist < 0, 32, np.where(dist < 16, dist, np.minimum(large, 31)))
    base = (np.arange(33)[:, None] == bucket[None]).astype(np.float32)
    member = (np.arange(GS)[:, None] == np.arange(GT)[None] // SEQ).astype(np.float32)
    earlier = (np.arange(P)[:, None] < np.arange(P)[None]).astype(np.float32)
    nobody = np.tile(np.arange(SLOT_TILES * P, dtype=np.uint32)[:, None] + 2 * BATCH * SEQ, (1, ROW - HID)).view(np.float32)
    home = (2 * (np.arange(P)[:, None, None] + P * np.arange(ALL_TILES)[None, :, None]) + np.arange(2)).astype(np.uint32)
    plan = np.concatenate([earlier, np.ones((P, P)), wide(P * np.arange(ALL_TILES)), wide(np.arange(SLOT_TILES)),
                           wide(np.tile(np.arange(ALL_TILES) > 0, E1))], 1).astype(np.float32)

    experts = [np.concatenate([
        np.concatenate([rows(g, KH), rows(u, KH)], 2).reshape(P, -1), w], 1)
        for g, u, w in zip([*a["L1_ffn_w_gate"], a["L1_ffn_ws_gate"]], [*a["L1_ffn_w_up"], a["L1_ffn_ws_up"]],
                           [*a["L1_ffn_w_down"], a["L1_ffn_ws_down"]])]
    host = {
        "x": x, "wp": rows(a["L0_tok_Wp"].T, KP), "pos": np.tile(pos, (2, 1)), "tokb": wide(a["L0_tok_b"]),
        "bo": wide(a["L1_attn_bo"]), "iota": wide(np.arange(E1, dtype=np.float32)), "ident": np.eye(P, dtype=np.float32),
        "b_dt": column(a["L0_attn_b_dt"]), "skip_d": column(a["L0_attn_D_vec"]),
        "a_log": rows(a["L0_attn_A_log"], KH), "bmat": rows(a["L0_attn_B_mat"], KH), "cmat": rows(a["L0_attn_C_mat"], KH),
        "cols": np.stack([column(a["L0_ffn_" + n]) for n in ("ln_g", "ln_b", "bn_g", "bn_b", "bn_mean", "bn_var", "bn_var", "bn_var")], 1),
        "b_down": column(a["L0_ffn_b_down"].reshape(-1)), "wr": rows(a["L0_ffn_Wr"], KH),
        "br": np.broadcast_to(a["L0_ffn_br"], (E0, E0)), "gate_w": rows(a["L1_ffn_gate_w"].T, KH), "member": member,
        "rel": a["L1_attn_rel_emb"], "base": base, "b_up": a["L0_ffn_b_up"],
        "w_dt": rows(a["L0_attn_W_dt"].T, KH), "w_down": rows(a["L0_ffn_W_down"].transpose(1, 0, 2).reshape(HID, -1), KH),
        "w_up": rows(a["L0_ffn_W_up"].reshape(E0 * H0, HID), 4),
        "w_qkv": rows(np.concatenate([a["L1_attn_Wq"], a["L1_attn_Wkv"]], 1), KH), "w_o": rows(a["L1_attn_Wo"], HP),
        "experts": np.stack(experts), "plan": plan, "home": home, "nobody": nobody,
        "blank": np.zeros((P, HID), np.float32),
    }
    nc = bacc.Bacc("TRN2", target_bir_lowering=False, num_devices=1)
    arrays, d = {}, {}
    for name, v in host.items():
        arrays["in_" + name] = np.ascontiguousarray(v)
        d[name] = nc.dram_tensor("in_" + name, v.shape, mybir.dt.from_np(v.dtype), kind="ExternalInput").ap()
    d["h_mid"] = nc.dram_tensor("h_mid", (GROUPS, P, TILES, HID), F32, kind="Internal").ap()
    d["z_mid"] = nc.dram_tensor("z_mid", (GROUPS, P, TILES, HID), F32, kind="Internal").ap()
    d["z_slots"] = nc.dram_tensor("z_slots", (SLOT_TILES * P, ROW), F32, kind="Internal").ap()
    d["y_tok"] = nc.dram_tensor("y_tok", (2 * BATCH * SEQ + SLOT_TILES * P, HID), F32, kind="Internal").ap()
    out = nc.dram_tensor("out", (GROUPS, P, TILES, HID), F32, kind="ExternalOutput").ap()
    build(nc, d, out)
    got = run_bass_kernel_spmd(nc, [arrays], core_ids=[0]).results[0]["out"]
    return got.reshape(GROUPS, P, TILES, HID).transpose(0, 2, 1, 3).reshape(BATCH, SEQ, HID)
```
